# Optimizing a Trainium2 kernel written in Bass

```python
import numpy as np
import jax
import jax.numpy as jnp

def _softmax(x, axis=-1):
    return jax.nn.softmax(x, axis=axis)

def _gelu(x):
    return jax.nn.gelu(x, approximate=True)

def _silu(x):
    return jax.nn.silu(x)

def _sigmoid(x):
    return jax.nn.sigmoid(x)

def _layernorm(x, axis=-1, eps=1e-05):
    m = jnp.mean(x, axis=axis, keepdims=True)
    v = jnp.var(x, axis=axis, keepdims=True)
    return (x - m) / jnp.sqrt(v + eps)

def _scatter_add(tgt, idx, src, axis=0):
    return tgt.at[idx].add(src)

def _segment_sum(src, seg, n):
    return jax.ops.segment_sum(src, seg, n)
kernel_name = 'mk_xattn_seq_d4_seqx_r8_82c14f'

def setup_inputs(seed: int=0):
    np.random.seed(seed)
    _w = jnp.asarray

    def _rec_inputs():
        import jax
        import jax.numpy as jnp
        _rk = jax.random.key(seed)
        x = -0.0002928 + 1 * jax.random.normal(jax.random.fold_in(_rk, 1), (32, 64, 128), jnp.float32)
        _lenS = 64 - jax.random.randint(jax.random.fold_in(_rk, 7), (32,), 0, max(1, 64 // 4) + 1, jnp.int32)
        _lenS2 = 64 - jax.random.randint(jax.random.fold_in(_rk, 8), (32,), 0, max(1, 64 // 4) + 1, jnp.int32)
        _ctx_1024P = jax.random.normal(jax.random.fold_in(_rk, 11), (32, 16, 128), jnp.float32)
        _ctx_1024c = jax.random.dirichlet(jax.random.fold_in(_rk, 511), 0.3 * jnp.ones((16,), jnp.float32), (32, 64))
        _ctx_1024t = jnp.einsum('bsk,bkd->bsd', _ctx_1024c, _ctx_1024P)
        _ctx_1024t = _ctx_1024t * jax.lax.rsqrt(jnp.mean(jnp.square(_ctx_1024t)) + 1e-12) * 0.953939
        ctx_1024 = -1.39393e-06 + 0.999914 * (_ctx_1024t + 0.3 * jax.random.normal(jax.random.fold_in(_rk, 611), (32, 64, 128), jnp.float32))
        _validS = jnp.arange(64)[None, :] < _lenS[:, None]
        _validS2 = jnp.arange(64)[None, :] < _lenS2[:, None]
        _causal = jnp.tril(jnp.ones((64, 64), dtype=bool))
        mask_BxSxS2_ik0 = jnp.where(jnp.broadcast_to(_validS2[:, None, :], (32, 64, 64)), 0, 1).astype(jnp.int32)
        mask_BxSxS2_if1 = jnp.where(jnp.ones((32, 64, 64), dtype=bool), 1, 0).astype(jnp.int32)
        mask_BxSxS_ik0 = jnp.where(jnp.broadcast_to(_validS[:, None, :], (32, 64, 64)), 0, 1).astype(jnp.int32)
        mask_BxSxS2_ik1 = jnp.where(jnp.broadcast_to(_validS2[:, None, :], (32, 64, 64)), 1, 0).astype(jnp.int32)
        return (x, ctx_1024, mask_BxSxS2_ik0, mask_BxSxS2_if1, mask_BxSxS_ik0, mask_BxSxS2_ik1)
    x, ctx_1024, mask_BxSxS2_ik0, mask_BxSxS2_if1, mask_BxSxS_ik0, mask_BxSxS2_ik1 = _rec_inputs()

    def _L0_xattn_setup():
        import jax, jax.numpy as jnp
        import numpy as np
        B, S, D, H, DFF = (2, 256, 128, 16, 512)
        DK = D // H
        LN_EPS = 1e-05

        def _mha(q, k, v, mask, wq, bq, wk, bk, wv, bv, wo, bo):
            b, sq, _ = q.shape
            sk = k.shape[1]
            Q = (q @ wq + bq).reshape(b, sq, H, DK).transpose(0, 2, 1, 3)
            K = (k @ wk + bk).reshape(b, sk, H, DK).transpose(0, 2, 1, 3)
            V = (v @ wv + bv).reshape(b, sk, H, DK).transpose(0, 2, 1, 3)
            scores = jnp.einsum('bhqd,bhkd->bhqk', Q, K) / np.float32(np.sqrt(DK))
            if mask is not None:
                scores = jnp.where(mask[:, None, :, :] == 0, jnp.float32(-1e+20), scores)
            A = jax.nn.softmax(scores, axis=-1)
            out = jnp.einsum('bhqk,bhkd->bhqd', A, V).transpose(0, 2, 1, 3).reshape(b, sq, D)
            return out @ wo + bo

        def _ln(x, g, b):
            m = jnp.mean(x, axis=-1, keepdims=True)
            v = jnp.var(x, axis=-1, keepdims=True)
            return (x - m) * jax.lax.rsqrt(v + LN_EPS) * g + b
        key = jax.random.key(seed)
        ks = jax.random.split(key, 32)
        ki = iter(range(32))

        def w(shape, scale=0.02):
            return (jax.random.normal(ks[next(ki)], shape, jnp.float32) * scale).astype(jnp.float32)
        inp = {}
        inp['x'] = jax.random.normal(ks[next(ki)], (B, S, D), jnp.float32)
        inp['enc_output'] = jax.random.normal(ks[next(ki)], (B, S, D), jnp.float32)
        causal = jnp.tril(jnp.ones((S, S), jnp.int32))
        inp['tgt_mask'] = jnp.broadcast_to(causal, (B, S, S))
        inp['memory_mask'] = jnp.ones((B, S, S), jnp.int32)
        for p in ('sa', 'ca'):
            for n in ('q', 'k', 'v', 'o'):
                inp[f'{p}_w{n}'] = w((D, D))
                inp[f'{p}_b{n}'] = jnp.zeros((D,), jnp.float32)
        inp['ff_w1'] = w((D, DFF))
        inp['ff_b1'] = jnp.zeros((DFF,), jnp.float32)
        inp['ff_w2'] = w((DFF, D))
        inp['ff_b2'] = jnp.zeros((D,), jnp.float32)
        for i in (1, 2, 3):
            inp[f'ln{i}_g'] = jnp.ones((D,), jnp.float32)
            inp[f'ln{i}_b'] = jnp.zeros((D,), jnp.float32)
        return inp
    _L0_xattn_all = _L0_xattn_setup()
    _L0_xattn_in = {k: v for k, v in _L0_xattn_all.items() if k in ('sa_wq', 'sa_bq', 'sa_wk', 'sa_bk', 'sa_wv', 'sa_bv', 'sa_wo', 'sa_bo', 'ca_wq', 'ca_bq', 'ca_wk', 'ca_bk', 'ca_wv', 'ca_bv', 'ca_wo', 'ca_bo', 'ff_w1', 'ff_b1', 'ff_w2', 'ff_b2', 'ln1_g', 'ln1_b', 'ln2_g', 'ln2_b', 'ln3_g', 'ln3_b')}
    del _L0_xattn_all

    def _L1_xattn_setup():
        import jax, jax.numpy as jnp
        import numpy as np
        B, T, S_ENC, D, H, E, K = (4, 128, 64, 128, 16, 8, 2)
        DK = D // H
        HID = 4 * D
        NEG = -65504.0
        EPS = 1e-05

        def rmsnorm(x, w):
            return w * (x * jax.lax.rsqrt(jnp.mean(x * x, axis=-1, keepdims=True) + EPS))

        def mha(xq, xk, xv, mask, wq, wk, wv, wo):
            q = jnp.einsum('bsd,ed->bse', xq, wq).reshape(xq.shape[0], -1, H, DK).transpose(0, 2, 1, 3)
            k = jnp.einsum('bsd,ed->bse', xk, wk).reshape(xk.shape[0], -1, H, DK).transpose(0, 2, 1, 3)
            v = jnp.einsum('bsd,ed->bse', xv, wv).reshape(xv.shape[0], -1, H, DK).transpose(0, 2, 1, 3)
            scores = jnp.einsum('bhqd,bhkd->bhqk', q, k) / jnp.sqrt(jnp.float32(DK))
            scores = jnp.where(mask[:, None, :, :] == 0, NEG, scores)
            attn = jax.nn.softmax(scores, axis=-1)
            out = jnp.einsum('bhqk,bhkd->bhqd', attn, v)
            out = out.transpose(0, 2, 1, 3).reshape(xq.shape[0], -1, D)
            return jnp.einsum('bsd,ed->bse', out, wo)

        def moe_ffn(x, gate_w, exp_w1, exp_w2, sh_w1, sh_w2):
            b, s, d = x.shape
            xf = x.reshape(-1, d)
            sh = jnp.einsum('nd,hd->nh', xf, sh_w1)
            sh = jax.nn.silu(sh)
            sh = jnp.einsum('nh,dh->nd', sh, sh_w2)
            logits = jnp.einsum('nd,ed->ne', xf, gate_w)
            topk_vals, topk_idx = jax.lax.top_k(logits, K)
            topk_gates = jax.nn.softmax(topk_vals, axis=-1)
            n = xf.shape[0]
            gates = jnp.zeros((n, E), dtype=xf.dtype).at[jnp.arange(n)[:, None], topk_idx].set(topk_gates)
            h = jnp.einsum('nd,ehd->neh', xf, exp_w1)
            h = jax.nn.silu(h)
            eo = jnp.einsum('neh,edh->ned', h, exp_w2)
            sel = jnp.einsum('ned,ne->nd', eo, gates)
            return (sh + sel).reshape(b, s, d)
        key = jax.random.key(seed)
        ks = jax.random.split(key, 16)
        sd = 1.0 / np.sqrt(D)
        inp = {'x': jax.random.normal(ks[0], (B, T, D), jnp.float32), 'encoder_output': jax.random.normal(ks[1], (B, S_ENC, D), jnp.float32), 'tgt_mask': jnp.tril(jnp.ones((T, T), jnp.int32))[None].repeat(B, 0), 'src_mask': jnp.ones((B, T, S_ENC), jnp.int32), 'norm1_w': jnp.ones((D,), jnp.float32), 'norm2_w': jnp.ones((D,), jnp.float32), 'norm3_w': jnp.ones((D,), jnp.float32), 'sa_wq': jax.random.normal(ks[2], (D, D), jnp.float32) * sd, 'sa_wk': jax.random.normal(ks[3], (D, D), jnp.float32) * sd, 'sa_wv': jax.random.normal(ks[4], (D, D), jnp.float32) * sd, 'sa_wo': jax.random.normal(ks[5], (D, D), jnp.float32) * sd, 'ca_wq': jax.random.normal(ks[6], (D, D), jnp.float32) * sd, 'ca_wk': jax.random.normal(ks[7], (D, D), jnp.float32) * sd, 'ca_wv': jax.random.normal(ks[8], (D, D), jnp.float32) * sd, 'ca_wo': jax.random.normal(ks[9], (D, D), jnp.float32) * sd, 'gate_w': jax.random.normal(ks[10], (E, D), jnp.float32) * 0.02, 'exp_w1': jax.random.normal(ks[11], (E, HID, D), jnp.float32) * sd, 'exp_w2': jax.random.normal(ks[12], (E, D, HID), jnp.float32) / np.sqrt(HID), 'sh_w1': jax.random.normal(ks[13], (HID, D), jnp.float32) * sd, 'sh_w2': jax.random.normal(ks[14], (D, HID), jnp.float32) / np.sqrt(HID)}
        return inp
    _L1_xattn_all = _L1_xattn_setup()
    _L1_xattn_in = {k: v for k, v in _L1_xattn_all.items() if k in ('norm1_w', 'norm2_w', 'norm3_w', 'sa_wq', 'sa_wk', 'sa_wv', 'sa_wo', 'ca_wq', 'ca_wk', 'ca_wv', 'ca_wo', 'gate_w', 'exp_w1', 'exp_w2', 'sh_w1', 'sh_w2')}
    del _L1_xattn_all

    def _L2_xattn_setup():
        import jax, jax.numpy as jnp
        import numpy as np
        H = 128
        NH = 16
        HD = H // NH
        EPS = 1e-05

        def _split_heads(x, B, L):
            return x.reshape(B, L, NH, HD).transpose(0, 2, 1, 3)
        key = jax.random.key(seed)
        ks = jax.random.split(key, 16)
        B, LQ, LK = (2, 128, 256)
        s = 1.0 / np.sqrt(H)
        inp = {'query': jax.random.normal(ks[0], (B, LQ, H), jnp.float32), 'key': jax.random.normal(ks[1], (B, LK, H), jnp.float32), 'value': jax.random.normal(ks[2], (B, LK, H), jnp.float32), 'mask': jax.random.randint(ks[3], (B, LQ, LK), 0, 2, jnp.int32), 'Wq': jax.random.normal(ks[4], (H, H), jnp.float32) * s, 'bq': jnp.zeros((H,), jnp.float32), 'Wk': jax.random.normal(ks[5], (H, H), jnp.float32) * s, 'bk': jnp.zeros((H,), jnp.float32), 'Wv': jax.random.normal(ks[6], (H, H), jnp.float32) * s, 'bv': jnp.zeros((H,), jnp.float32), 'Wo': jax.random.normal(ks[7], (H, H), jnp.float32) * s, 'bo': jnp.zeros((H,), jnp.float32), 'ln_g': jnp.ones((H,), jnp.float32), 'ln_b': jnp.zeros((H,), jnp.float32)}
        return inp
    _L2_xattn_all = _L2_xattn_setup()
    _L2_xattn_in = {k: v for k, v in _L2_xattn_all.items() if k in ('Wq', 'bq', 'Wk', 'bk', 'Wv', 'bv', 'Wo', 'bo', 'ln_g', 'ln_b')}
    del _L2_xattn_all

    def _L3_xattn_setup():
        import jax, jax.numpy as jnp
        import numpy as np
        B, L, D = (32, 64, 128)
        H, DK, DV = (8, 16, 16)

        def _xavier(key, shape):
            fan_in, fan_out = (shape[0], shape[1])
            std = (2.0 / (fan_in + fan_out)) ** 0.5
            return std * jax.random.normal(key, shape, dtype=jnp.float32)
        key = jax.random.key(seed)
        ks = jax.random.split(key, 11)
        return {'Q': jax.random.normal(ks[0], (B, L, D), jnp.float32), 'K': jax.random.normal(ks[1], (B, L, D), jnp.float32), 'V': jax.random.normal(ks[2], (B, L, D), jnp.float32), 'W_q': _xavier(ks[3], (D, H * DK)), 'W_k': _xavier(ks[4], (D, H * DK)), 'W_v': _xavier(ks[5], (D, H * DV)), 'W_o': _xavier(ks[6], (H * DV, D)), 'w1': _xavier(ks[7], (D, D)), 'b1': jnp.zeros((D,), jnp.float32), 'w2': _xavier(ks[8], (D, D)), 'b2': jnp.zeros((D,), jnp.float32)}
    _L3_xattn_all = _L3_xattn_setup()
    _L3_xattn_in = {k: v for k, v in _L3_xattn_all.items() if k in ('W_q', 'W_k', 'W_v', 'W_o', 'w1', 'b1', 'w2', 'b2')}
    del _L3_xattn_all
    return {'x': x, 'ctx_1024': ctx_1024, 'mask_BxSxS2_ik0': mask_BxSxS2_ik0, 'mask_BxSxS2_if1': mask_BxSxS2_if1, 'mask_BxSxS_ik0': mask_BxSxS_ik0, 'mask_BxSxS2_ik1': mask_BxSxS2_ik1, 'L0_xattn_sa_wq': _L0_xattn_in['sa_wq'], 'L0_xattn_sa_bq': _L0_xattn_in['sa_bq'], 'L0_xattn_sa_wk': _L0_xattn_in['sa_wk'], 'L0_xattn_sa_bk': _L0_xattn_in['sa_bk'], 'L0_xattn_sa_wv': _L0_xattn_in['sa_wv'], 'L0_xattn_sa_bv': _L0_xattn_in['sa_bv'], 'L0_xattn_sa_wo': _L0_xattn_in['sa_wo'], 'L0_xattn_sa_bo': _L0_xattn_in['sa_bo'], 'L0_xattn_ca_wq': _L0_xattn_in['ca_wq'], 'L0_xattn_ca_bq': _L0_xattn_in['ca_bq'], 'L0_xattn_ca_wk': _L0_xattn_in['ca_wk'], 'L0_xattn_ca_bk': _L0_xattn_in['ca_bk'], 'L0_xattn_ca_wv': _L0_xattn_in['ca_wv'], 'L0_xattn_ca_bv': _L0_xattn_in['ca_bv'], 'L0_xattn_ca_wo': _L0_xattn_in['ca_wo'], 'L0_xattn_ca_bo': _L0_xattn_in['ca_bo'], 'L0_xattn_ff_w1': _L0_xattn_in['ff_w1'], 'L0_xattn_ff_b1': _L0_xattn_in['ff_b1'], 'L0_xattn_ff_w2': _L0_xattn_in['ff_w2'], 'L0_xattn_ff_b2': _L0_xattn_in['ff_b2'], 'L0_xattn_ln1_g': _L0_xattn_in['ln1_g'], 'L0_xattn_ln1_b': _L0_xattn_in['ln1_b'], 'L0_xattn_ln2_g': _L0_xattn_in['ln2_g'], 'L0_xattn_ln2_b': _L0_xattn_in['ln2_b'], 'L0_xattn_ln3_g': _L0_xattn_in['ln3_g'], 'L0_xattn_ln3_b': _L0_xattn_in['ln3_b'], 'L1_xattn_norm1_w': _L1_xattn_in['norm1_w'], 'L1_xattn_norm2_w': _L1_xattn_in['norm2_w'], 'L1_xattn_norm3_w': _L1_xattn_in['norm3_w'], 'L1_xattn_sa_wq': _L1_xattn_in['sa_wq'], 'L1_xattn_sa_wk': _L1_xattn_in['sa_wk'], 'L1_xattn_sa_wv': _L1_xattn_in['sa_wv'], 'L1_xattn_sa_wo': _L1_xattn_in['sa_wo'], 'L1_xattn_ca_wq': _L1_xattn_in['ca_wq'], 'L1_xattn_ca_wk': _L1_xattn_in['ca_wk'], 'L1_xattn_ca_wv': _L1_xattn_in['ca_wv'], 'L1_xattn_ca_wo': _L1_xattn_in['ca_wo'], 'L1_xattn_gate_w': _L1_xattn_in['gate_w'], 'L1_xattn_exp_w1': _L1_xattn_in['exp_w1'], 'L1_xattn_exp_w2': _L1_xattn_in['exp_w2'], 'L1_xattn_sh_w1': _L1_xattn_in['sh_w1'], 'L1_xattn_sh_w2': _L1_xattn_in['sh_w2'], 'L2_xattn_Wq': _L2_xattn_in['Wq'], 'L2_xattn_bq': _L2_xattn_in['bq'], 'L2_xattn_Wk': _L2_xattn_in['Wk'], 'L2_xattn_bk': _L2_xattn_in['bk'], 'L2_xattn_Wv': _L2_xattn_in['Wv'], 'L2_xattn_bv': _L2_xattn_in['bv'], 'L2_xattn_Wo': _L2_xattn_in['Wo'], 'L2_xattn_bo': _L2_xattn_in['bo'], 'L2_xattn_ln_g': _L2_xattn_in['ln_g'], 'L2_xattn_ln_b': _L2_xattn_in['ln_b'], 'L3_xattn_W_q': _L3_xattn_in['W_q'], 'L3_xattn_W_k': _L3_xattn_in['W_k'], 'L3_xattn_W_v': _L3_xattn_in['W_v'], 'L3_xattn_W_o': _L3_xattn_in['W_o'], 'L3_xattn_w1': _L3_xattn_in['w1'], 'L3_xattn_b1': _L3_xattn_in['b1'], 'L3_xattn_w2': _L3_xattn_in['w2'], 'L3_xattn_b2': _L3_xattn_in['b2']}

def reference(x, ctx_1024, mask_BxSxS2_ik0, mask_BxSxS2_if1, mask_BxSxS_ik0, mask_BxSxS2_ik1, L0_xattn_sa_wq, L0_xattn_sa_bq, L0_xattn_sa_wk, L0_xattn_sa_bk, L0_xattn_sa_wv, L0_xattn_sa_bv, L0_xattn_sa_wo, L0_xattn_sa_bo, L0_xattn_ca_wq, L0_xattn_ca_bq, L0_xattn_ca_wk, L0_xattn_ca_bk, L0_xattn_ca_wv, L0_xattn_ca_bv, L0_xattn_ca_wo, L0_xattn_ca_bo, L0_xattn_ff_w1, L0_xattn_ff_b1, L0_xattn_ff_w2, L0_xattn_ff_b2, L0_xattn_ln1_g, L0_xattn_ln1_b, L0_xattn_ln2_g, L0_xattn_ln2_b, L0_xattn_ln3_g, L0_xattn_ln3_b, L1_xattn_norm1_w, L1_xattn_norm2_w, L1_xattn_norm3_w, L1_xattn_sa_wq, L1_xattn_sa_wk, L1_xattn_sa_wv, L1_xattn_sa_wo, L1_xattn_ca_wq, L1_xattn_ca_wk, L1_xattn_ca_wv, L1_xattn_ca_wo, L1_xattn_gate_w, L1_xattn_exp_w1, L1_xattn_exp_w2, L1_xattn_sh_w1, L1_xattn_sh_w2, L2_xattn_Wq, L2_xattn_bq, L2_xattn_Wk, L2_xattn_bk, L2_xattn_Wv, L2_xattn_bv, L2_xattn_Wo, L2_xattn_bo, L2_xattn_ln_g, L2_xattn_ln_b, L3_xattn_W_q, L3_xattn_W_k, L3_xattn_W_v, L3_xattn_W_o, L3_xattn_w1, L3_xattn_b1, L3_xattn_w2, L3_xattn_b2):
    import jax
    import jax.numpy as jnp

    def _L0_xattn_ref(x, enc_output, tgt_mask, memory_mask, sa_wq, sa_bq, sa_wk, sa_bk, sa_wv, sa_bv, sa_wo, sa_bo, ca_wq, ca_bq, ca_wk, ca_bk, ca_wv, ca_bv, ca_wo, ca_bo, ff_w1, ff_b1, ff_w2, ff_b2, ln1_g, ln1_b, ln2_g, ln2_b, ln3_g, ln3_b):
        import jax, jax.numpy as jnp
        import numpy as np
        B, S, D, H, DFF = (2, 256, 128, 16, 512)
        DK = D // H
        LN_EPS = 1e-05

        def _mha(q, k, v, mask, wq, bq, wk, bk, wv, bv, wo, bo):
            b, sq, _ = q.shape
            sk = k.shape[1]
            Q = (q @ wq + bq).reshape(b, sq, H, DK).transpose(0, 2, 1, 3)
            K = (k @ wk + bk).reshape(b, sk, H, DK).transpose(0, 2, 1, 3)
            V = (v @ wv + bv).reshape(b, sk, H, DK).transpose(0, 2, 1, 3)
            scores = jnp.einsum('bhqd,bhkd->bhqk', Q, K) / np.float32(np.sqrt(DK))
            if mask is not None:
                scores = jnp.where(mask[:, None, :, :] == 0, jnp.float32(-1e+20), scores)
            A = jax.nn.softmax(scores, axis=-1)
            out = jnp.einsum('bhqk,bhkd->bhqd', A, V).transpose(0, 2, 1, 3).reshape(b, sq, D)
            return out @ wo + bo

        def _ln(x, g, b):
            m = jnp.mean(x, axis=-1, keepdims=True)
            v = jnp.var(x, axis=-1, keepdims=True)
            return (x - m) * jax.lax.rsqrt(v + LN_EPS) * g + b
        sa = _mha(x, x, x, tgt_mask, sa_wq, sa_bq, sa_wk, sa_bk, sa_wv, sa_bv, sa_wo, sa_bo)
        x = _ln(x + sa, ln1_g, ln1_b)
        ca = _mha(x, enc_output, enc_output, memory_mask, ca_wq, ca_bq, ca_wk, ca_bk, ca_wv, ca_bv, ca_wo, ca_bo)
        x = _ln(x + ca, ln2_g, ln2_b)
        ff = jax.nn.relu(x @ ff_w1 + ff_b1) @ ff_w2 + ff_b2
        x = _ln(x + ff, ln3_g, ln3_b)
        return x

    def _L1_xattn_ref(x, encoder_output, tgt_mask, src_mask, norm1_w, norm2_w, norm3_w, sa_wq, sa_wk, sa_wv, sa_wo, ca_wq, ca_wk, ca_wv, ca_wo, gate_w, exp_w1, exp_w2, sh_w1, sh_w2):
        import jax, jax.numpy as jnp
        import numpy as np
        B, T, S_ENC, D, H, E, K = (4, 128, 64, 128, 16, 8, 2)
        DK = D // H
        HID = 4 * D
        NEG = -65504.0
        EPS = 1e-05

        def rmsnorm(x, w):
            return w * (x * jax.lax.rsqrt(jnp.mean(x * x, axis=-1, keepdims=True) + EPS))

        def mha(xq, xk, xv, mask, wq, wk, wv, wo):
            q = jnp.einsum('bsd,ed->bse', xq, wq).reshape(xq.shape[0], -1, H, DK).transpose(0, 2, 1, 3)
            k = jnp.einsum('bsd,ed->bse', xk, wk).reshape(xk.shape[0], -1, H, DK).transpose(0, 2, 1, 3)
            v = jnp.einsum('bsd,ed->bse', xv, wv).reshape(xv.shape[0], -1, H, DK).transpose(0, 2, 1, 3)
            scores = jnp.einsum('bhqd,bhkd->bhqk', q, k) / jnp.sqrt(jnp.float32(DK))
            scores = jnp.where(mask[:, None, :, :] == 0, NEG, scores)
            attn = jax.nn.softmax(scores, axis=-1)
            out = jnp.einsum('bhqk,bhkd->bhqd', attn, v)
            out = out.transpose(0, 2, 1, 3).reshape(xq.shape[0], -1, D)
            return jnp.einsum('bsd,ed->bse', out, wo)

        def moe_ffn(x, gate_w, exp_w1, exp_w2, sh_w1, sh_w2):
            b, s, d = x.shape
            xf = x.reshape(-1, d)
            sh = jnp.einsum('nd,hd->nh', xf, sh_w1)
            sh = jax.nn.silu(sh)
            sh = jnp.einsum('nh,dh->nd', sh, sh_w2)
            logits = jnp.einsum('nd,ed->ne', xf, gate_w)
            topk_vals, topk_idx = jax.lax.top_k(logits, K)
            topk_gates = jax.nn.softmax(topk_vals, axis=-1)
            n = xf.shape[0]
            gates = jnp.zeros((n, E), dtype=xf.dtype).at[jnp.arange(n)[:, None], topk_idx].set(topk_gates)
            h = jnp.einsum('nd,ehd->neh', xf, exp_w1)
            h = jax.nn.silu(h)
            eo = jnp.einsum('neh,edh->ned', h, exp_w2)
            sel = jnp.einsum('ned,ne->nd', eo, gates)
            return (sh + sel).reshape(b, s, d)
        xn = rmsnorm(x, norm1_w)
        h = x + mha(xn, xn, xn, tgt_mask, sa_wq, sa_wk, sa_wv, sa_wo)
        hn = rmsnorm(h, norm2_w)
        h = h + mha(hn, encoder_output, encoder_output, src_mask, ca_wq, ca_wk, ca_wv, ca_wo)
        hn = rmsnorm(h, norm3_w)
        return h + moe_ffn(hn, gate_w, exp_w1, exp_w2, sh_w1, sh_w2)

    def _L2_xattn_ref(query, key, value, mask, Wq, bq, Wk, bk, Wv, bv, Wo, bo, ln_g, ln_b):
        import jax, jax.numpy as jnp
        import numpy as np
        H = 128
        NH = 16
        HD = H // NH
        EPS = 1e-05

        def _split_heads(x, B, L):
            return x.reshape(B, L, NH, HD).transpose(0, 2, 1, 3)
        B, LQ, _ = query.shape
        LK = key.shape[1]
        Q = _split_heads(query @ Wq.T + bq, B, LQ)
        K = _split_heads(key @ Wk.T + bk, B, LK)
        V = _split_heads(value @ Wv.T + bv, B, LK)
        scores = jnp.einsum('bhqd,bhkd->bhqk', Q, K) / np.sqrt(HD)
        scores = jnp.where(mask[:, None, :, :] == 0, jnp.float32(-1000000000.0), scores)
        attn = jax.nn.softmax(scores, axis=-1)
        ctx = jnp.einsum('bhqk,bhkd->bhqd', attn, V)
        ctx = ctx.transpose(0, 2, 1, 3).reshape(B, LQ, H)
        out = ctx @ Wo.T + bo
        x = out + query
        mu = jnp.mean(x, axis=-1, keepdims=True)
        var = jnp.mean(jnp.square(x - mu), axis=-1, keepdims=True)
        return (x - mu) / jnp.sqrt(var + EPS) * ln_g + ln_b

    def _L3_xattn_ref(Q, K, V, W_q, W_k, W_v, W_o, w1, b1, w2, b2):
        import jax, jax.numpy as jnp
        import numpy as np
        B, L, D = (32, 64, 128)
        H, DK, DV = (8, 16, 16)

        def _xavier(key, shape):
            fan_in, fan_out = (shape[0], shape[1])
            std = (2.0 / (fan_in + fan_out)) ** 0.5
            return std * jax.random.normal(key, shape, dtype=jnp.float32)
        b, lq, _ = Q.shape
        lk = K.shape[1]
        Qh = (Q @ W_q).reshape(b, lq, H, DK)
        Kh = (K @ W_k).reshape(b, lk, H, DK)
        Vh = (V @ W_v).reshape(b, lk, H, DV)
        scale = 1.0 / jnp.sqrt(jnp.float32(DK))
        scores = jnp.einsum('bqhd,bkhd->bhqk', Qh, Kh) * scale
        attn = jax.nn.softmax(scores, axis=-1)
        ctx = jnp.einsum('bhqk,bkhd->bqhd', attn, Vh).reshape(b, lq, H * DV)
        attn_out = ctx @ W_o
        X = Q + attn_out
        h = jax.nn.relu(X @ w1.T + b1)
        ffn_out = h @ w2.T + b2
        return ffn_out + X
    x = _L0_xattn_ref(x, ctx_1024, mask_BxSxS2_ik0, mask_BxSxS2_if1, L0_xattn_sa_wq, L0_xattn_sa_bq, L0_xattn_sa_wk, L0_xattn_sa_bk, L0_xattn_sa_wv, L0_xattn_sa_bv, L0_xattn_sa_wo, L0_xattn_sa_bo, L0_xattn_ca_wq, L0_xattn_ca_bq, L0_xattn_ca_wk, L0_xattn_ca_bk, L0_xattn_ca_wv, L0_xattn_ca_bv, L0_xattn_ca_wo, L0_xattn_ca_bo, L0_xattn_ff_w1, L0_xattn_ff_b1, L0_xattn_ff_w2, L0_xattn_ff_b2, L0_xattn_ln1_g, L0_xattn_ln1_b, L0_xattn_ln2_g, L0_xattn_ln2_b, L0_xattn_ln3_g, L0_xattn_ln3_b)
    x = _L1_xattn_ref(x, ctx_1024, mask_BxSxS_ik0, mask_BxSxS2_if1, L1_xattn_norm1_w, L1_xattn_norm2_w, L1_xattn_norm3_w, L1_xattn_sa_wq, L1_xattn_sa_wk, L1_xattn_sa_wv, L1_xattn_sa_wo, L1_xattn_ca_wq, L1_xattn_ca_wk, L1_xattn_ca_wv, L1_xattn_ca_wo, L1_xattn_gate_w, L1_xattn_exp_w1, L1_xattn_exp_w2, L1_xattn_sh_w1, L1_xattn_sh_w2)
    x = _L2_xattn_ref(x, ctx_1024, ctx_1024, mask_BxSxS2_ik1, L2_xattn_Wq, L2_xattn_bq, L2_xattn_Wk, L2_xattn_bk, L2_xattn_Wv, L2_xattn_bv, L2_xattn_Wo, L2_xattn_bo, L2_xattn_ln_g, L2_xattn_ln_b)
    x = _L3_xattn_ref(x, ctx_1024, ctx_1024, L3_xattn_W_q, L3_xattn_W_k, L3_xattn_W_v, L3_xattn_W_o, L3_xattn_w1, L3_xattn_b1, L3_xattn_w2, L3_xattn_b2)
    return x

_drawn_inputs = setup_inputs


def setup_inputs(seed=0):
    import zlib

    import numpy as np

    out = dict(_drawn_inputs(seed))
    spreads = {'L0_xattn_sa_bq': (0.0, 0.8),
     'L0_xattn_sa_bk': (0.0, 0.8),
     'L0_xattn_sa_bv': (0.0, 0.1),
     'L0_xattn_sa_bo': (0.0, 0.1),
     'L0_xattn_ca_bq': (0.0, 0.8),
     'L0_xattn_ca_bk': (0.0, 0.8),
     'L0_xattn_ca_bv': (0.0, 0.1),
     'L0_xattn_ca_bo': (0.0, 0.1),
     'L0_xattn_ff_b1': (0.0, 0.1),
     'L0_xattn_ff_b2': (0.0, 0.1),
     'L0_xattn_ln1_g': (1.0, 0.2),
     'L0_xattn_ln1_b': (0.0, 0.1),
     'L0_xattn_ln2_g': (1.0, 0.2),
     'L0_xattn_ln2_b': (0.0, 0.1),
     'L0_xattn_ln3_g': (1.0, 0.2),
     'L0_xattn_ln3_b': (0.0, 0.1),
     'L1_xattn_norm1_w': (1.0, 0.2),
     'L1_xattn_norm2_w': (1.0, 0.2),
     'L1_xattn_norm3_w': (1.0, 0.2),
     'L2_xattn_bq': (0.0, 0.563),
     'L2_xattn_bk': (0.0, 0.8),
     'L2_xattn_bv': (0.0, 0.1),
     'L2_xattn_bo': (0.0, 0.1),
     'L2_xattn_ln_g': (1.0, 0.2),
     'L2_xattn_ln_b': (0.0, 0.1),
     'L3_xattn_b1': (0.0, 0.1),
     'L3_xattn_b2': (0.0, 0.1)}
    factors = {'L0_xattn_sa_wq': 8.0, 'L0_xattn_sa_wk': 7.5, 'L0_xattn_ca_wq': 8.0, 'L0_xattn_ca_wk': 8.0}
    for name, (base, spread) in spreads.items():
        noise = np.random.default_rng([zlib.crc32(name.encode()), seed]).standard_normal(out[name].shape)
        drawn = base * np.exp(spread * noise) if base else spread * noise
        out[name] = jnp.asarray(drawn.astype(out[name].dtype))
    for name, factor in factors.items():
        out[name] = (out[name] * factor).astype(out[name].dtype)
    return out
```

```python
from contextlib import ExitStack

import numpy as np

import concourse.bass as bass
from concourse import mybir

F32 = mybir.dt.float32
BF16 = mybir.dt.bfloat16
I32 = mybir.dt.int32
U32 = mybir.dt.uint32
ACT = mybir.ActivationFunctionType
ALU = mybir.AluOpType
AX = mybir.AxisListType

B, S, D = 32, 64, 128
TOK = 2 * S
NP = B // 2
E, HID = 8, 512
HC = HID // 128
TILE = 512
NT = B * S // TILE
SUB = TILE // 128
EPS = 1e-5
NEG = -1e20

HEADS = [16, 16, 16, 16, 16, 8]
SELF = [True, False, True, False, False, False]
MASKED = [True, True, True, True, True, False]
POST = ["ln", "ln", "rms", "rms", "ln", "none"]
LN_BEFORE = [0, NP, 2 * NP, 2 * NP, 2 * NP, 3 * NP]

VECS = ["bq0", "bk0", "bq1", "bk1", "bq4", "bk4", "bv0", "bv1", "bv4",
        "g1", "b1", "g2", "b2", "n1", "n2", "n3", "gL2", "bL2", "ffb2", "l3b1", "l3b2"] + \
       [f"ffb1_{c}" for c in range(HC)]
VCOL = {name: n for n, name in enumerate(VECS)}
ROWS = ["g1", "b1", "g2", "b2", "g3", "b3", "gL2", "bL2", "bo0", "bo1", "bo4"]
ROW = {name: n for n, name in enumerate(ROWS)}
BIASED = {0: 0, 1: 1, 4: 2}
C_ID, C_G, C_J16, C_J8, C_IOTA, C_END = 0, 128, 132, 136, 138, 146

OFF_PROJ, OFF_V, OFF_SCORE, OFF_PV, OFF_OUT, OFF_XT = 0, 1, 2, 3, 4, 5
LAST_OFF = OFF_XT
STEADY = 6


class Pair:

    def __init__(self, phase, i, half, parity):
        self.phase, self.i, self.p = phase, i, parity
        self.n = i + NP * phase
        self.half = half + NP // 2 * phase


def run_slots(eng, group, slot):

    def fixed(s):
        def at(off):
            m = s - off
            if not 0 <= m < 2 * NP:
                return None
            i = m % NP
            return Pair(2 * group + m // NP, i, i // 2, i % 2)
        return at

    for part in range(2):
        for s in range(STEADY):
            slot(fixed(part * NP + s))
        with eng.Fori(STEADY // 2, NP // 2) as h:
            for u in range(2):
                def at(off, h=h, u=u):
                    return Pair(2 * group + part, 2 * h + (u - off), h + (u - off) // 2, (u - off) % 2)
                slot(at)
    for s in range(2 * NP, 2 * NP + LAST_OFF):
        slot(fixed(s))


class Mlp:

    def __init__(self, name, phase, experts, chunks, func, w1, w2, b1, b2, gated):
        self.name, self.phase, self.experts, self.chunks, self.func = name, phase, experts, chunks, func
        self.w1, self.w2, self.b1, self.b2, self.gated = w1, w2, b1, b2, gated
        self.n = experts * chunks
        self.ring = min(4, self.n)
        assert self.n % self.ring == 0


def build(nc, a, out_t):
    ctx = ExitStack()
    with ctx:
        def sb(name, shape, dt=F32):
            return ctx.enter_context(nc.sbuf_tensor(name, shape, dt))

        def sem(name):
            return ctx.enter_context(nc.semaphore(name))

        cst = sb("cst", [128, C_END])
        sel = sb("sel", [128, E, 128])
        idb = sb("idb", [128, 128], BF16)
        vec = sb("vec", [128, len(VECS)])
        rows = sb("rows", [128, len(ROWS), D])
        wat = sb("wat", [128, 6, 4, D])
        ffw1, ffw2 = sb("ffw1", [128, 1, HID]), sb("ffw2", [128, 1, HC, D])
        mow1, mow2 = sb("mow1", [128, 1 + E, HID]), sb("mow2", [128, 1 + E, HC, D])
        l3w1, l3w2 = sb("l3w1", [128, 1, D]), sb("l3w2", [128, 1, 1, D])
        gatew = sb("gatew", [128, 128])
        ident, maskg = cst[:, C_ID:C_ID + 128], cst[:, C_G:C_G + 4]
        iota = cst[:, C_IOTA:C_IOTA + E]
        x_tok = sb("x_tok", [128, NP, D])
        x_t = sb("x_t", [128, NP * TOK])
        bv_cols = sb("bv_cols", [128, 3, TOK])
        row_bias = sb("row_bias", [128, 3, D])
        half_neg = sb("half_neg", [128, SUB])

        stage_x = sb("stage_x", [128, 2, TOK])
        stage_kv = sb("stage_kv", [128, 2, TOK])
        stage_m = sb("stage_m", [128, 2, S], I32)
        q_t, k_t = sb("q_t", [128, 2, TOK]), sb("k_t", [128, 2, TOK])
        q_by_g = sb("q_by_g", [128, 2, 4, TOK])
        k_by_j = sb("k_by_j", [128, 2, 4, TOK])
        v_16 = sb("v_16", [128, 2, 2, 8, 32])
        v_8 = sb("v_8", [128, 2, 2, 4, 32])
        neg_m = sb("neg_m", [128, 2, S], BF16)
        top = sb("top", [128, 2, 16])
        prob = sb("prob", [128, 2, 16 * S])
        prob_t = sb("prob_t", [128, 2, 2, 512])
        total = sb("total", [128, 2, 16])
        inv = sb("inv", [128, 2, D])
        inv_t = sb("inv_t", [128, 2, TOK])
        heads_t = sb("heads_t", [128, 2, TOK])
        y = sb("y", [128, 2, D])
        squares = sb("squares", [128, 2, D])
        stats = sb("stats", [128, 2, 6])
        moments = sb("moments", [128, 2, 2])
        spread = sb("spread", [128, 2, 1])
        rstd = sb("rstd", [128, 2, 1])
        normed = sb("normed", [128, 2, D])
        scaled = sb("scaled", [128, 2, D])

        hid = sb("hid", [128, 4, TILE])
        gated_h = sb("gated_h", [128, 4, TILE])
        mlp_o = sb("mlp_o", [128, TILE])
        y4 = sb("y4", [128, SUB, D])
        n4 = sb("n4", [128, SUB, D])
        z4 = sb("z4", [128, SUB, D])
        w4 = sb("w4", [128, SUB, D])
        st4 = sb("st4", [128, SUB, 6])
        mo4 = sb("mo4", [128, SUB, 2])
        sp4 = sb("sp4", [128, SUB])
        rs4 = sb("rs4", [128, SUB])
        sp4b = sb("sp4b", [128, SUB])
        rs4b = sb("rs4b", [128, SUB])
        gates_t = sb("gates_t", [128, NP * TOK])
        logit_t = sb("logit_t", [128, TILE])
        logit = sb("logit", [128, SUB, E])
        best = sb("best", [128, SUB, 8])
        best_at = sb("best_at", [128, SUB, 8], U32)
        best_f = sb("best_f", [128, SUB, 8])
        gap = sb("gap", [128, SUB])
        e_gap = sb("e_gap", [128, SUB])
        den = sb("den", [128, SUB])
        gate1 = sb("gate1", [128, SUB])
        gate2 = sb("gate2", [128, SUB])
        hot1 = sb("hot1", [128, SUB, E])
        hot2 = sb("hot2", [128, SUB, E])
        gates = sb("gates", [128, SUB, E])

        ps = ctx.enter_context(nc.psum_tensor("ps", [128, 8, 512], F32))
        B_PROJ, B_HEADS, B_OUT, B_XT = 4, 5, 6, 7
        B_ACC, B_TAIL, B_GATE = 5, 7, (4, 6)

        loaded = {k: sem(f"loaded_{k}") for k in ("small", "x_tok", "x_t", "rows", "wat", "ff", "mo1", "mo2", "l3", "sel")}
        set_zero, set_id, set_bv, set_mm, set_bias = (
            sem(k) for k in ("set_zero", "set_id", "set_bv", "set_mm", "set_bias"))
        ld_x = [sem(f"ld_x{p}") for p in range(2)]
        ld_kv = [sem(f"ld_kv{p}") for p in range(2)]
        ld_m = [sem(f"ld_m{p}") for p in range(2)]
        proj_d, vproj_d, score_d, pt0_d, pt1_d, rt_d, pv_d, out_d, xt_d = (
            sem(k) for k in ("proj_d", "vproj_d", "score_d", "pt0_d", "pt1_d", "rt_d", "pv_d", "out_d", "xt_d"))
        q_e, k_e, v_e, exp_d, pt0_e, pt1_e, rt_e, xt_e = (
            sem(k) for k in ("q_e", "k_e", "v_e", "exp_d", "pt0_e", "pt1_e", "rt_e", "xt_e"))
        top_d, sub_d, sum_d, inv_d, heads_d, y_d, bns_d, agg_d, spread_d, norm_d = (
            sem(k) for k in ("top_d", "sub_d", "sum_d", "inv_d", "heads_d", "y_d", "bns_d", "agg_d", "spread_d", "norm_d"))
        neg_d, qg_d, kj_d, rstd_d, gsc_d, res_d = (sem(k) for k in ("neg_d", "qg_d", "kj_d", "rstd_d", "gsc_d", "res_d"))

        mlps = [
            Mlp("ff", 1, 1, HC, ACT.Relu, ffw1, ffw2, "ffb1_", "ffb2", False),
            Mlp("mo", 3, 1 + E, HC, ACT.Silu, mow1, mow2, None, None, True),
            Mlp("l3", 5, 1, 1, ACT.Relu, l3w1, l3w2, "l3b1", "l3b2", False),
        ]
        for m in mlps:
            m.h_d, m.act_d, m.gated_d, m.acc_d = (sem(f"{m.name}_{k}") for k in ("h_d", "act_d", "gated_d", "acc_d"))
            m.gate_d = sem(f"{m.name}_gate_d")
            m.o_e, m.turn_d, m.y_d, m.n_d, m.back_d, m.xt_e, m.res_d = (
                sem(f"{m.name}_{k}") for k in ("o_e", "turn_d", "y_d", "n_d", "back_d", "xt_e", "res_d"))
        ff, mo, l3 = mlps
        f_st, f_ag, f_sp, f_rs, f_nn, f_gm, f_x, f_sp2, f_ms, f_rs2 = (
            sem(f"f_{k}") for k in ("st", "ag", "sp", "rs", "nn", "gm", "x", "sp2", "ms", "rs2"))
        r_lt, r_le, r_l, r_lc, r_mx, r_ix, r_fx, r_gap, r_exp, r_den, r_g1, r_g2, r_h, r_a, r_g, r_t, r_te = (
            sem(f"r_{k}") for k in ("lt", "le", "l", "lc", "mx", "ix", "fx", "gap", "exp", "den", "g1", "g2",
                                    "h", "a", "g", "t", "te"))
        stored = sem("stored")

        def v(name):
            return vec[:, VCOL[name]:VCOL[name] + 1]

        def heads(pair):
            return HEADS[pair.phase]

        def tiles(eng, body):
            body(0, True)
            with eng.Fori(1, NT) as t:
                body(t, False)

        def wait_apart(eng, sem_, value):
            eng.wait_ge(loaded["small"], 48)
            eng.wait_ge(sem_, value)

        def wait_pair(eng, sem_, pair, back=0, apart=False):
            if isinstance(pair.n, int) and pair.n - back < 0:
                return
            (wait_apart if apart else lambda e, *x: e.wait_ge(*x))(eng, sem_, pair.n + (1 - back))

        block = ctx.enter_context(nc.Block())

        @block.sync
        def _(sp):
            sp.dma_start(x_t[:, :], a["x_t"]).then_inc(loaded["x_t"], 16)
            sp.dma_start(wat[:, 0:2, :, :], a["wat"][:, 0:2, :, :]).then_inc(loaded["wat"], 16)
            sp.dma_start(cst[:, :], a["cst"]).then_inc(loaded["small"], 16)
            sp.dma_start(vec[:, :], a["vec"]).then_inc(loaded["small"], 16)
            sp.dma_start(gatew[:, :], a["gatew"]).then_inc(loaded["small"], 16)
            sp.dma_start(x_tok[:, :, :], a["x_tok"].rearrange("i p d -> p i d")).then_inc(loaded["x_tok"], 16)
            sp.dma_start(rows[:, :, :], a["rows"].partition_broadcast(128)).then_inc(loaded["rows"], 16)
            sp.dma_start(wat[:, 2:6, :, :], a["wat"][:, 2:6, :, :]).then_inc(loaded["wat"], 16)
            sp.wait_ge(set_zero, 5)
            sp.dma_start(sel[0:E, :, :], a["sel"]).then_inc(loaded["sel"], 16)
            masks = [a["m0"], a["m1"], a["m2"], a["m1"], a["m4"], None]

            def slot(at):
                pr = at(OFF_PROJ)
                if pr is None:
                    return
                ph, i, p = pr.phase, pr.i, pr.p
                if ph == 0:
                    sp.wait_ge(loaded["x_t"], 16)
                elif ph % 2 == 0:
                    m = mlps[ph // 2 - 1]
                    sp.wait_ge(m.xt_e, i // SUB + 1 if isinstance(i, int) else NT)
                wait_pair(sp, proj_d, pr, 2)
                tok = x_t[:, bass.ds(i * TOK, TOK)]
                sp.dma_start(stage_x[:, p, :], tok).then_inc(ld_x[p], 16)
                src = tok if SELF[ph] else a["ctx_t"][bass.ds(i, 1), :, :].rearrange("a p t -> p (a t)")
                wait_pair(sp, vproj_d, pr, 2)
                sp.dma_start(stage_kv[:, p, :], src).then_inc(ld_kv[p], 16)
                if MASKED[ph]:
                    wait_pair(sp, neg_d, pr, 2)
                    sp.dma_start(stage_m[:, p, :], masks[ph][bass.ds(i, 1), :, :].rearrange("a p t -> p (a t)"))\
                        .then_inc(ld_m[p], 16)

            for group in range(3):
                run_slots(sp, group, slot)

            def store(t, first):
                sp.wait_ge(l3.y_d, t + 1)
                sp.dma_start(out_t[:, bass.ds(t * TILE, TILE)], x_t[:, bass.ds(t * TILE, TILE)]).then_inc(stored, 16)

            tiles(sp, store)
            sp.wait_ge(stored, 16 * NT)

        @block.gpsimd
        def _(pool):
            pool.memset(v_16[:, :, :, :, :], 0.0).then_inc(set_zero, 1)
            pool.memset(v_8[:, :, :, :, :], 0.0).then_inc(set_zero, 1)
            pool.memset(half_neg[:, :], -0.5).then_inc(set_zero, 1)
            pool.memset(gates_t[:, :], 0.0).then_inc(set_zero, 1)
            pool.memset(sel[:, :, :], 0.0).then_inc(set_zero, 1)
            pool.wait_ge(set_zero, 5)
            pool.wait_ge(loaded["small"], 48)
            pool.wait_ge(loaded["rows"], 16)

            def slot(at):
                pr = at(OFF_XT)
                if pr is not None and POST[pr.phase] != "none":
                    p = pr.p
                    wait_pair(pool, spread_d, pr)
                    wait_pair(pool, norm_d, pr, 2)
                    pool.tensor_tensor(rstd[:, p, :], spread[:, p, :], half_neg[:, 0:1], ALU.pow)\
                        .then_inc(rstd_d, 1)
                pr = at(OFF_PROJ)
                if pr is not None:
                    p, nj = pr.p, heads(pr) // 4
                    cj = C_J16 if nj == 4 else C_J8
                    wait_pair(pool, q_e, pr)
                    wait_pair(pool, score_d, pr, 2)
                    pool.tensor_tensor(q_by_g[:, p, :, :], q_t[:, p:p + 1, :].broadcast_to([128, 4, TOK]),
                                       maskg.unsqueeze(2).broadcast_to([128, 4, TOK]), ALU.mult).then_inc(qg_d, 1)
                    wait_pair(pool, k_e, pr)
                    pool.tensor_tensor(k_by_j[:, p, 0:nj, :], k_t[:, p:p + 1, :].broadcast_to([128, nj, TOK]),
                                       cst[:, cj:cj + nj].unsqueeze(2).broadcast_to([128, nj, TOK]), ALU.mult)\
                        .then_inc(kj_d, 1)
                pr = at(OFF_XT)
                if pr is not None and POST[pr.phase] == "ln":
                    p = pr.p
                    g, b = {0: (rows[:, ROW["g1"], :], row_bias[:, 1, :]),
                            1: (rows[:, ROW["g2"], :], rows[:, ROW["b2"], :]),
                            4: (rows[:, ROW["gL2"], :], rows[:, ROW["bL2"], :])}[pr.phase]
                    wait_pair(pool, norm_d, pr)
                    if not (isinstance(pr.n, int) and pr.n == 0):
                        pool.wait_ge(res_d, pr.n)
                    pool.tensor_tensor(scaled[:, p, :], normed[:, p, :], g, ALU.mult).then_inc(gsc_d, 1)
                    pool.wait_ge(gsc_d, pr.i + LN_BEFORE[pr.phase] + 1)
                    if pr.phase == 0:
                        pool.wait_ge(set_bias, 3)
                    pool.tensor_tensor(x_tok[:, pr.i, :], scaled[:, p, :], b, ALU.add).then_inc(res_d, 1)
                elif pr is not None and POST[pr.phase] == "rms":
                    wait_pair(pool, y_d, pr, 0, apart=True)
                    pool.tensor_copy(x_tok[:, pr.i, :], y[:, pr.p, :]).then_inc(res_d, 1)

            def ff_end(t, first):
                pool.wait_ge(f_sp, t + 1)
                pool.tensor_tensor(rs4[:, :], sp4[:, :], half_neg[:, :], ALU.pow).then_inc(f_rs, 1)
                pool.wait_ge(f_nn, SUB * (t + 1))
                pool.tensor_tensor(z4[:, :, :], n4[:, :, :],
                                   rows[:, ROW["g3"]:ROW["g3"] + 1, :].broadcast_to([128, SUB, D]), ALU.mult)\
                    .then_inc(f_gm, 1)
                pool.wait_ge(f_gm, t + 1)
                pool.tensor_tensor(x_tok[:, bass.ds(t * SUB, SUB), :], z4[:, :, :],
                                   rows[:, ROW["b3"]:ROW["b3"] + 1, :].broadcast_to([128, SUB, D]), ALU.add)\
                    .then_inc(f_x, 1)
                pool.tensor_tensor(w4[:, :, :], z4[:, :, :],
                                   rows[:, ROW["b3"]:ROW["b3"] + 1, :].broadcast_to([128, SUB, D]), ALU.add)\
                    .then_inc(ff.res_d, 1)
                pool.wait_ge(f_ms, SUB * (t + 1))
                pool.tensor_tensor(rs4b[:, :], sp4b[:, :], half_neg[:, :], ALU.pow).then_inc(f_rs2, 1)

            def mo_end(t, first):
                pool.wait_ge(mo.y_d, t + 1)
                pool.tensor_tensor(x_tok[:, bass.ds(t * SUB, SUB), :], y4[:, :, :],
                                   row_bias[:, 2:3, :].broadcast_to([128, SUB, D]), ALU.add).then_inc(mo.res_d, 1)

            run_slots(pool, 0, slot)
            tiles(pool, ff_end)
            run_slots(pool, 1, slot)
            tiles(pool, mo_end)
            run_slots(pool, 2, slot)

        @block.tensor
        def _(pe):
            pe.wait_ge(set_bv, 3)
            pe.wait_ge(loaded["wat"], 32)
            for ph, c in BIASED.items():
                mm = pe.matmul(ps[:, B_OUT, c * D:(c + 1) * D], bv_cols[:, c, :], wat[:, ph, 3, :], start=True, stop=True)
            mm.then_inc(set_mm, 1)
            pe.wait_ge(set_bias, 3)
            pe.wait_ge(set_id, 1)

            def slot(at):
                pr = at(OFF_SCORE)
                if pr is not None:
                    p, nj = pr.p, heads(pr) // 4
                    masked = MASKED[pr.phase]
                    hb = min(8, heads(pr))
                    if masked:
                        wait_pair(pe, neg_d, pr)
                    wait_pair(pe, pt1_e, pr, 2)
                    wait_pair(pe, qg_d, pr)
                    wait_pair(pe, kj_d, pr)
                    for bank in range(heads(pr) // hb):
                        if masked:
                            pe.matmul(ps[:, 2 * p + bank, :].rearrange("p (h k) -> p h k", k=S), idb[:, :],
                                      neg_m[:, p:p + 1, :].broadcast_to([128, hb, S]), start=True, stop=False,
                                      skip_group_check=True)
                        per = hb // nj
                        for k in range(per):
                            g = bank * per + k
                            for b in range(2):
                                mm = pe.matmul(
                                    ps[S * b:S * b + S, 2 * p + bank, k * nj * S:(k + 1) * nj * S]
                                    .rearrange("p (h k) -> p h k", k=S),
                                    q_by_g[:, p, g, S * b:S * b + S], k_by_j[:, p, 0:nj, S * b:S * b + S],
                                    start=not masked and k == 0, stop=True, skip_group_check=True)
                    mm.then_inc(score_d, 1)
                pr = at(OFF_PV)
                if pr is not None:
                    p, npr = pr.p, heads(pr) // 2
                    wait_pair(pe, exp_d, pr)
                    for half, done in enumerate((pt0_d, pt1_d)):
                        for k in range(npr // 2):
                            q = half * (npr // 2) + k
                            mm = pe.transpose(ps[:, 2 * p + half, k * 128:(k + 1) * 128],
                                              prob[:, p, q * 128:(q + 1) * 128], ident)
                        mm.then_inc(done, 1)
                    wait_pair(pe, inv_d, pr)
                    wait_pair(pe, heads_d, pr, 1)
                    pe.transpose(ps[:, B_HEADS, 128:256], inv[:, p, :], ident).then_inc(rt_d, 1)
                pr = at(OFF_V)
                if pr is not None:
                    ph, p, dk = pr.phase, pr.p, D // heads(pr)
                    wait_pair(pe, k_e, pr)
                    wait_pair(pe, v_e, pr, 1)
                    wv = wat[:, ph, 2, :].rearrange("c (h par d) -> c par h d", par=2, d=dk)
                    for b in range(2):
                        for par in range(2):
                            mm = pe.matmul(ps[S * par:S * par + S, B_PROJ, 256 + 64 * b:320 + 64 * b]
                                           .rearrange("p (h d) -> p h d", d=dk),
                                           stage_kv[:, p, S * b:S * b + S], wv[:, par], start=True, stop=True,
                                           skip_group_check=True)
                    mm.then_inc(vproj_d, 1)
                pr = at(OFF_PROJ)
                if pr is not None:
                    ph, p = pr.phase, pr.p
                    pe.wait_ge(ld_x[p], 16 * (pr.half + 1))
                    pe.wait_ge(ld_kv[p], 16 * (pr.half + 1))
                    pe.matmul(ps[:, B_PROJ, 0:128], wat[:, ph, 0, :], stage_x[:, p, :], start=True, stop=True)
                    pe.matmul(ps[:, B_PROJ, 128:256], wat[:, ph, 1, :], stage_kv[:, p, :], start=True, stop=True)\
                        .then_inc(proj_d, 1)
                pr = at(OFF_OUT)
                if pr is not None:
                    wait_pair(pe, heads_d, pr)
                    wait_pair(pe, y_d, pr, 1)
                    pe.matmul(ps[:, B_OUT, 0:D], heads_t[:, pr.p, :], wat[:, pr.phase, 3, :], start=True, stop=True)\
                        .then_inc(out_d, 1)
                pr = at(OFF_XT)
                if pr is not None:
                    wait_pair(pe, norm_d, pr)
                    wait_pair(pe, xt_e, pr, 1)
                    pe.transpose(ps[:, B_XT, 0:TOK], normed[:, pr.p, :], ident).then_inc(xt_d, 1)
                pr = at(OFF_PV)
                if pr is not None:
                    p, npr = pr.p, heads(pr) // 2
                    vb = v_16 if npr == 8 else v_8
                    wait_pair(pe, v_e, pr)
                    wait_pair(pe, rt_e, pr)
                    wait_pair(pe, pt0_e, pr)
                    wait_pair(pe, pt1_e, pr)
                    step = npr // 4
                    for b in range(2):
                        for k in range(step):
                            for g in range(4):
                                q = g * step + k
                                half, c = divmod(q, npr // 2)
                                mm = pe.matmul(ps[32 * g:32 * g + 32, B_HEADS, S * b:S * b + S],
                                               vb[:, p, b, q, :],
                                               prob_t[:, p, half, c * 128 + S * b:c * 128 + S * b + S],
                                               start=k == 0, stop=k == step - 1, skip_group_check=True)
                    mm.then_inc(pv_d, 1)

            def mlp(m):
                n, ring = m.n, m.ring

                def free(k, t):
                    if isinstance(t, int) and t == 0 and k < ring:
                        return
                    pe.wait_ge(m.act_d, n * t + (k - ring + 1))

                def turn(t):
                    pe.wait_ge(m.o_e, t + 1)
                    if not (isinstance(t, int) and t == 0):
                        pe.wait_ge(m.xt_e, t)
                    for s in range(SUB):
                        mm = pe.transpose(ps[:, B_TAIL, s * 128:(s + 1) * 128], mlp_o[:, s * 128:(s + 1) * 128], ident)
                    mm.then_inc(m.turn_d, 1)

                def back(t):
                    pe.wait_ge(m.n_d if m is ff else m.y_d, t + 1)
                    src = w4 if m is ff else y4
                    for s in range(SUB):
                        mm = pe.transpose(ps[:, B_TAIL, s * 128:(s + 1) * 128], src[:, s, :], ident)
                    mm.then_inc(m.back_d, 1)

                def tile(t, first):
                    x = x_t[:, bass.ds(t * TILE, TILE)]
                    if first:
                        for name, count in {"ff": [("ff", 32)], "mo": [("mo1", 16), ("mo2", 16)], "l3": [("l3", 32)]}[m.name]:
                            pe.wait_ge(loaded[name], count)
                    pe.wait_ge(xt_e, NP * m.phase + SUB * t + SUB)
                    lag = min(2, n)
                    for k in range(n + lag):
                        if k < n:
                            e, c = divmod(k, m.chunks)
                            free(k, t)
                            pe.matmul(ps[:, k % ring, :], m.w1[:, e, c * 128:(c + 1) * 128], x, start=True, stop=True)\
                                .then_inc(m.h_d, 1)
                            if m.gated and e == 1 and c == 0 and first:
                                pe.wait_ge(loaded["sel"], 16)
                            if m.gated and e >= 1 and c == 0:
                                if not (first and e <= 2):
                                    pe.wait_ge(m.gated_d, E * HC * t + HC * (e - 2))
                                pe.matmul(ps[:, B_GATE[e % 2], :], sel[:, e - 1, :], gates_t[:, bass.ds(t * TILE, TILE)],
                                          start=True, stop=True).then_inc(m.gate_d, 1)
                        if m is not l3 and not first and k == min(3, n - 1):
                            turn(t - 1)
                        if k >= lag:
                            q = k - lag
                            e, c = divmod(q, m.chunks)
                            if m.gated and e >= 1:
                                pe.wait_ge(m.gated_d, E * HC * t + (q - HC + 1))
                                rhs = gated_h[:, q % ring, :]
                            else:
                                pe.wait_ge(m.act_d, n * t + (q + 1))
                                rhs = hid[:, q % ring, :]
                            if q == 0 and not first:
                                pe.wait_ge(m.o_e, t)
                            pe.matmul(ps[:, B_ACC, :], m.w2[:, e, c, :], rhs, start=q == 0, stop=q == n - 1)\
                                .then_inc(m.acc_d, 1)
                        if m is not l3 and not first and k == min(14, n + lag - 1):
                            back(t - 1)

                tiles(pe, tile)
                if m is not l3:
                    turn(NT - 1)
                    back(NT - 1)

            def router():
                def tile(t, first):
                    pe.wait_ge(xt_e, NP * 3 + SUB * t + SUB)
                    if not first:
                        pe.wait_ge(r_te, t)
                    pe.matmul(ps[:, 0, :], gatew[:, :], x_t[:, bass.ds(t * TILE, TILE)], start=True, stop=True)\
                        .then_inc(r_lt, 1)
                    pe.wait_ge(r_le, t + 1)
                    for s in range(SUB):
                        mm = pe.transpose(ps[:, 1, s * 128:(s + 1) * 128], logit_t[:, s * 128:(s + 1) * 128], ident)
                    mm.then_inc(r_l, 1)
                    pe.wait_ge(r_g, t + 1)
                    for s in range(SUB):
                        mm = pe.transpose(ps[0:E, 2, s * 128:(s + 1) * 128], gates[:, s, :], ident)
                    mm.then_inc(r_t, 1)

                tiles(pe, tile)
                pe.wait_ge(r_te, NT)

            run_slots(pe, 0, slot)
            mlp(ff)
            run_slots(pe, 1, slot)
            router()
            mlp(mo)
            run_slots(pe, 2, slot)
            mlp(l3)

        @block.scalar
        def _(act):
            act.dma_start(ffw1[:, :, :], a["ffw1"]).then_inc(loaded["ff"], 16)
            act.dma_start(ffw2[:, :, :, :], a["ffw2"]).then_inc(loaded["ff"], 16)
            act.dma_start(mow1[:, :, :], a["mow1"]).then_inc(loaded["mo1"], 16)
            act.dma_start(mow2[:, :, :, :], a["mow2"]).then_inc(loaded["mo2"], 16)
            act.dma_start(l3w1[:, :, :], a["l3w1"]).then_inc(loaded["l3"], 16)
            act.dma_start(l3w2[:, :, :, :], a["l3w2"]).then_inc(loaded["l3"], 16)
            act.wait_ge(loaded["small"], 48)
            act.wait_ge(set_zero, 2)
            biases = {0: ("bq0", "bk0"), 1: ("bq1", "bk1"), 4: ("bq4", "bk4")}

            def slot(at):
                pr = at(OFF_PV)
                if pr is not None:
                    p = pr.p
                    w = 128 * (heads(pr) // 4)
                    wait_pair(act, pv_d, pr, 2)
                    wait_pair(act, pt0_d, pr)
                    act.activation(prob_t[:, p, 0, 0:w], ps[:, 2 * p, 0:w], ACT.Copy).then_inc(pt0_e, 1)
                    wait_pair(act, pt1_d, pr)
                    act.activation(prob_t[:, p, 1, 0:w], ps[:, 2 * p + 1, 0:w], ACT.Copy).then_inc(pt1_e, 1)
                    wait_pair(act, rt_d, pr)
                    wait_pair(act, heads_d, pr, 2)
                    act.activation(inv_t[:, p, :], ps[:, B_HEADS, 128:256], ACT.Copy).then_inc(rt_e, 1)
                pr = at(OFF_PROJ)
                if pr is not None:
                    p = pr.p
                    wait_pair(act, proj_d, pr)
                    wait_pair(act, qg_d, pr, 2)
                    wait_pair(act, kj_d, pr, 2)
                    for n, (dst, done) in enumerate(((q_t, q_e), (k_t, k_e))):
                        src = ps[:, B_PROJ, 128 * n:128 * n + 128]
                        if pr.phase in biases:
                            act.activation(dst[:, p, :], src, ACT.Identity, bias=v(biases[pr.phase][n])).then_inc(done, 1)
                        else:
                            act.activation(dst[:, p, :], src, ACT.Copy).then_inc(done, 1)
                pr = at(OFF_XT)
                if pr is not None:
                    ph = pr.phase
                    wait_pair(act, xt_d, pr)
                    dst, src = x_t[:, bass.ds(pr.i * TOK, TOK)], ps[:, B_XT, 0:TOK]
                    if POST[ph] == "ln":
                        g, b = {0: ("g1", "b1"), 1: ("g2", "b2"), 4: ("gL2", "bL2")}[ph]
                        act.activation(dst, src, ACT.Identity, bias=v(b), scale=v(g)).then_inc(xt_e, 1)
                    elif POST[ph] == "rms":
                        act.activation(dst, src, ACT.Copy, scale=v({2: "n2", 3: "n3"}[ph])).then_inc(xt_e, 1)
                    else:
                        act.activation(dst, src, ACT.Copy).then_inc(xt_e, 1)
                pr = at(OFF_SCORE)
                if pr is not None:
                    p, w = pr.p, heads(pr) * S
                    wait_pair(act, sub_d, pr)
                    act.activation(prob[:, p, 0:w], prob[:, p, 0:w], ACT.Exp,
                                   scale=float(D // heads(pr)) ** -0.5).then_inc(exp_d, 1)
                pr = at(OFF_V)
                if pr is not None:
                    p, dk = pr.p, D // heads(pr)
                    wait_pair(act, vproj_d, pr)
                    wait_pair(act, pv_d, pr, 2)
                    for par in range(2):
                        rows_p = slice(S * par, S * par + S)
                        src = ps[rows_p, B_PROJ, 256:384]
                        if dk == 8:
                            dst = v_16[rows_p, p, :, :, :].rearrange("r b (g k) c -> r (b g) (k c)", k=2)
                            dst = dst.rearrange("r bg (k c) -> r bg k c", k=2)
                            for k in range(2):
                                ins = act.activation(
                                    dst[:, :, k, 16 * k + 8 * par:16 * k + 8 * par + 8],
                                    src.rearrange("r (bg k d) -> r bg k d", k=2, d=8)[:, :, k, :], ACT.Copy)
                        else:
                            ins = act.activation(
                                v_8[rows_p, p, :, :, 16 * par:16 * par + 16].rearrange("r b q c -> r (b q) c"),
                                src.rearrange("r (bq d) -> r bq d", d=16), ACT.Copy)
                    ins.then_inc(v_e, 1)

            def mlp(m):
                n, ring = m.n, m.ring

                def tile(t, first):
                    for k in range(n):
                        act.wait_ge(m.h_d, n * t + (k + 1))
                        q = k - ring
                        if m.gated and (q >= HC or q < 0):
                            if not (first and q < 0):
                                act.wait_ge(m.gated_d, E * HC * t + ((q - HC + 1) if q >= 0 else (q + 1)))
                        elif not (first and q < 0):
                            act.wait_ge(m.acc_d, n * t + (q + 1))
                        kw = {}
                        if m.b1 is not None:
                            kw["bias"] = v(m.b1 if m is l3 else f"{m.b1}{k}")
                        act.activation(hid[:, k % ring, :], ps[:, k % ring, :], m.func, **kw).then_inc(m.act_d, 1)
                        if m is not l3 and not first and k == min(16, n - 1):
                            back(t - 1)
                    act.wait_ge(m.acc_d, n * t + n)
                    if m is not l3:
                        if not first:
                            act.wait_ge(m.turn_d, t)
                    elif not first:
                        act.wait_ge(m.y_d, t)
                    if m.b2 is not None:
                        act.activation(mlp_o[:, :], ps[:, B_ACC, :], ACT.Identity, bias=v(m.b2)).then_inc(m.o_e, 1)
                    else:
                        act.activation(mlp_o[:, :], ps[:, B_ACC, :], ACT.Copy).then_inc(m.o_e, 1)

                def back(t):
                    act.wait_ge(m.back_d, t + 1)
                    dst = x_t[:, bass.ds(t * TILE, TILE)]
                    if m is ff:
                        act.activation(dst, ps[:, B_TAIL, :], ACT.Copy, scale=v("n1")).then_inc(m.xt_e, 1)
                    else:
                        act.activation(dst, ps[:, B_TAIL, :], ACT.Copy).then_inc(m.xt_e, 1)

                tiles(act, tile)
                if m is not l3:
                    back(NT - 1)

            def router():
                def tile(t, first):
                    act.wait_ge(r_lt, t + 1)
                    if not first:
                        act.wait_ge(r_l, t)
                    act.activation(logit_t[:, :], ps[:, 0, :], ACT.Copy).then_inc(r_le, 1)
                    act.wait_ge(r_gap, t + 1)
                    act.activation(e_gap[:, :], gap[:, :], ACT.Exp).then_inc(r_exp, 1)
                    act.wait_ge(r_t, t + 1)
                    act.activation(gates_t[0:E, bass.ds(t * TILE, TILE)], ps[0:E, 2, :], ACT.Copy).then_inc(r_te, 1)

                tiles(act, tile)

            run_slots(act, 0, slot)
            mlp(ff)
            run_slots(act, 1, slot)
            router()
            mlp(mo)
            run_slots(act, 2, slot)
            mlp(l3)

        @block.vector
        def _(dve):
            dve.wait_ge(loaded["small"], 48)
            dve.tensor_scalar(idb[:, :], ident, NEG, None, ALU.mult).then_inc(set_id, 1)
            for ph, c in BIASED.items():
                dve.tensor_copy(bv_cols[:, c, :], v(f"bv{ph}").broadcast_to([128, TOK])).then_inc(set_bv, 1)
            dve.wait_ge(set_mm, 1)
            dve.wait_ge(loaded["rows"], 16)
            bo = rows[:, ROW["bo0"]:ROW["bo0"] + 3, :]
            dve.tensor_tensor(row_bias[:, :, :], ps[:, B_OUT, 0:3 * D].rearrange("p (c d) -> p c d", c=3), bo, ALU.add)\
                .then_inc(set_bias, 1)
            dve.wait_ge(set_bias, 1)
            dve.tensor_tensor(row_bias[:, 1, :], row_bias[:, 1, :], rows[:, ROW["b1"], :], ALU.add).then_inc(set_bias, 1)
            dve.wait_ge(loaded["x_tok"], 16)
            dve.tensor_tensor(x_tok[:, :, :], x_tok[:, :, :], row_bias[:, 0:1, :].broadcast_to([128, NP, D]), ALU.add)\
                .then_inc(set_bias, 1)
            dve.wait_ge(set_bias, 3)

            def slot(at):
                pr = at(OFF_OUT)
                if pr is not None:
                    p = pr.p
                    wait_pair(dve, pv_d, pr)
                    wait_pair(dve, out_d, pr, 2)
                    dve.tensor_tensor(heads_t[:, p, :], ps[:, B_HEADS, 0:TOK], inv_t[:, p, :], ALU.mult)\
                        .then_inc(heads_d, 1)
                pr = at(OFF_PV)
                if pr is not None:
                    p, nh = pr.p, heads(pr)
                    wait_pair(dve, exp_d, pr)
                    wait_pair(dve, inv_d, pr, 2)
                    dve.tensor_reduce(total[:, p, 0:nh], prob[:, p, 0:nh * S].rearrange("p (h k) -> p h k", k=S),
                                      AX.X, ALU.add).then_inc(sum_d, 1)
                    wait_pair(dve, sum_d, pr)
                    wait_pair(dve, rt_d, pr, 2)
                    dve.reciprocal(inv[:, p, :].rearrange("p (h d) -> p h d", h=nh),
                                   total[:, p, 0:nh].unsqueeze(2).broadcast_to([128, nh, D // nh])).then_inc(inv_d, 1)
                pr = at(OFF_XT)
                if pr is not None:
                    p, kind = pr.p, POST[pr.phase]
                    wait_pair(dve, xt_d, pr, 2)
                    if kind != "none":
                        wait_pair(dve, rstd_d, pr)
                    if kind != "none":
                        wait_pair(dve, res_d, pr, 2)
                    else:
                        dve.wait_ge(res_d, 5 * NP - 1 if isinstance(pr.i, int) else 5 * NP)
                    if kind == "ln":
                        dve.tensor_scalar(normed[:, p, :], y[:, p, :], moments[:, p, 0:1], rstd[:, p, :],
                                          ALU.subtract, ALU.mult).then_inc(norm_d, 1)
                    elif kind == "rms":
                        dve.tensor_scalar(normed[:, p, :], y[:, p, :], rstd[:, p, :], None, ALU.mult).then_inc(norm_d, 1)
                    else:
                        wait_pair(dve, y_d, pr)
                        dve.tensor_copy(normed[:, p, :], y[:, p, :]).then_inc(norm_d, 1)
                pr = at(OFF_PROJ)
                if pr is not None and MASKED[pr.phase]:
                    p = pr.p
                    dve.wait_ge(ld_m[p], 16 * (pr.half + 1))
                    wait_pair(dve, score_d, pr, 2)
                    dve.tensor_scalar(neg_m[:, p, :], stage_m[:, p, :], 0, None, ALU.is_equal).then_inc(neg_d, 1)
                pr = at(OFF_SCORE)
                if pr is not None:
                    p, nh = pr.p, heads(pr)
                    sc = ps[:, 2 * p:2 * p + nh // 8, :].rearrange("p b (h k) -> p (b h) k", k=S)
                    wait_pair(dve, score_d, pr)
                    wait_pair(dve, sub_d, pr, 2)
                    dve.tensor_reduce(top[:, p, 0:nh], sc, AX.X, ALU.max).then_inc(top_d, 1)
                    wait_pair(dve, top_d, pr)
                    wait_pair(dve, pt1_d, pr, 2)
                    wait_pair(dve, sum_d, pr, 2)
                    dve.tensor_tensor(prob[:, p, 0:nh * S].rearrange("p (h k) -> p h k", k=S), sc,
                                      top[:, p, 0:nh].unsqueeze(2).broadcast_to([128, nh, S]), ALU.subtract)\
                        .then_inc(sub_d, 1)
                pr = at(OFF_OUT)
                if pr is not None:
                    p, ph = pr.p, pr.phase
                    wait_pair(dve, out_d, pr)
                    wait_pair(dve, norm_d, pr, 2)
                    if ph > 0:
                        if ph % 2 == 1:
                            dve.wait_ge(res_d, RES_BEFORE[ph - 1] + 1 + pr.i)
                        else:
                            m = mlps[ph // 2 - 1]
                            dve.wait_ge(m.res_d, pr.i // SUB + 1 if isinstance(pr.i, int) else NT)
                    if not (isinstance(pr.n, int) and pr.n < 2) and POST[ph] != "none":
                        wait_pair(dve, res_d, pr, 2)
                    dve.tensor_tensor(y[:, p, :], ps[:, B_OUT, 0:D], x_tok[:, pr.i, :], ALU.add).then_inc(y_d, 1)
                    if POST[ph] == "ln":
                        wait_pair(dve, y_d, pr)
                        dve.bn_stats(stats[:, p, :], y[:, p, :]).then_inc(bns_d, 1)
                        wait_pair(dve, bns_d, pr, apart=True)
                        dve.bn_aggr(moments[:, p, :], stats[:, p, :]).then_inc(agg_d, 1)
                        wait_pair(dve, agg_d, pr)
                        dve.tensor_scalar(spread[:, p, :], moments[:, p, 1:2], EPS, None, ALU.add).then_inc(spread_d, 1)
                    elif POST[ph] == "rms":
                        wait_pair(dve, y_d, pr)
                        dve.tensor_tensor_reduce(squares[:, p, :], y[:, p, :], y[:, p, :], 1.0 / D, EPS,
                                                 ALU.mult, ALU.add, spread[:, p, :]).then_inc(spread_d, 1)

            def ff_end(t):
                dve.wait_ge(ff.turn_d, t + 1)
                dve.tensor_tensor(y4[:, :, :], ps[:, B_TAIL, :].rearrange("p (s d) -> p s d", s=SUB),
                                  x_tok[:, bass.ds(t * SUB, SUB), :], ALU.add).then_inc(ff.y_d, 1)
                dve.wait_ge(ff.y_d, t + 1)
                for s in range(SUB):
                    ins = dve.bn_stats(st4[:, s, :], y4[:, s, :])
                ins.then_inc(f_st, 1)
                wait_apart(dve, f_st, t + 1)
                for s in range(SUB):
                    ins = dve.bn_aggr(mo4[:, s, :], st4[:, s, :])
                ins.then_inc(f_ag, 1)
                dve.wait_ge(f_ag, t + 1)
                dve.tensor_scalar(sp4[:, :], mo4[:, :, 1], EPS, None, ALU.add).then_inc(f_sp, 1)
                dve.wait_ge(f_rs, t + 1)
                for s in range(SUB):
                    dve.tensor_scalar(n4[:, s, :], y4[:, s, :], mo4[:, s, 0:1], rs4[:, s:s + 1],
                                      ALU.subtract, ALU.mult).then_inc(f_nn, 1)
                dve.wait_ge(ff.res_d, t + 1)
                for s in range(SUB):
                    dve.tensor_tensor_reduce(z4[:, s, :], w4[:, s, :], w4[:, s, :], 1.0 / D, EPS,
                                             ALU.mult, ALU.add, sp4b[:, s:s + 1]).then_inc(f_ms, 1)
                dve.wait_ge(f_rs2, t + 1)
                for s in range(SUB):
                    ins = dve.tensor_scalar(w4[:, s, :], w4[:, s, :], rs4b[:, s:s + 1], None, ALU.mult)
                ins.then_inc(ff.n_d, 1)

            def mo_end(t):
                dve.wait_ge(mo.turn_d, t + 1)
                if not (isinstance(t, int) and t == 0):
                    dve.wait_ge(mo.res_d, t)
                dve.tensor_tensor(y4[:, :, :], ps[:, B_TAIL, :].rearrange("p (s d) -> p s d", s=SUB),
                                  x_tok[:, bass.ds(t * SUB, SUB), :], ALU.add).then_inc(mo.y_d, 1)

            def ff_tiles():
                with dve.Fori(0, NT) as t:
                    ff_end(t)

            def mo_tile(t, first):
                for q in range(E * HC):
                    e, c = divmod(q, HC)
                    k = q + HC
                    if c == 0:
                        dve.wait_ge(mo.gate_d, E * t + (e + 1))
                    dve.wait_ge(mo.act_d, mo.n * t + (k + 1))
                    if not (first and q < mo.ring):
                        dve.wait_ge(mo.acc_d, mo.n * t + ((k - mo.ring + 1) if q >= mo.ring else (q - mo.ring + 1)))
                    dve.tensor_tensor(gated_h[:, k % mo.ring, :], hid[:, k % mo.ring, :], ps[:, B_GATE[(e + 1) % 2], :],
                                      ALU.mult).then_inc(mo.gated_d, 1)
                    if q == 4 and not first:
                        mo_end(t - 1)

            def router_tile(t, first):
                dve.wait_ge(r_l, t + 1)
                dve.tensor_copy(logit[:, :, :], ps[:, 1, :].rearrange("p (s e) -> p s e", s=SUB)[:, :, 0:E]).then_inc(r_lc, 1)
                wait_apart(dve, r_lc, t + 1)
                for s in range(SUB):
                    ins = dve.max(best[:, s, :], logit[:, s, :])
                ins.then_inc(r_mx, 1)
                wait_apart(dve, r_mx, t + 1)
                for s in range(SUB):
                    ins = dve.max_index(best_at[:, s, :], best[:, s, :], logit[:, s, :])
                ins.then_inc(r_ix, 1)
                dve.tensor_tensor(gap[:, :], best[:, :, 1], best[:, :, 0], ALU.subtract).then_inc(r_gap, 1)
                dve.wait_ge(r_ix, t + 1)
                dve.tensor_copy(best_f[:, :, :], best_at[:, :, :]).then_inc(r_fx, 1)
                dve.wait_ge(r_fx, t + 1)
                for hot, k in ((hot1, 0), (hot2, 1)):
                    dve.tensor_tensor(hot[:, :, :], iota.rearrange("p (s e) -> p s e", s=1).broadcast_to([128, SUB, E]),
                                      best_f[:, :, k:k + 1].broadcast_to([128, SUB, E]), ALU.is_equal).then_inc(r_h, 1)
                dve.wait_ge(r_exp, t + 1)
                dve.tensor_scalar(den[:, :], e_gap[:, :], 1.0, None, ALU.add).then_inc(r_den, 1)
                dve.wait_ge(r_den, t + 1)
                dve.reciprocal(gate1[:, :], den[:, :]).then_inc(r_g1, 1)
                dve.wait_ge(r_g1, t + 1)
                dve.tensor_tensor(gate2[:, :], e_gap[:, :], gate1[:, :], ALU.mult).then_inc(r_g2, 1)
                dve.wait_ge(r_h, 2 * t + 2)
                dve.tensor_tensor(hot1[:, :, :], hot1[:, :, :], gate1[:, :].unsqueeze(2).broadcast_to([128, SUB, E]),
                                  ALU.mult).then_inc(r_a, 1)
                dve.wait_ge(r_g2, t + 1)
                dve.tensor_tensor(hot2[:, :, :], hot2[:, :, :], gate2[:, :].unsqueeze(2).broadcast_to([128, SUB, E]),
                                  ALU.mult).then_inc(r_a, 1)
                dve.wait_ge(r_a, 2 * t + 2)
                dve.tensor_tensor(gates[:, :, :], hot1[:, :, :], hot2[:, :, :], ALU.add).then_inc(r_g, 1)

            def l3_tile(t, first):
                dve.wait_ge(l3.o_e, t + 1)
                x = x_t[:, bass.ds(t * TILE, TILE)]
                dve.tensor_tensor(x, mlp_o[:, :], x, ALU.add).then_inc(l3.y_d, 1)

            run_slots(dve, 0, slot)
            ff_tiles()
            run_slots(dve, 1, slot)
            tiles(dve, router_tile)
            tiles(dve, mo_tile)
            mo_end(NT - 1)
            dve.sem_inc(bns_d, 2 * NP)
            dve.sem_inc(agg_d, 2 * NP)
            run_slots(dve, 2, slot)
            tiles(dve, l3_tile)


RES_BEFORE = [NP * sum(k != "none" for k in POST[:n]) for n in range(len(POST))]


def constants():
    r = np.arange(128)
    cst = np.zeros((128, C_END), np.float32)
    cst[:, C_ID:C_ID + 128] = np.eye(128)
    cst[:, C_G:C_G + 4] = r[:, None] // 32 == np.arange(4)
    cst[:, C_J16:C_J16 + 4] = r[:, None] % 32 // 8 == np.arange(4)
    cst[:, C_J8:C_J8 + 2] = r[:, None] % 32 // 16 == np.arange(2)
    cst[:, C_IOTA:C_IOTA + E] = np.arange(E)
    sel = np.zeros((E, E, 128), np.float32)
    sel[np.arange(E), np.arange(E)] = 1.0
    return cst, sel


def kernel(**inputs):
    import concourse.bacc as _bacc
    from concourse.bass_utils import run_bass_kernel_spmd as _run

    w = {k: np.asarray(x) for k, x in inputs.items()}
    L0, L1, L2, L3 = ({k[9:]: x for k, x in w.items() if k.startswith(f"L{n}_xattn_")} for n in range(4))
    cst, sel = constants()
    wat = np.stack([
        np.stack([L0["sa_wq"], L0["sa_wk"], L0["sa_wv"], L0["sa_wo"]]),
        np.stack([L0["ca_wq"], L0["ca_wk"], L0["ca_wv"], L0["ca_wo"]]),
        np.stack([L1[f"sa_w{k}"].T for k in "qkvo"]),
        np.stack([L1[f"ca_w{k}"].T for k in "qkvo"]),
        np.stack([L2[f"W{k}"].T for k in "qkvo"]),
        np.stack([L3[f"W_{k}"] for k in "qkvo"]),
    ])
    by_name = {
        "bq0": L0["sa_bq"], "bk0": L0["sa_bk"], "bv0": L0["sa_bv"], "bo0": L0["sa_bo"],
        "bq1": L0["ca_bq"], "bk1": L0["ca_bk"], "bv1": L0["ca_bv"], "bo1": L0["ca_bo"],
        "bq4": L2["bq"], "bk4": L2["bk"], "bv4": L2["bv"], "bo4": L2["bo"],
        "g1": L0["ln1_g"], "b1": L0["ln1_b"], "g2": L0["ln2_g"], "b2": L0["ln2_b"],
        "g3": L0["ln3_g"], "b3": L0["ln3_b"], "n1": L1["norm1_w"], "n2": L1["norm2_w"], "n3": L1["norm3_w"],
        "gL2": L2["ln_g"], "bL2": L2["ln_b"], "ffb2": L0["ff_b2"], "l3b1": L3["b1"], "l3b2": L3["b2"],
    }
    for c in range(HC):
        by_name[f"ffb1_{c}"] = L0["ff_b1"][128 * c:128 * c + 128]
    x = w["x"].reshape(NP, TOK, D)
    arrays = {
        "x_tok": x,
        "x_t": x.reshape(NP * TOK, D).T,
        "ctx_t": w["ctx_1024"].reshape(NP, TOK, D).transpose(0, 2, 1),
        "m0": w["mask_BxSxS2_ik0"].reshape(NP, TOK, S),
        "m1": w["mask_BxSxS2_if1"].reshape(NP, TOK, S),
        "m2": w["mask_BxSxS_ik0"].reshape(NP, TOK, S),
        "m4": w["mask_BxSxS2_ik1"].reshape(NP, TOK, S),
        "cst": cst,
        "sel": sel,
        "vec": np.stack([by_name[k] for k in VECS], axis=1),
        "rows": np.stack([by_name[k] for k in ROWS]),
        "wat": wat.transpose(2, 0, 1, 3),
        "ffw1": L0["ff_w1"][:, None, :],
        "ffw2": L0["ff_w2"].reshape(HC, 128, D).transpose(1, 0, 2)[:, None],
        "gatew": np.pad(L1["gate_w"].T, ((0, 0), (0, 128 - E))),
        "mow1": np.concatenate([L1["sh_w1"][None], L1["exp_w1"]]).transpose(2, 0, 1),
        "mow2": np.concatenate([L1["sh_w2"][None], L1["exp_w2"]]).reshape(1 + E, D, HC, 128).transpose(3, 0, 2, 1),
        "l3w1": L3["w1"].T[:, None, :],
        "l3w2": L3["w2"].T[:, None, None, :],
    }
    nc = _bacc.Bacc("TRN2", target_bir_lowering=False, num_devices=1)
    feed, aps = {}, {}
    for name, arr in arrays.items():
        arr = np.ascontiguousarray(arr)
        feed[f"in_{name}"] = arr
        aps[name] = nc.dram_tensor(f"in_{name}", arr.shape, mybir.dt.from_np(arr.dtype), kind="ExternalInput").ap()
    out_t = nc.dram_tensor("out_t", [D, NP * TOK], F32, kind="ExternalOutput").ap()
    build(nc, aps, out_t)
    r = _run(nc, [feed], core_ids=[0])
    return np.ascontiguousarray(r.results[0]["out_t"].T).reshape(B, S, D)
```

```python
from contextlib import ExitStack

import numpy as np

import concourse.bass as bass
from concourse import mybir

F32 = mybir.dt.float32
BF16 = mybir.dt.bfloat16
I32 = mybir.dt.int32
U32 = mybir.dt.uint32
ACT = mybir.ActivationFunctionType
ALU = mybir.AluOpType
AX = mybir.AxisListType

B, S, D = 32, 64, 128
TOK = 2 * S
NP = B // 2
E, HID = 8, 512
HC = HID // 128
TILE = 512
NT = B * S // TILE
SUB = TILE // 128
EPS = 1e-5
NEG = -1e20

HEADS = [16, 16, 16, 16, 16, 8]
SELF = [True, False, True, False, False, False]
MASKED = [True, True, True, True, True, False]
POST = ["ln", "ln", "rms", "rms", "ln", "none"]
LN_BEFORE = [0, NP, 2 * NP, 2 * NP, 2 * NP, 3 * NP]

VECS = ["bq0", "bk0", "bq1", "bk1", "bq4", "bk4", "bv0", "bv1", "bv4",
        "g1", "b1", "g2", "b2", "n1", "n2", "n3", "gL2", "bL2", "ffb2", "l3b1", "l3b2"] + \
       [f"ffb1_{c}" for c in range(HC)]
VCOL = {name: n for n, name in enumerate(VECS)}
ROWS = ["g1", "b1", "g2", "b2", "g3", "b3", "gL2", "bL2", "bo0", "bo1", "bo4"]
ROW = {name: n for n, name in enumerate(ROWS)}
BIASED = {0: 0, 1: 1, 4: 2}
C_ID, C_G, C_J16, C_J8, C_IOTA, C_END = 0, 128, 132, 136, 138, 146

OFF_PROJ, OFF_V, OFF_SCORE, OFF_PV, OFF_OUT, OFF_XT = 0, 1, 2, 3, 4, 5
OFF_F = 6
OFF_FY, OFF_FN, OFF_FB = 7, 8, 9
OFF_R1, OFF_R2, OFF_RT = 6, 7, 8
OFF_L3, OFF_ST = 7, 8
FF, RO, LAST = 1, 3, 5
STEADY = [6, 10, 10, 8, 6, 8]
LAST_OFF = OFF_FB


class Pair:

    def __init__(self, phase, i, half, parity):
        self.phase, self.i, self.p = phase, i, parity
        self.n = i + NP * phase
        self.half = half + NP // 2 * phase


def run_slots(eng, phases, slot, before=()):

    def fixed(s):
        def at(off):
            m = s - off
            if not 0 <= m < len(phases) * NP:
                return None
            i = m % NP
            return Pair(phases[m // NP], i, i // 2, i % 2)
        return at

    before = dict(before)
    for part, phase in enumerate(phases):
        for s in range(STEADY[phase]):
            if part * NP + s in before:
                before[part * NP + s]()
            slot(fixed(part * NP + s))
        with eng.Fori(STEADY[phase] // 2, NP // 2) as h:
            for u in range(2):
                def at(off, h=h, u=u):
                    return Pair(phase, 2 * h + (u - off), h + (u - off) // 2, (u - off) % 2)
                slot(at)
    for s in range(len(phases) * NP, len(phases) * NP + LAST_OFF):
        slot(fixed(s))


GROUPS = [[0, 1, 2, 3], [4, 5]]


def build(nc, a, out_t):
    ctx = ExitStack()
    with ctx:
        def sb(name, shape, dt=F32):
            return ctx.enter_context(nc.sbuf_tensor(name, shape, dt))

        def sem(name):
            return ctx.enter_context(nc.semaphore(name))

        cst = sb("cst", [128, C_END])
        sel = sb("sel", [128, E, 128])
        idb = sb("idb", [128, 128], BF16)
        vec = sb("vec", [128, len(VECS)])
        rows = sb("rows", [128, len(ROWS), D])
        wat = sb("wat", [128, 6, 4, D])
        ffw1, ffw2 = sb("ffw1", [128, 1, HID]), sb("ffw2", [128, 1, HC, D])
        mow1, mow2 = sb("mow1", [128, 1 + E, HID]), sb("mow2", [128, 1 + E, HC, D])
        l3w1, l3w2 = sb("l3w1", [128, 1, D]), sb("l3w2", [128, 1, 1, D])
        gatew = sb("gatew", [128, 128])
        ident, maskg = cst[:, C_ID:C_ID + 128], cst[:, C_G:C_G + 4]
        iota = cst[:, C_IOTA:C_IOTA + E]
        x_tok = sb("x_tok", [128, NP, D])
        x_t = sb("x_t", [128, NP * TOK])
        bv_cols = sb("bv_cols", [128, 3, TOK])
        row_bias = sb("row_bias", [128, 3, D])
        half_neg = sb("half_neg", [128, SUB])

        inv_h = sb("inv_h", [128, 2, 16])
        stage_x = sb("stage_x", [128, 2, TOK])
        stage_kv = sb("stage_kv", [128, 2, TOK])
        stage_m = sb("stage_m", [128, 2, S], I32)
        q_t, k_t = sb("q_t", [128, 2, TOK]), sb("k_t", [128, 2, TOK])
        q_by_g = sb("q_by_g", [128, 2, 4, TOK])
        k_by_j = sb("k_by_j", [128, 2, 4, TOK])
        v_16 = sb("v_16", [128, 2, 2, 8, 32])
        v_8 = sb("v_8", [128, 2, 2, 4, 32])
        neg_m = sb("neg_m", [128, 2, S], BF16)
        top = sb("top", [128, 2, 16])
        prob = sb("prob", [128, 2, 16 * S])
        prob_t = sb("prob_t", [128, 2, 2, 512])
        total = sb("total", [128, 2, 16])
        inv = sb("inv", [128, 2, D])
        inv_t = sb("inv_t", [128, 2, TOK])
        heads_t = sb("heads_t", [128, 2, TOK])
        y = sb("y", [128, 2, D])
        squares = sb("squares", [128, 2, D])
        squares_f = sb("squares_f", [128, 2, D])
        stats = sb("stats", [128, 2, 6])
        moments = sb("moments", [128, 2, 2])
        spread = sb("spread", [128, 2, 1])
        rstd = sb("rstd", [128, 2, 1])
        normed = sb("normed", [128, 2, D])
        scaled = sb("scaled", [128, 2, D])

        ring = 4
        hid = sb("hid", [128, ring, TILE])
        gated_h = sb("gated_h", [128, ring, TILE])
        mlp_o = sb("mlp_o", [128, TILE])
        y4 = sb("y4", [128, SUB, D])
        gates_t = sb("gates_t", [128, NP * TOK])

        hid_f = sb("hid_f", [128, 2, HC, TOK])
        sum_f = sb("sum_f", [128, 2, TOK])
        y_f = sb("y_f", [128, 2, D])
        stats_f = sb("stats_f", [128, 2, 6])
        mom_f = sb("mom_f", [128, 2, 2])
        spread_f, rstd_f = sb("spread_f", [128, 2, 1]), sb("rstd_f", [128, 2, 1])
        n_f, z_f, w_f = (sb(k, [128, 2, D]) for k in ("n_f", "z_f", "w_f"))
        meansq_f, rrms_f = sb("meansq_f", [128, 2, 1]), sb("rrms_f", [128, 2, 1])
        xn_f = sb("xn_f", [128, 2, D])

        hn_t = sb("hn_t", [128, 2, TOK])
        logit = sb("logit", [128, 2, E])
        best = sb("best", [128, 2, 8])
        best_at = sb("best_at", [128, 2, 8], U32)
        best_f = sb("best_f", [128, 2, 8])
        gap, e_gap, den, gate1, gate2 = (sb(k, [128, 2, 1]) for k in ("gap", "e_gap", "den", "gate1", "gate2"))
        hot1, hot2, gates = (sb(k, [128, 2, E]) for k in ("hot1", "hot2", "gates"))

        ps = ctx.enter_context(nc.psum_tensor("ps", [128, 8, 512], F32))
        B_PROJ, B_HEADS, B_OUT, B_F = 4, 5, 6, 7
        XT, FB, OUT, TURN = (slice(128 * n, 128 * n + 128) for n in range(4))
        B_ACC, B_TAIL, B_GATE = 5, 7, (4, 6)

        loaded = {k: sem(f"loaded_{k}") for k in ("small", "x_tok", "rows", "wat", "ff", "mo1", "mo2", "l3", "sel")}
        set_zero, set_id, set_bv, set_mm, set_bias = (
            sem(k) for k in ("set_zero", "set_id", "set_bv", "set_mm", "set_bias"))
        ld_x = [sem(f"ld_x{p}") for p in range(2)]
        ld_kv = [sem(f"ld_kv{p}") for p in range(2)]
        ld_m = [sem(f"ld_m{p}") for p in range(2)]
        proj_d, vproj_d, score_d, pt0_d, pt1_d, rt_d, pv_d, out_d, xt_d = (
            sem(k) for k in ("proj_d", "vproj_d", "score_d", "pt0_d", "pt1_d", "rt_d", "pv_d", "out_d", "xt_d"))
        q_e, k_e, v_e, exp_d, pt0_e, pt1_e, rt_e, xt_e = (
            sem(k) for k in ("q_e", "k_e", "v_e", "exp_d", "pt0_e", "pt1_e", "rt_e", "xt_e"))
        top_d, sub_d, sum_d, rcp_d, inv_d, heads_d, y_d, bns_d, agg_d, spread_d, norm_d = (
            sem(k) for k in ("top_d", "sub_d", "sum_d", "rcp_d", "inv_d", "heads_d", "y_d", "bns_d", "agg_d", "spread_d", "norm_d"))
        neg_d, qg_d, kj_d, rstd_d, gsc_d, res_d = (sem(k) for k in ("neg_d", "qg_d", "kj_d", "rstd_d", "gsc_d", "res_d"))

        f_h, f_r, f_acc, f_o, f_turn, f_y, f_st, f_ag, f_sp, f_rs, f_nn, f_z, f_w, f_x, f_ms, f_rr, f_xn, f_back, f_xt = (
            sem(f"f_{k}") for k in ("h", "r", "acc", "o", "turn", "y", "st", "ag", "sp", "rs", "nn", "z", "w", "x",
                                    "ms", "rr", "xn", "back", "xt"))
        l_h, l_r, l_acc, l_o, l_y = (sem(f"l_{k}") for k in ("h", "r", "acc", "o", "y"))
        r_x, r_l, r_lc, r_mx, r_ix, r_gap, r_exp, r_fx, r_den, r_g1, r_g2, r_h, r_a, r_g, r_t, r_te = (
            sem(f"r_{k}") for k in ("x", "l", "lc", "mx", "ix", "gap", "exp", "fx", "den", "g1", "g2", "h", "a", "g",
                                    "t", "te"))
        m_h, m_act, m_gated, m_acc, m_gate, m_o, m_turn, m_y, m_back, m_xt, m_res = (
            sem(f"m_{k}") for k in ("h", "act", "gated", "acc", "gate", "o", "turn", "y", "back", "xt", "res"))
        stored = sem("stored")

        def v(name):
            return vec[:, VCOL[name]:VCOL[name] + 1]

        def heads(pair):
            return HEADS[pair.phase]

        def tiles(eng, body):
            body(0, True)
            with eng.Fori(1, NT) as t:
                body(t, False)

        def wait_apart(eng, sem_, value):
            eng.wait_ge(loaded["small"], 48)
            eng.wait_ge(sem_, value)

        def wait_pair(eng, sem_, pair, back=0, apart=False):
            if isinstance(pair.n, int) and pair.n - back < 0:
                return
            (wait_apart if apart else lambda e, *x: e.wait_ge(*x))(eng, sem_, pair.n + (1 - back))

        def wait_own(eng, sem_, pr, back=0, apart=False):
            if isinstance(pr.i, int) and pr.i - back < 0:
                return
            (wait_apart if apart else lambda e, *x: e.wait_ge(*x))(eng, sem_, pr.i + (1 - back))

        def follows(at, off, phase):
            pr = at(off)
            return pr if pr is not None and pr.phase == phase else None

        block = ctx.enter_context(nc.Block())

        @block.sync
        def _(sp):
            sp.dma_start(wat[:, 0:1, :, :], a["wat"][:, 0:1, :, :]).then_inc(loaded["wat"], 16)
            sp.dma_start(vec[:, :], a["vec"]).then_inc(loaded["small"], 16)
            sp.dma_start(cst[:, :], a["cst"]).then_inc(loaded["small"], 16)
            sp.dma_start(gatew[:, :], a["gatew"]).then_inc(loaded["small"], 16)

            def load_next():
                sp.dma_start(wat[:, 1:6, :, :], a["wat"][:, 1:6, :, :]).then_inc(loaded["wat"], 16)
                sp.dma_start(rows[:, :, :], a["rows"].partition_broadcast(128)).then_inc(loaded["rows"], 16)
                sp.dma_start(x_tok[:, :, :], a["x_tok"].rearrange("i p d -> p i d")).then_inc(loaded["x_tok"], 16)

            def load_ff():
                sp.dma_start(ffw1[:, :, :], a["ffw1"]).then_inc(loaded["ff"], 16)
                sp.dma_start(ffw2[:, :, :, :], a["ffw2"]).then_inc(loaded["ff"], 16)

            def load_experts():
                sp.dma_start(mow1[:, :, :], a["mow1"]).then_inc(loaded["mo1"], 16)
                sp.dma_start(mow2[:, :, :, :], a["mow2"]).then_inc(loaded["mo2"], 16)
                sp.dma_start(l3w1[:, :, :], a["l3w1"]).then_inc(loaded["l3"], 16)
                sp.dma_start(l3w2[:, :, :, :], a["l3w2"]).then_inc(loaded["l3"], 16)
                sp.wait_ge(set_zero, 5)
                sp.dma_start(sel[0:E, :, :], a["sel"]).then_inc(loaded["sel"], 16)

            masks = [a["m0"], a["m1"], a["m2"], a["m1"], a["m4"], None]

            def load(pr):
                ph, i, p = pr.phase, pr.i, pr.p
                if ph == FF + 1:
                    sp.wait_ge(f_xt, i + 1 if isinstance(i, int) else NP)
                elif ph == RO + 1:
                    sp.wait_ge(m_xt, i // SUB + 1 if isinstance(i, int) else NT)
                wait_pair(sp, proj_d, pr, 2)
                if ph == 0:
                    tok = a["x_t"][bass.ds(i, 1), :, :].rearrange("a p t -> p (a t)")
                else:
                    tok = x_t[:, bass.ds(i * TOK, TOK)]
                sp.dma_start(stage_x[:, p, :], tok).then_inc(ld_x[p], 16)
                src = tok if SELF[ph] else a["ctx_t"][bass.ds(i, 1), :, :].rearrange("a p t -> p (a t)")
                wait_pair(sp, vproj_d, pr, 2)
                sp.dma_start(stage_kv[:, p, :], src).then_inc(ld_kv[p], 16)
                if MASKED[ph]:
                    wait_pair(sp, neg_d, pr, 2)
                    sp.dma_start(stage_m[:, p, :], masks[ph][bass.ds(i, 1), :, :].rearrange("a p t -> p (a t)"))\
                        .then_inc(ld_m[p], 16)

            def slot(at):
                pr = at(OFF_PROJ)
                if pr is not None:
                    load(pr)
                pr = follows(at, OFF_ST, LAST)
                if pr is not None:
                    wait_own(sp, l_y, pr)
                    cols = bass.ds(pr.i * TOK, TOK)
                    sp.dma_start(out_t[:, cols], x_t[:, cols]).then_inc(stored, 16)

            run_slots(sp, GROUPS[0], slot, {1: load_next, 5: load_ff, NP: load_experts})
            run_slots(sp, GROUPS[1], slot)
            sp.wait_ge(stored, 16 * NP)

        @block.gpsimd
        def _(pool):
            pool.memset(v_16[:, :, :, :, :], 0.0).then_inc(set_zero, 1)
            pool.memset(v_8[:, :, :, :, :], 0.0).then_inc(set_zero, 1)
            pool.memset(half_neg[:, :], -0.5).then_inc(set_zero, 1)
            pool.memset(gates_t[:, :], 0.0).then_inc(set_zero, 1)
            pool.memset(sel[:, :, :], 0.0).then_inc(set_zero, 1)
            pool.wait_ge(set_zero, 5)
            pool.wait_ge(loaded["small"], 48)

            def slot(at):
                pr = at(OFF_XT)
                if pr is not None and POST[pr.phase] != "none":
                    p = pr.p
                    wait_pair(pool, spread_d, pr)
                    wait_pair(pool, norm_d, pr, 2)
                    pool.tensor_tensor(rstd[:, p, :], spread[:, p, :], half_neg[:, 0:1], ALU.pow)\
                        .then_inc(rstd_d, 1)
                pr = follows(at, OFF_FN, FF)
                if pr is not None:
                    wait_own(pool, f_sp, pr)
                    wait_own(pool, f_nn, pr, 2)
                    pool.tensor_tensor(rstd_f[:, pr.p, :], spread_f[:, pr.p, :], half_neg[:, 0:1], ALU.pow)\
                        .then_inc(f_rs, 1)
                pr = follows(at, OFF_FB, FF)
                if pr is not None:
                    wait_own(pool, f_ms, pr)
                    wait_own(pool, f_xn, pr, 2)
                    pool.tensor_tensor(rrms_f[:, pr.p, :], meansq_f[:, pr.p, :], half_neg[:, 0:1], ALU.pow)\
                        .then_inc(f_rr, 1)
                pr = follows(at, OFF_FN, FF)
                if pr is not None:
                    p = pr.p
                    wait_own(pool, f_nn, pr)
                    wait_own(pool, f_x, pr, 2)
                    pool.tensor_tensor(z_f[:, p, :], n_f[:, p, :], rows[:, ROW["g3"], :], ALU.mult).then_inc(f_z, 1)
                    wait_own(pool, f_z, pr)
                    wait_own(pool, f_xn, pr, 2)
                    pool.tensor_tensor(w_f[:, p, :], z_f[:, p, :], rows[:, ROW["b3"], :], ALU.add).then_inc(f_w, 1)
                    pool.tensor_tensor(x_tok[:, pr.i, :], z_f[:, p, :], rows[:, ROW["b3"], :], ALU.add).then_inc(f_x, 1)
                pr = at(OFF_XT)
                if pr is not None and POST[pr.phase] == "ln":
                    p = pr.p
                    g, b = {0: (rows[:, ROW["g1"], :], row_bias[:, 1, :]),
                            1: (rows[:, ROW["g2"], :], rows[:, ROW["b2"], :]),
                            4: (rows[:, ROW["gL2"], :], rows[:, ROW["bL2"], :])}[pr.phase]
                    if isinstance(pr.n, int) and pr.n == 0:
                        pool.wait_ge(loaded["rows"], 16)
                        pool.wait_ge(set_bias, 3)
                    wait_pair(pool, norm_d, pr)
                    if not (isinstance(pr.n, int) and pr.n == 0):
                        pool.wait_ge(res_d, pr.n)
                    pool.tensor_tensor(scaled[:, p, :], normed[:, p, :], g, ALU.mult).then_inc(gsc_d, 1)
                    pool.wait_ge(gsc_d, pr.i + LN_BEFORE[pr.phase] + 1)
                    pool.tensor_tensor(x_tok[:, pr.i, :], scaled[:, p, :], b, ALU.add).then_inc(res_d, 1)
                elif pr is not None and POST[pr.phase] == "rms":
                    wait_pair(pool, y_d, pr, 0, apart=True)
                    pool.tensor_copy(x_tok[:, pr.i, :], y[:, pr.p, :]).then_inc(res_d, 1)
                pr = at(OFF_PROJ)
                if pr is not None:
                    p, nj = pr.p, heads(pr) // 4
                    cj = C_J16 if nj == 4 else C_J8
                    wait_pair(pool, q_e, pr)
                    wait_pair(pool, score_d, pr, 2)
                    pool.tensor_tensor(q_by_g[:, p, :, :], q_t[:, p:p + 1, :].broadcast_to([128, 4, TOK]),
                                       maskg.unsqueeze(2).broadcast_to([128, 4, TOK]), ALU.mult).then_inc(qg_d, 1)
                    wait_pair(pool, k_e, pr)
                    pool.tensor_tensor(k_by_j[:, p, 0:nj, :], k_t[:, p:p + 1, :].broadcast_to([128, nj, TOK]),
                                       cst[:, cj:cj + nj].unsqueeze(2).broadcast_to([128, nj, TOK]), ALU.mult)\
                        .then_inc(kj_d, 1)

            def experts_end(t, first):
                pool.wait_ge(m_y, t + 1)
                pool.tensor_tensor(x_tok[:, bass.ds(t * SUB, SUB), :], y4[:, :, :],
                                   row_bias[:, 2:3, :].broadcast_to([128, SUB, D]), ALU.add).then_inc(m_res, 1)

            run_slots(pool, GROUPS[0], slot)
            tiles(pool, experts_end)
            run_slots(pool, GROUPS[1], slot)

        @block.tensor
        def _(pe):
            def bias_rows():
                pe.wait_ge(set_bv, 3)
                pe.wait_ge(loaded["wat"], 32)
                for ph, c in BIASED.items():
                    mm = pe.matmul(ps[:, B_OUT, c * D:(c + 1) * D], bv_cols[:, c, :], wat[:, ph, 3, :],
                                   start=True, stop=True)
                mm.then_inc(set_mm, 1)

            def bias_out():
                pe.wait_ge(set_bias, 1)

            pe.wait_ge(loaded["wat"], 16)
            pe.wait_ge(set_id, 1)

            def slot(at):
                pr = at(OFF_SCORE)
                if pr is not None:
                    p, nj = pr.p, heads(pr) // 4
                    masked = MASKED[pr.phase]
                    hb = min(8, heads(pr))
                    if masked:
                        wait_pair(pe, neg_d, pr)
                    wait_pair(pe, pt1_e, pr, 2)
                    wait_pair(pe, qg_d, pr)
                    wait_pair(pe, kj_d, pr)
                    for bank in range(heads(pr) // hb):
                        if masked:
                            pe.matmul(ps[:, 2 * p + bank, :].rearrange("p (h k) -> p h k", k=S), idb[:, :],
                                      neg_m[:, p:p + 1, :].broadcast_to([128, hb, S]), start=True, stop=False,
                                      skip_group_check=True)
                        per = hb // nj
                        for k in range(per):
                            g = bank * per + k
                            for b in range(2):
                                mm = pe.matmul(
                                    ps[S * b:S * b + S, 2 * p + bank, k * nj * S:(k + 1) * nj * S]
                                    .rearrange("p (h k) -> p h k", k=S),
                                    q_by_g[:, p, g, S * b:S * b + S], k_by_j[:, p, 0:nj, S * b:S * b + S],
                                    start=not masked and k == 0, stop=True, skip_group_check=True)
                    mm.then_inc(score_d, 1)
                pr = at(OFF_XT)
                if pr is not None:
                    wait_pair(pe, norm_d, pr)
                    if pr.phase == FF or pr.phase == FF + 1:
                        done = follows(at, OFF_FN, FF)
                        if done is not None:
                            wait_own(pe, f_y, done)
                    done = follows(at, OFF_FB, FF)
                    if done is not None:
                        wait_own(pe, f_xn, done)
                        pe.transpose(ps[:, B_OUT, FB], xn_f[:, done.p, :], ident).then_inc(f_back, 1)
                    pe.transpose(ps[:, B_OUT, XT], normed[:, pr.p, :], ident).then_inc(xt_d, 1)
                pr = follows(at, OFF_RT, RO)
                if pr is not None:
                    wait_own(pe, r_te, pr, 1)
                    wait_own(pe, r_g, pr)
                    if not (isinstance(pr.i, int) and pr.i == NP - 1):
                        wait_own(pe, r_lc, pr, -1)
                    pe.transpose(ps[0:E, B_F, 0:TOK], gates[:, pr.p, :], ident).then_inc(r_t, 1)
                pr = at(OFF_PV)
                if pr is not None:
                    p, npr = pr.p, heads(pr) // 2
                    wait_pair(pe, exp_d, pr)
                    for half, done in enumerate((pt0_d, pt1_d)):
                        for k in range(npr // 2):
                            q = half * (npr // 2) + k
                            mm = pe.transpose(ps[:, 2 * p + half, k * 128:(k + 1) * 128],
                                              prob[:, p, q * 128:(q + 1) * 128], ident)
                        mm.then_inc(done, 1)
                    wait_pair(pe, inv_d, pr)
                    wait_pair(pe, heads_d, pr, 1)
                    pe.transpose(ps[:, B_HEADS, 128:256], inv[:, p, :], ident).then_inc(rt_d, 1)
                pr = at(OFF_V)
                if pr is not None:
                    ph, p, dk = pr.phase, pr.p, D // heads(pr)
                    wait_pair(pe, k_e, pr)
                    wait_pair(pe, v_e, pr, 1)
                    wv = wat[:, ph, 2, :].rearrange("c (h par d) -> c par h d", par=2, d=dk)
                    for b in range(2):
                        for par in range(2):
                            mm = pe.matmul(ps[S * par:S * par + S, B_PROJ, 256 + 64 * b:320 + 64 * b]
                                           .rearrange("p (h d) -> p h d", d=dk),
                                           stage_kv[:, p, S * b:S * b + S], wv[:, par], start=True, stop=True,
                                           skip_group_check=True)
                    mm.then_inc(vproj_d, 1)
                pr = at(OFF_PROJ)
                if pr is not None:
                    ph, p = pr.phase, pr.p
                    pe.wait_ge(ld_x[p], 16 * (pr.half + 1))
                    pe.wait_ge(ld_kv[p], 16 * (pr.half + 1))
                    pe.matmul(ps[:, B_PROJ, 0:128], wat[:, ph, 0, :], stage_x[:, p, :], start=True, stop=True)
                    pe.matmul(ps[:, B_PROJ, 128:256], wat[:, ph, 1, :], stage_kv[:, p, :], start=True, stop=True)\
                        .then_inc(proj_d, 1)
                pr = follows(at, OFF_F, FF)
                if pr is not None:
                    x = x_t[:, bass.ds(pr.i * TOK, TOK)]
                    if isinstance(pr.i, int) and pr.i == 0:
                        pe.wait_ge(loaded["ff"], 32)
                    wait_own(pe, f_o, pr, 1)
                    wait_pair(pe, xt_e, pr)
                    for c in range(HC):
                        mm = pe.matmul(ps[:, B_F, c * 128:(c + 1) * 128], ffw1[:, 0, c * 128:(c + 1) * 128], x,
                                       start=True, stop=True)
                    mm.then_inc(f_h, 1)
                pr = follows(at, OFF_R1, RO)
                if pr is not None:
                    wait_own(pe, r_te, pr, 2)
                    wait_own(pe, r_lc, pr, 1)
                    wait_own(pe, r_x, pr)
                    pe.matmul(ps[:, B_F, 128:128 + E], hn_t[:, pr.p, :], gatew[:, 0:E], start=True, stop=True)\
                        .then_inc(r_l, 1)
                pr = follows(at, OFF_F, LAST)
                if pr is not None:
                    if isinstance(pr.i, int) and pr.i == 0:
                        pe.wait_ge(loaded["l3"], 32)
                    wait_own(pe, l_o, pr, 1)
                    wait_pair(pe, xt_e, pr)
                    pe.matmul(ps[:, B_F, 0:TOK], l3w1[:, 0, :], x_t[:, bass.ds(pr.i * TOK, TOK)], start=True, stop=True)\
                        .then_inc(l_h, 1)
                pr = at(OFF_OUT)
                if pr is not None:
                    wait_pair(pe, heads_d, pr)
                    before = at(OFF_XT)
                    if before is not None:
                        wait_pair(pe, xt_e, before)
                        before = follows(at, OFF_FB, FF)
                        if before is not None:
                            wait_own(pe, f_xt, before)
                    done = follows(at, OFF_FY, FF)
                    if done is not None:
                        wait_own(pe, f_o, done)
                        pe.transpose(ps[:, B_OUT, TURN], sum_f[:, done.p, :], ident).then_inc(f_turn, 1)
                    pe.matmul(ps[:, B_OUT, OUT], heads_t[:, pr.p, :], wat[:, pr.phase, 3, :], start=True, stop=True)\
                        .then_inc(out_d, 1)
                pr = at(OFF_PV)
                if pr is not None:
                    p, npr = pr.p, heads(pr) // 2
                    vb = v_16 if npr == 8 else v_8
                    wait_pair(pe, v_e, pr)
                    wait_pair(pe, rt_e, pr)
                    wait_pair(pe, pt0_e, pr)
                    wait_pair(pe, pt1_e, pr)
                    step = npr // 4
                    for b in range(2):
                        for k in range(step):
                            for g in range(4):
                                q = g * step + k
                                half, c = divmod(q, npr // 2)
                                mm = pe.matmul(ps[32 * g:32 * g + 32, B_HEADS, S * b:S * b + S],
                                               vb[:, p, b, q, :],
                                               prob_t[:, p, half, c * 128 + S * b:c * 128 + S * b + S],
                                               start=k == 0, stop=k == step - 1, skip_group_check=True)
                    mm.then_inc(pv_d, 1)
                pr = follows(at, OFF_F, FF)
                if pr is not None:
                    wait_own(pe, f_r, pr)
                    for c in range(HC):
                        mm = pe.matmul(ps[:, B_F, 0:TOK], ffw2[:, 0, c, :], hid_f[:, pr.p, c, :], start=c == 0, stop=c == HC - 1)
                    mm.then_inc(f_acc, 1)
                pr = follows(at, OFF_F, LAST)
                if pr is not None:
                    wait_own(pe, l_r, pr)
                    pe.matmul(ps[:, B_F, 128:128 + TOK], l3w2[:, 0, 0, :], hid_f[:, pr.p, 0, :], start=True, stop=True)\
                        .then_inc(l_acc, 1)

            chunks = (1 + E) * HC

            def turn(t):
                pe.wait_ge(m_o, t + 1)
                if not (isinstance(t, int) and t == 0):
                    pe.wait_ge(m_xt, t)
                for s in range(SUB):
                    mm = pe.transpose(ps[:, B_TAIL, s * 128:(s + 1) * 128], mlp_o[:, s * 128:(s + 1) * 128], ident)
                mm.then_inc(m_turn, 1)

            def back(t):
                pe.wait_ge(m_y, t + 1)
                for s in range(SUB):
                    mm = pe.transpose(ps[:, B_TAIL, s * 128:(s + 1) * 128], y4[:, s, :], ident)
                mm.then_inc(m_back, 1)

            def experts(t, first):
                x = x_t[:, bass.ds(t * TILE, TILE)]
                if first:
                    pe.wait_ge(loaded["mo1"], 16)
                    pe.wait_ge(loaded["mo2"], 16)
                    pe.wait_ge(loaded["sel"], 16)
                    pe.wait_ge(xt_e, NP * (RO + 1))
                    pe.wait_ge(r_te, NP)
                lag = 2
                for k in range(chunks + lag):
                    if k < chunks:
                        e, c = divmod(k, HC)
                        if not (first and k < ring):
                            pe.wait_ge(m_act, chunks * t + (k - ring + 1))
                        pe.matmul(ps[:, k % ring, :], mow1[:, e, c * 128:(c + 1) * 128], x, start=True, stop=True)\
                            .then_inc(m_h, 1)
                        if e >= 1 and c == 0:
                            if not (first and e <= 2):
                                pe.wait_ge(m_gated, E * HC * t + HC * (e - 2))
                            pe.matmul(ps[:, B_GATE[e % 2], :], sel[:, e - 1, :], gates_t[:, bass.ds(t * TILE, TILE)],
                                      start=True, stop=True).then_inc(m_gate, 1)
                    if not first and k == 3:
                        turn(t - 1)
                    if k >= lag:
                        q = k - lag
                        e, c = divmod(q, HC)
                        if e >= 1:
                            pe.wait_ge(m_gated, E * HC * t + (q - HC + 1))
                            rhs = gated_h[:, q % ring, :]
                        else:
                            pe.wait_ge(m_act, chunks * t + (q + 1))
                            rhs = hid[:, q % ring, :]
                        if q == 0 and not first:
                            pe.wait_ge(m_o, t)
                        pe.matmul(ps[:, B_ACC, :], mow2[:, e, c, :], rhs, start=q == 0, stop=q == chunks - 1)\
                            .then_inc(m_acc, 1)
                    if not first and k == 14:
                        back(t - 1)

            run_slots(pe, GROUPS[0], slot, {3: bias_rows, 4: bias_out})
            tiles(pe, experts)
            turn(NT - 1)
            back(NT - 1)
            run_slots(pe, GROUPS[1], slot)

        @block.scalar
        def _(act):
            act.wait_ge(loaded["small"], 48)
            act.wait_ge(set_zero, 2)
            biases = {0: ("bq0", "bk0"), 1: ("bq1", "bk1"), 4: ("bq4", "bk4")}

            def slot(at):
                pr = at(OFF_XT)
                if pr is not None:
                    ph = pr.phase
                    wait_pair(act, xt_d, pr)
                    dst, src = x_t[:, bass.ds(pr.i * TOK, TOK)], ps[:, B_OUT, XT]
                    if ph == RO:
                        wait_own(act, r_l, pr, 2)
                        act.activation(hn_t[:, pr.p, :], src, ACT.Copy, scale=v("n3")).then_inc(r_x, 1)
                    if POST[ph] == "ln":
                        g, b = {0: ("g1", "b1"), 1: ("g2", "b2"), 4: ("gL2", "bL2")}[ph]
                        act.activation(dst, src, ACT.Identity, bias=v(b), scale=v(g)).then_inc(xt_e, 1)
                    elif POST[ph] == "rms":
                        act.activation(dst, src, ACT.Copy, scale=v({2: "n2", 3: "n3"}[ph])).then_inc(xt_e, 1)
                    else:
                        act.activation(dst, src, ACT.Copy).then_inc(xt_e, 1)
                pr = follows(at, OFF_FB, FF)
                if pr is not None:
                    wait_own(act, f_back, pr)
                    act.activation(x_t[:, bass.ds(pr.i * TOK, TOK)], ps[:, B_OUT, FB], ACT.Copy, scale=v("n1"))\
                        .then_inc(f_xt, 1)
                pr = follows(at, OFF_RT, RO)
                if pr is not None:
                    wait_own(act, r_t, pr)
                    act.activation(gates_t[0:E, bass.ds(pr.i * TOK, TOK)], ps[0:E, B_F, 0:TOK], ACT.Copy).then_inc(r_te, 1)
                pr = at(OFF_PV)
                if pr is not None:
                    p = pr.p
                    w = 128 * (heads(pr) // 4)
                    wait_pair(act, pv_d, pr, 2)
                    wait_pair(act, pt0_d, pr)
                    act.activation(prob_t[:, p, 0, 0:w], ps[:, 2 * p, 0:w], ACT.Copy).then_inc(pt0_e, 1)
                    wait_pair(act, pt1_d, pr)
                    act.activation(prob_t[:, p, 1, 0:w], ps[:, 2 * p + 1, 0:w], ACT.Copy).then_inc(pt1_e, 1)
                    wait_pair(act, rt_d, pr)
                    wait_pair(act, heads_d, pr, 2)
                    act.activation(inv_t[:, p, :], ps[:, B_HEADS, 128:256], ACT.Copy).then_inc(rt_e, 1)
                pr = at(OFF_PROJ)
                if pr is not None:
                    p = pr.p
                    wait_pair(act, proj_d, pr)
                    wait_pair(act, qg_d, pr, 2)
                    wait_pair(act, kj_d, pr, 2)
                    for n, (dst, done) in enumerate(((q_t, q_e), (k_t, k_e))):
                        src = ps[:, B_PROJ, 128 * n:128 * n + 128]
                        if pr.phase in biases:
                            act.activation(dst[:, p, :], src, ACT.Identity, bias=v(biases[pr.phase][n])).then_inc(done, 1)
                        else:
                            act.activation(dst[:, p, :], src, ACT.Copy).then_inc(done, 1)
                pr = follows(at, OFF_F, FF)
                if pr is not None:
                    wait_own(act, f_h, pr)
                    wait_own(act, f_acc, pr, 2)
                    for c in range(HC):
                        ins = act.activation(hid_f[:, pr.p, c, :], ps[:, B_F, c * 128:(c + 1) * 128], ACT.Relu,
                                             bias=v(f"ffb1_{c}"))
                    ins.then_inc(f_r, 1)
                pr = follows(at, OFF_F, LAST)
                if pr is not None:
                    wait_own(act, l_h, pr)
                    wait_own(act, l_acc, pr, 2)
                    act.activation(hid_f[:, pr.p, 0, :], ps[:, B_F, 0:TOK], ACT.Relu, bias=v("l3b1")).then_inc(l_r, 1)
                pr = at(OFF_SCORE)
                if pr is not None:
                    p, w = pr.p, heads(pr) * S
                    wait_pair(act, sub_d, pr)
                    act.activation(prob[:, p, 0:w], prob[:, p, 0:w], ACT.Exp,
                                   scale=float(D // heads(pr)) ** -0.5).then_inc(exp_d, 1)
                pr = at(OFF_V)
                if pr is not None:
                    p, dk = pr.p, D // heads(pr)
                    wait_pair(act, vproj_d, pr)
                    wait_pair(act, pv_d, pr, 2)
                    for par in range(2):
                        rows_p = slice(S * par, S * par + S)
                        src = ps[rows_p, B_PROJ, 256:384]
                        if dk == 8:
                            dst = v_16[rows_p, p, :, :, :].rearrange("r b (g k) c -> r (b g) (k c)", k=2)
                            dst = dst.rearrange("r bg (k c) -> r bg k c", k=2)
                            for k in range(2):
                                ins = act.activation(
                                    dst[:, :, k, 16 * k + 8 * par:16 * k + 8 * par + 8],
                                    src.rearrange("r (bg k d) -> r bg k d", k=2, d=8)[:, :, k, :], ACT.Copy)
                        else:
                            ins = act.activation(
                                v_8[rows_p, p, :, :, 16 * par:16 * par + 16].rearrange("r b q c -> r (b q) c"),
                                src.rearrange("r (bq d) -> r bq d", d=16), ACT.Copy)
                    ins.then_inc(v_e, 1)
                pr = follows(at, OFF_F, FF)
                if pr is not None:
                    wait_own(act, f_acc, pr)
                    wait_own(act, f_turn, pr, 2)
                    act.activation(sum_f[:, pr.p, :], ps[:, B_F, 0:TOK], ACT.Identity, bias=v("ffb2")).then_inc(f_o, 1)
                pr = follows(at, OFF_F, LAST)
                if pr is not None:
                    wait_own(act, l_acc, pr)
                    wait_own(act, l_y, pr, 2)
                    act.activation(sum_f[:, pr.p, :], ps[:, B_F, 128:128 + TOK], ACT.Identity, bias=v("l3b2"))\
                        .then_inc(l_o, 1)
                pr = follows(at, OFF_R1, RO)
                if pr is not None:
                    wait_own(act, r_gap, pr)
                    wait_own(act, r_g2, pr, 2)
                    act.activation(e_gap[:, pr.p, :], gap[:, pr.p, :], ACT.Exp).then_inc(r_exp, 1)

            chunks = (1 + E) * HC

            def back(t):
                act.wait_ge(m_back, t + 1)
                act.activation(x_t[:, bass.ds(t * TILE, TILE)], ps[:, B_TAIL, :], ACT.Copy).then_inc(m_xt, 1)

            def experts(t, first):
                for k in range(chunks):
                    act.wait_ge(m_h, chunks * t + (k + 1))
                    q = k - ring
                    if q >= HC or q < 0:
                        if not (first and q < 0):
                            act.wait_ge(m_gated, E * HC * t + ((q - HC + 1) if q >= 0 else (q + 1)))
                    else:
                        act.wait_ge(m_acc, chunks * t + (q + 1))
                    act.activation(hid[:, k % ring, :], ps[:, k % ring, :], ACT.Silu).then_inc(m_act, 1)
                    if not first and k == 16:
                        back(t - 1)
                act.wait_ge(m_acc, chunks * t + chunks)
                if not first:
                    act.wait_ge(m_turn, t)
                act.activation(mlp_o[:, :], ps[:, B_ACC, :], ACT.Copy).then_inc(m_o, 1)

            run_slots(act, GROUPS[0], slot)
            tiles(act, experts)
            back(NT - 1)
            run_slots(act, GROUPS[1], slot)

        @block.vector
        def _(dve):
            dve.wait_ge(loaded["small"], 48)
            dve.tensor_scalar(idb[:, :], ident, NEG, None, ALU.mult).then_inc(set_id, 1)
            for ph, c in BIASED.items():
                dve.tensor_copy(bv_cols[:, c, :], v(f"bv{ph}").broadcast_to([128, TOK])).then_inc(set_bv, 1)

            def residuals():
                dve.wait_ge(set_mm, 1)
                dve.wait_ge(loaded["rows"], 16)
                bo = rows[:, ROW["bo0"]:ROW["bo0"] + 3, :]
                dve.tensor_tensor(row_bias[:, :, :], ps[:, B_OUT, 0:3 * D].rearrange("p (c d) -> p c d", c=3), bo, ALU.add)\
                    .then_inc(set_bias, 1)
                dve.wait_ge(set_bias, 1)
                dve.tensor_tensor(row_bias[:, 1, :], row_bias[:, 1, :], rows[:, ROW["b1"], :], ALU.add).then_inc(set_bias, 1)
                dve.wait_ge(loaded["x_tok"], 16)
                dve.tensor_tensor(x_tok[:, :, :], x_tok[:, :, :], row_bias[:, 0:1, :].broadcast_to([128, NP, D]), ALU.add)\
                    .then_inc(set_bias, 1)
                dve.wait_ge(set_bias, 3)

            def slot(at):
                pr = at(OFF_OUT)
                if pr is not None:
                    p = pr.p
                    wait_pair(dve, pv_d, pr)
                    wait_pair(dve, out_d, pr, 2)
                    dve.tensor_tensor(heads_t[:, p, :], ps[:, B_HEADS, 0:TOK], inv_t[:, p, :], ALU.mult)\
                        .then_inc(heads_d, 1)
                pr = at(OFF_XT)
                if pr is not None:
                    p, kind = pr.p, POST[pr.phase]
                    wait_pair(dve, xt_d, pr, 2)
                    if kind != "none":
                        wait_pair(dve, rstd_d, pr)
                    if kind != "none":
                        wait_pair(dve, res_d, pr, 2)
                    else:
                        dve.wait_ge(res_d, LAST * NP - 1 if isinstance(pr.i, int) and pr.i == 0 else LAST * NP)
                    if kind == "ln":
                        dve.tensor_scalar(normed[:, p, :], y[:, p, :], moments[:, p, 0:1], rstd[:, p, :],
                                          ALU.subtract, ALU.mult).then_inc(norm_d, 1)
                    elif kind == "rms":
                        dve.tensor_scalar(normed[:, p, :], y[:, p, :], rstd[:, p, :], None, ALU.mult).then_inc(norm_d, 1)
                    else:
                        wait_pair(dve, y_d, pr)
                        dve.tensor_copy(normed[:, p, :], y[:, p, :]).then_inc(norm_d, 1)
                pr = follows(at, OFF_FN, FF)
                if pr is not None:
                    p = pr.p
                    wait_own(dve, f_rs, pr)
                    wait_own(dve, f_z, pr, 2)
                    dve.tensor_scalar(n_f[:, p, :], y_f[:, p, :], mom_f[:, p, 0:1], rstd_f[:, p, :],
                                      ALU.subtract, ALU.mult).then_inc(f_nn, 1)
                pr = follows(at, OFF_FB, FF)
                if pr is not None:
                    p = pr.p
                    wait_own(dve, f_rr, pr)
                    wait_own(dve, f_back, pr, 2)
                    dve.tensor_scalar(xn_f[:, p, :], w_f[:, p, :], rrms_f[:, p, :], None, ALU.mult).then_inc(f_xn, 1)
                pr = at(OFF_PV)
                if pr is not None:
                    p, nh = pr.p, heads(pr)
                    wait_pair(dve, exp_d, pr)
                    wait_pair(dve, inv_d, pr, 2)
                    dve.tensor_reduce(total[:, p, 0:nh], prob[:, p, 0:nh * S].rearrange("p (h k) -> p h k", k=S),
                                      AX.X, ALU.add).then_inc(sum_d, 1)
                    wait_pair(dve, sum_d, pr)
                    dve.reciprocal(inv_h[:, p, 0:nh], total[:, p, 0:nh]).then_inc(rcp_d, 1)
                    wait_pair(dve, rcp_d, pr)
                    wait_pair(dve, rt_d, pr, 2)
                    dve.tensor_copy(inv[:, p, :].rearrange("p (h d) -> p h d", h=nh),
                                    inv_h[:, p, 0:nh].unsqueeze(2).broadcast_to([128, nh, D // nh])).then_inc(inv_d, 1)
                pr = at(OFF_PROJ)
                if pr is not None and MASKED[pr.phase]:
                    p = pr.p
                    dve.wait_ge(ld_m[p], 16 * (pr.half + 1))
                    wait_pair(dve, score_d, pr, 2)
                    dve.tensor_scalar(neg_m[:, p, :], stage_m[:, p, :], 0, None, ALU.is_equal).then_inc(neg_d, 1)
                pr = at(OFF_SCORE)
                if pr is not None:
                    p, nh = pr.p, heads(pr)
                    sc = ps[:, 2 * p:2 * p + nh // 8, :].rearrange("p b (h k) -> p (b h) k", k=S)
                    wait_pair(dve, score_d, pr)
                    wait_pair(dve, sub_d, pr, 2)
                    dve.tensor_reduce(top[:, p, 0:nh], sc, AX.X, ALU.max).then_inc(top_d, 1)
                    wait_pair(dve, top_d, pr)
                    wait_pair(dve, pt1_d, pr, 2)
                    wait_pair(dve, sum_d, pr, 2)
                    dve.tensor_tensor(prob[:, p, 0:nh * S].rearrange("p (h k) -> p h k", k=S), sc,
                                      top[:, p, 0:nh].unsqueeze(2).broadcast_to([128, nh, S]), ALU.subtract)\
                        .then_inc(sub_d, 1)
                pr = at(OFF_OUT)
                if pr is not None:
                    p, ph = pr.p, pr.phase
                    wait_pair(dve, out_d, pr)
                    wait_pair(dve, norm_d, pr, 2)
                    if ph > 0:
                        if ph == FF + 1:
                            wait_own(dve, f_x, pr)
                        elif ph == RO + 1:
                            dve.wait_ge(m_res, pr.i // SUB + 1 if isinstance(pr.i, int) else NT)
                        else:
                            dve.wait_ge(res_d, RES_BEFORE[ph - 1] + 1 + pr.i)
                    if not (isinstance(pr.n, int) and pr.n < 2) and POST[ph] != "none":
                        wait_pair(dve, res_d, pr, 2)
                    dve.tensor_tensor(y[:, p, :], ps[:, B_OUT, OUT], x_tok[:, pr.i, :], ALU.add).then_inc(y_d, 1)
                    if POST[ph] == "ln":
                        wait_pair(dve, y_d, pr)
                        dve.bn_stats(stats[:, p, :], y[:, p, :]).then_inc(bns_d, 1)
                        wait_pair(dve, bns_d, pr, apart=True)
                        dve.bn_aggr(moments[:, p, :], stats[:, p, :]).then_inc(agg_d, 1)
                        wait_pair(dve, agg_d, pr)
                        dve.tensor_scalar(spread[:, p, :], moments[:, p, 1:2], EPS, None, ALU.add).then_inc(spread_d, 1)
                    elif POST[ph] == "rms":
                        wait_pair(dve, y_d, pr)
                        dve.tensor_tensor_reduce(squares[:, p, :], y[:, p, :], y[:, p, :], 1.0 / D, EPS,
                                                 ALU.mult, ALU.add, spread[:, p, :]).then_inc(spread_d, 1)

                pr = follows(at, OFF_FY, FF)
                if pr is not None:
                    p = pr.p
                    wait_own(dve, f_turn, pr)
                    wait_own(dve, f_nn, pr, 2)
                    wait_pair(dve, res_d, pr)
                    dve.tensor_tensor(y_f[:, p, :], ps[:, B_OUT, TURN], x_tok[:, pr.i, :], ALU.add).then_inc(f_y, 1)
                    wait_own(dve, f_y, pr)
                    dve.bn_stats(stats_f[:, p, :], y_f[:, p, :]).then_inc(f_st, 1)
                    wait_own(dve, f_st, pr, apart=True)
                    dve.bn_aggr(mom_f[:, p, :], stats_f[:, p, :]).then_inc(f_ag, 1)
                    wait_own(dve, f_ag, pr)
                    dve.tensor_scalar(spread_f[:, p, :], mom_f[:, p, 1:2], EPS, None, ALU.add).then_inc(f_sp, 1)
                pr = follows(at, OFF_FN, FF)
                if pr is not None:
                    p = pr.p
                    wait_own(dve, f_w, pr)
                    dve.tensor_tensor_reduce(squares_f[:, p, :], w_f[:, p, :], w_f[:, p, :], 1.0 / D, EPS,
                                             ALU.mult, ALU.add, meansq_f[:, p, :]).then_inc(f_ms, 1)
                pr = follows(at, OFF_R2, RO)
                if pr is not None:
                    p = pr.p
                    wait_own(dve, r_ix, pr)
                    dve.tensor_copy(best_f[:, p, :], best_at[:, p, :]).then_inc(r_fx, 1)
                    wait_own(dve, r_exp, pr)
                    dve.tensor_scalar(den[:, p, :], e_gap[:, p, :], 1.0, None, ALU.add).then_inc(r_den, 1)
                    wait_own(dve, r_den, pr)
                    dve.reciprocal(gate1[:, p, :], den[:, p, :]).then_inc(r_g1, 1)
                    wait_own(dve, r_g1, pr)
                    dve.tensor_tensor(gate2[:, p, :], e_gap[:, p, :], gate1[:, p, :], ALU.mult).then_inc(r_g2, 1)
                    wait_own(dve, r_fx, pr)
                    dve.tensor_scalar(hot1[:, p, :], iota, best_f[:, p, 0:1], gate1[:, p, :],
                                      ALU.is_equal, ALU.mult).then_inc(r_h, 1)
                    wait_own(dve, r_g2, pr)
                    dve.tensor_scalar(hot2[:, p, :], iota, best_f[:, p, 1:2], gate2[:, p, :],
                                      ALU.is_equal, ALU.mult).then_inc(r_a, 1)
                    wait_own(dve, r_h, pr)
                    wait_own(dve, r_a, pr)
                    wait_own(dve, r_t, pr, 2)
                    dve.tensor_tensor(gates[:, p, :], hot1[:, p, :], hot2[:, p, :], ALU.add).then_inc(r_g, 1)
                pr = follows(at, OFF_R1, RO)
                if pr is not None:
                    p = pr.p
                    wait_own(dve, r_l, pr)
                    dve.tensor_copy(logit[:, p, :], ps[:, B_F, 128:128 + E]).then_inc(r_lc, 1)
                    wait_own(dve, r_lc, pr, apart=True)
                    dve.max(best[:, p, :], logit[:, p, :]).then_inc(r_mx, 1)
                    wait_own(dve, r_mx, pr, apart=True)
                    dve.max_index(best_at[:, p, :], best[:, p, :], logit[:, p, :]).then_inc(r_ix, 1)
                    dve.tensor_tensor(gap[:, p, :], best[:, p, 1:2], best[:, p, 0:1], ALU.subtract).then_inc(r_gap, 1)
                pr = follows(at, OFF_L3, LAST)
                if pr is not None:
                    wait_own(dve, l_o, pr)
                    x = x_t[:, bass.ds(pr.i * TOK, TOK)]
                    dve.tensor_tensor(x, sum_f[:, pr.p, :], x, ALU.add).then_inc(l_y, 1)

            def experts_end(t):
                dve.wait_ge(m_turn, t + 1)
                if not (isinstance(t, int) and t == 0):
                    dve.wait_ge(m_res, t)
                dve.tensor_tensor(y4[:, :, :], ps[:, B_TAIL, :].rearrange("p (s d) -> p s d", s=SUB),
                                  x_tok[:, bass.ds(t * SUB, SUB), :], ALU.add).then_inc(m_y, 1)

            def experts(t, first):
                chunks = (1 + E) * HC
                for q in range(E * HC):
                    e, c = divmod(q, HC)
                    k = q + HC
                    if c == 0:
                        dve.wait_ge(m_gate, E * t + (e + 1))
                    dve.wait_ge(m_act, chunks * t + (k + 1))
                    if not (first and q < ring):
                        dve.wait_ge(m_acc, chunks * t + ((k - ring + 1) if q >= ring else (q - ring + 1)))
                    dve.tensor_tensor(gated_h[:, k % ring, :], hid[:, k % ring, :], ps[:, B_GATE[(e + 1) % 2], :],
                                      ALU.mult).then_inc(m_gated, 1)
                    if q == 4 and not first:
                        experts_end(t - 1)

            run_slots(dve, GROUPS[0], slot, {4: residuals})
            tiles(dve, experts)
            experts_end(NT - 1)
            dve.sem_inc(bns_d, 2 * NP)
            dve.sem_inc(agg_d, 2 * NP)
            run_slots(dve, GROUPS[1], slot)


RES_BEFORE = [NP * sum(k != "none" for k in POST[:n]) for n in range(len(POST))]


def constants():
    r = np.arange(128)
    cst = np.zeros((128, C_END), np.float32)
    cst[:, C_ID:C_ID + 128] = np.eye(128)
    cst[:, C_G:C_G + 4] = r[:, None] // 32 == np.arange(4)
    cst[:, C_J16:C_J16 + 4] = r[:, None] % 32 // 8 == np.arange(4)
    cst[:, C_J8:C_J8 + 2] = r[:, None] % 32 // 16 == np.arange(2)
    cst[:, C_IOTA:C_IOTA + E] = np.arange(E)
    sel = np.zeros((E, E, 128), np.float32)
    sel[np.arange(E), np.arange(E)] = 1.0
    return cst, sel


def kernel(**inputs):
    import concourse.bacc as _bacc
    from concourse.bass_utils import run_bass_kernel_spmd as _run

    w = {k: np.asarray(x) for k, x in inputs.items()}
    L0, L1, L2, L3 = ({k[9:]: x for k, x in w.items() if k.startswith(f"L{n}_xattn_")} for n in range(4))
    cst, sel = constants()
    wat = np.stack([
        np.stack([L0["sa_wq"], L0["sa_wk"], L0["sa_wv"], L0["sa_wo"]]),
        np.stack([L0["ca_wq"], L0["ca_wk"], L0["ca_wv"], L0["ca_wo"]]),
        np.stack([L1[f"sa_w{k}"].T for k in "qkvo"]),
        np.stack([L1[f"ca_w{k}"].T for k in "qkvo"]),
        np.stack([L2[f"W{k}"].T for k in "qkvo"]),
        np.stack([L3[f"W_{k}"] for k in "qkvo"]),
    ])
    by_name = {
        "bq0": L0["sa_bq"], "bk0": L0["sa_bk"], "bv0": L0["sa_bv"], "bo0": L0["sa_bo"],
        "bq1": L0["ca_bq"], "bk1": L0["ca_bk"], "bv1": L0["ca_bv"], "bo1": L0["ca_bo"],
        "bq4": L2["bq"], "bk4": L2["bk"], "bv4": L2["bv"], "bo4": L2["bo"],
        "g1": L0["ln1_g"], "b1": L0["ln1_b"], "g2": L0["ln2_g"], "b2": L0["ln2_b"],
        "g3": L0["ln3_g"], "b3": L0["ln3_b"], "n1": L1["norm1_w"], "n2": L1["norm2_w"], "n3": L1["norm3_w"],
        "gL2": L2["ln_g"], "bL2": L2["ln_b"], "ffb2": L0["ff_b2"], "l3b1": L3["b1"], "l3b2": L3["b2"],
    }
    for c in range(HC):
        by_name[f"ffb1_{c}"] = L0["ff_b1"][128 * c:128 * c + 128]
    x = w["x"].reshape(NP, TOK, D)
    arrays = {
        "x_tok": x,
        "x_t": x.transpose(0, 2, 1),
        "ctx_t": w["ctx_1024"].reshape(NP, TOK, D).transpose(0, 2, 1),
        "m0": w["mask_BxSxS2_ik0"].reshape(NP, TOK, S),
        "m1": w["mask_BxSxS2_if1"].reshape(NP, TOK, S),
        "m2": w["mask_BxSxS_ik0"].reshape(NP, TOK, S),
        "m4": w["mask_BxSxS2_ik1"].reshape(NP, TOK, S),
        "cst": cst,
        "sel": sel,
        "vec": np.stack([by_name[k] for k in VECS], axis=1),
        "rows": np.stack([by_name[k] for k in ROWS]),
        "wat": wat.transpose(2, 0, 1, 3),
        "ffw1": L0["ff_w1"][:, None, :],
        "ffw2": L0["ff_w2"].reshape(HC, 128, D).transpose(1, 0, 2)[:, None],
        "gatew": np.pad(L1["gate_w"].T, ((0, 0), (0, 128 - E))),
        "mow1": np.concatenate([L1["sh_w1"][None], L1["exp_w1"]]).transpose(2, 0, 1),
        "mow2": np.concatenate([L1["sh_w2"][None], L1["exp_w2"]]).reshape(1 + E, D, HC, 128).transpose(3, 0, 2, 1),
        "l3w1": L3["w1"].T[:, None, :],
        "l3w2": L3["w2"].T[:, None, None, :],
    }
    nc = _bacc.Bacc("TRN2", target_bir_lowering=False, num_devices=1)
    feed, aps = {}, {}
    for name, arr in arrays.items():
        arr = np.ascontiguousarray(arr)
        feed[f"in_{name}"] = arr
        aps[name] = nc.dram_tensor(f"in_{name}", arr.shape, mybir.dt.from_np(arr.dtype), kind="ExternalInput").ap()
    out_t = nc.dram_tensor("out_t", [D, NP * TOK], F32, kind="ExternalOutput").ap()
    build(nc, aps, out_t)
    r = _run(nc, [feed], core_ids=[0])
    return np.ascontiguousarray(r.results[0]["out_t"].T).reshape(B, S, D)
```

```python
from contextlib import ExitStack

import numpy as np

import concourse.bass as bass
from concourse import mybir

F32 = mybir.dt.float32
F32R = mybir.dt.float32r
BF16 = mybir.dt.bfloat16
I32 = mybir.dt.int32
U32 = mybir.dt.uint32
ACT = mybir.ActivationFunctionType
ALU = mybir.AluOpType
AX = mybir.AxisListType

B, S, D = 32, 64, 128
TOK = 2 * S
NP = B // 2
E, HID = 8, 512
HC = HID // 128
TILE = 512
NT = B * S // TILE
SUB = TILE // 128
EPS = 1e-5
NEG = -1e20

HEADS = [16, 16, 16, 16, 16, 8]
SELF = [True, False, True, False, False, False]
MASKED = [True, True, True, True, True, False]
POST = ["ln", "ln", "rms", "rms", "ln", "none"]
LN_BEFORE = [0, NP, 2 * NP, 2 * NP, 2 * NP, 3 * NP]

VECS = ["bq0", "bk0", "bq1", "bk1", "bq4", "bk4", "bv0", "bv1", "bv4",
        "g1", "b1", "g2", "b2", "n1", "n2", "n3", "gL2", "bL2", "ffb2", "l3b1", "l3b2"] + \
       [f"ffb1_{c}" for c in range(HC)]
VCOL = {name: n for n, name in enumerate(VECS)}
ROWS = ["g1", "b1", "g2", "b2", "g3", "b3", "gL2", "bL2", "bo0", "bo1", "bo4"]
ROW = {name: n for n, name in enumerate(ROWS)}
BIASED = {0: 0, 1: 1, 4: 2}
C_ID, C_G, C_J16, C_J8, C_IOTA, C_END = 0, 128, 132, 136, 138, 146

OFF_PROJ, OFF_V, OFF_SCORE, OFF_PV, OFF_OUT, OFF_XT = 0, 1, 2, 3, 4, 5
OFF_F = 6
OFF_FY, OFF_FN, OFF_FB = 7, 8, 9
OFF_R1, OFF_R2, OFF_RT = 6, 7, 9
OFF_L3, OFF_ST = 7, 8
FF, RO, LAST = 1, 3, 5
STEADY = [6, 10, 10, 10, 6, 8]
LAST_OFF = OFF_FB


class Pair:

    def __init__(self, phase, i, half, parity):
        self.phase, self.i, self.p = phase, i, parity
        self.n = i + NP * phase
        self.half = half + NP // 2 * phase


def run_slots(eng, phases, slot, before=(), after=()):

    def fixed(s):
        def at(off):
            m = s - off
            if not 0 <= m < len(phases) * NP:
                return None
            i = m % NP
            return Pair(phases[m // NP], i, i // 2, i % 2)
        return at

    before, after = dict(before), dict(after)
    for part, phase in enumerate(phases):
        for s in range(STEADY[phase]):
            if part * NP + s in before:
                before[part * NP + s]()
            slot(fixed(part * NP + s))
            if part * NP + s in after:
                after[part * NP + s]()
        with eng.Fori(STEADY[phase] // 2, NP // 2) as h:
            for u in range(2):
                def at(off, h=h, u=u):
                    return Pair(phase, 2 * h + (u - off), h + (u - off) // 2, (u - off) % 2)
                slot(at)
    for s in range(len(phases) * NP, len(phases) * NP + LAST_OFF):
        slot(fixed(s))


GROUPS = [[0, 1, 2, 3], [4, 5]]


def build(nc, a, out_t):
    ctx = ExitStack()
    with ctx:
        def sb(name, shape, dt=F32):
            return ctx.enter_context(nc.sbuf_tensor(name, shape, dt))

        def sem(name):
            return ctx.enter_context(nc.semaphore(name))

        cst = sb("cst", [128, C_END])
        sel = sb("sel", [128, E, 128], F32R)
        idb = sb("idb", [128, 128], BF16)
        vec = sb("vec", [128, len(VECS)])
        rows = sb("rows", [128, len(ROWS), D])
        wat = sb("wat", [128, 6, 4, D])
        ffw1, ffw2 = sb("ffw1", [128, 1, HID]), sb("ffw2", [128, 1, HC, D])
        mow1_hi, mow1_lo, mow2_hi, mow2_lo = (sb(k, [128, 1 + E, HID], F32R)
                                              for k in ("mow1_hi", "mow1_lo", "mow2_hi", "mow2_lo"))
        stage_w = sb("stage_w", [128, 2, HID])
        l3w1, l3w2 = sb("l3w1", [128, 1, D]), sb("l3w2", [128, 1, 1, D])
        gatew = sb("gatew", [128, 128])
        ident, maskg = cst[:, C_ID:C_ID + 128], cst[:, C_G:C_G + 4]
        iota = cst[:, C_IOTA:C_IOTA + E]
        x_tok = sb("x_tok", [128, NP, D])
        x_t = sb("x_t", [128, NP * TOK])
        row_bias = sb("row_bias", [128, 3, D])
        half_neg = sb("half_neg", [128, 1])
        ones = sb("ones", [128, E])

        inv_h = sb("inv_h", [128, 2, 16])
        stage_x = sb("stage_x", [128, 2, TOK])
        stage_kv = sb("stage_kv", [128, 2, TOK])
        stage_m = sb("stage_m", [128, 2, S], I32)
        q_t, k_t = sb("q_t", [128, 2, TOK]), sb("k_t", [128, 2, TOK])
        q_by_g = sb("q_by_g", [128, 2, 4, TOK])
        k_by_j = sb("k_by_j", [128, 2, 4, TOK])
        prob = sb("prob", [128, 2, 16 * S])
        sel_raw = prob[0:2 * E, 1, :].rearrange("p (e t) -> p e t", e=E)
        v_16 = sb("v_16", [128, 2, 2, 8, 32])
        v_8 = sb("v_8", [128, 2, 2, 4, 32])
        neg_m = sb("neg_m", [128, 2, S], BF16)
        top = sb("top", [128, 2, 16])
        prob_t = sb("prob_t", [128, 2, 2, 512])
        total = sb("total", [128, 2, 16])
        inv = sb("inv", [128, 2, D])
        inv_t = sb("inv_t", [128, 2, TOK])
        heads_t = sb("heads_t", [128, 2, TOK])
        y = sb("y", [128, 2, D])
        squares = sb("squares", [128, 2, D])
        stats = sb("stats", [128, 2, 6])
        moments = sb("moments", [128, 2, 2])
        spread = sb("spread", [128, 2, 1])
        rstd = sb("rstd", [128, 2, 1])
        normed = sb("normed", [128, 2, D])
        scaled = sb("scaled", [128, 2, D])

        ring = 4
        x_hi, x_lo = sb("x_hi", [128, TILE], F32R), sb("x_lo", [128, TILE], F32R)
        hid_hi, hid_lo = sb("hid_hi", [128, ring, TILE], F32R), sb("hid_lo", [128, ring, TILE], F32R)
        hid = prob[:, :, :].rearrange("p a (b c) -> p (a b) c", c=TILE)
        gate_b = k_by_j[:, :, :, :].rearrange("p a b c -> p a (b c)")
        weighted = prob_t[:, 0, 0, :]
        mlp_o = prob_t[:, 0, 1, :]
        y4 = prob_t[:, 1, 0, :].rearrange("p (s d) -> p s d", s=SUB)
        gates_t = sb("gates_t", [128, NP * TOK], F32R)

        hid_f = sb("hid_f", [128, 2, HC, TOK])
        bv_cols = hid_f[:, 0, 0:3, :]
        sum_f = sb("sum_f", [128, 2, TOK])
        y_f = sb("y_f", [128, 2, D])
        stats_f = sb("stats_f", [128, 2, 6])
        mom_f = sb("mom_f", [128, 2, 2])
        spread_f, rstd_f = sb("spread_f", [128, 2, 1]), sb("rstd_f", [128, 2, 1])
        n_f, z_f, w_f = (sb(k, [128, 2, D]) for k in ("n_f", "z_f", "w_f"))
        meansq_f, rrms_f = sb("meansq_f", [128, 2, 1]), sb("rrms_f", [128, 2, 1])
        xn_f = sb("xn_f", [128, 2, D])

        hn_t = n_f
        logit = sb("logit", [128, 2, E])
        best = sb("best", [128, 2, 8])
        best_at = sb("best_at", [128, 2, 8], U32)
        best_f = sb("best_f", [128, 2, 8])
        gap, e_gap, den, gate1, gate2 = (sb(k, [128, 2, 1]) for k in ("gap", "e_gap", "den", "gate1", "gate2"))
        hot1, hot2, gate_f = (sb(k, [128, 2, E]) for k in ("hot1", "hot2", "gate_f"))
        gates = sb("gates", [128, 2, 2 * E])

        ps = ctx.enter_context(nc.psum_tensor("ps", [128, 8, 512], F32))
        B_PROJ, B_HEADS, B_OUT, B_F = 4, 5, 6, 7
        XT, FB, OUT, TURN = (slice(128 * n, 128 * n + 128) for n in range(4))
        B_GATE, B_ACC, B_TAIL = (3, 4), (5, 6), 7
        h_banks = 3

        loaded = {k: sem(f"loaded_{k}") for k in ("small", "x_tok", "rows", "wat", "ff", "l3", "sel")}
        set_zero, set_id, set_bv, set_sel, set_mm, set_bias = (
            sem(k) for k in ("set_zero", "set_id", "set_bv", "set_sel", "set_mm", "set_bias"))
        ld_x = [sem(f"ld_x{p}") for p in range(2)]
        ld_kv = [sem(f"ld_kv{p}") for p in range(2)]
        ld_m = [sem(f"ld_m{p}") for p in range(2)]
        proj_d, vproj_d, score_d, pt0_d, pt1_d, rt_d, pv_d, out_d, xt_d = (
            sem(k) for k in ("proj_d", "vproj_d", "score_d", "pt0_d", "pt1_d", "rt_d", "pv_d", "out_d", "xt_d"))
        q_e, k_e, v_e, exp_d, pt0_e, pt1_e, rt_e, xt_e = (
            sem(k) for k in ("q_e", "k_e", "v_e", "exp_d", "pt0_e", "pt1_e", "rt_e", "xt_e"))
        top_d, sub_d, sum_d, rcp_d, inv_d, heads_d, y_d, bns_d, agg_d, spread_d, norm_d = (
            sem(k) for k in ("top_d", "sub_d", "sum_d", "rcp_d", "inv_d", "heads_d", "y_d", "bns_d", "agg_d", "spread_d", "norm_d"))
        neg_d = sem("neg_d")
        qg_d, kj_d, rstd_d, gsc_d, res_d = (sem(k) for k in ("qg_d", "kj_d", "rstd_d", "gsc_d", "res_d"))

        f_h, f_r, f_acc, f_o, f_turn, f_y, f_st, f_ag, f_sp, f_rs, f_nn, f_z, f_w, f_x, f_ms, f_rr, f_xn, f_back, f_xt = (
            sem(f"f_{k}") for k in ("h", "r", "acc", "o", "turn", "y", "st", "ag", "sp", "rs", "nn", "z", "w", "x",
                                    "ms", "rr", "xn", "back", "xt"))
        l_h, l_r, l_acc, l_o, l_y = (sem(f"l_{k}") for k in ("h", "r", "acc", "o", "y"))
        r_x, r_l, r_lc, r_mx, r_ix, r_gap, r_exp, r_fx, r_den, r_g1, r_g2, r_h, r_a, r_gf, r_gh, r_g, r_t, r_te = (
            sem(f"r_{k}") for k in ("x", "l", "lc", "mx", "ix", "gap", "exp", "fx", "den", "g1", "g2", "h", "a", "gf", "gh", "g",
                                    "t", "te"))
        m_xh, m_x, m_h, m_act, m_hi, m_lo, m_lop, m_acc, m_gate, m_gate_e, m_first, m_mul, m_add, m_turn, m_y, m_back, m_xt, m_res = (
            sem(f"m_{k}") for k in ("xh", "x", "h", "act", "hi", "lo", "lop", "acc", "gate", "gate_e", "first", "mul", "add",
                                    "turn", "y", "back", "xt", "res"))
        ld_w = [sem(f"ld_w{p}") for p in range(2)]
        split_hi, split_lo = sem("split_hi"), sem("split_lo")
        stored = sem("stored")

        def v(name):
            return vec[:, VCOL[name]:VCOL[name] + 1]

        def heads(pair):
            return HEADS[pair.phase]

        def tiles(eng, body):
            body(0, True)
            with eng.Fori(1, NT) as t:
                body(t, False)

        def wait_apart(eng, sem_, value):
            eng.wait_ge(loaded["small"], 48)
            eng.wait_ge(sem_, value)

        def wait_pair(eng, sem_, pair, back=0, apart=False):
            if isinstance(pair.n, int) and pair.n - back < 0:
                return
            (wait_apart if apart else lambda e, *x: e.wait_ge(*x))(eng, sem_, pair.n + (1 - back))

        def wait_own(eng, sem_, pr, back=0, apart=False):
            if isinstance(pr.i, int) and pr.i - back < 0:
                return
            (wait_apart if apart else lambda e, *x: e.wait_ge(*x))(eng, sem_, pr.i + (1 - back))

        def piece(n):
            e, which = divmod(n, 2)
            return ((mow1_hi[:, e, :], mow1_lo[:, e, :]), (mow2_hi[:, e, :], mow2_lo[:, e, :]))[which]

        pieces = 2 * (1 + E)
        split_at = dict(zip([2 * NP + s for s in range(STEADY[2])] + [3 * NP + s for s in range(STEADY[3])], range(pieces)))
        assert len(split_at) == pieces

        def low_by_pool(k):
            return k % 2 == 1

        def wait_low(eng, k, t):
            made = (1 + E) * HC // 2
            eng.wait_ge(m_lop if low_by_pool(k) else m_lo, made * t + (k // 2 + 1))

        def follows(at, off, phase):
            pr = at(off)
            return pr if pr is not None and pr.phase == phase else None

        block = ctx.enter_context(nc.Block())

        @block.sync
        def _(sp):
            sp.dma_start(wat[:, 0:1, :, :], a["wat"][:, 0:1, :, :]).then_inc(loaded["wat"], 16)
            sp.dma_start(vec[:, :], a["vec"]).then_inc(loaded["small"], 16)
            sp.dma_start(cst[:, :], a["cst"]).then_inc(loaded["small"], 16)
            sp.dma_start(sel_raw, a["sel"]).then_inc(loaded["sel"], 16)
            sp.dma_start(gatew[:, :], a["gatew"]).then_inc(loaded["small"], 16)

            def load_ff():
                sp.dma_start(ffw1[:, :, :], a["ffw1"]).then_inc(loaded["ff"], 16)
                sp.dma_start(ffw2[:, :, :, :], a["ffw2"]).then_inc(loaded["ff"], 16)

            def load_piece(n):
                e, which = divmod(n, 2)
                if n >= 2:
                    sp.wait_ge(split_lo, n - 1)
                sp.dma_start(stage_w[:, n % 2, :], a["mow2" if which else "mow1"][:, e, :]).then_inc(ld_w[n % 2], 16)

            def load_last():
                sp.dma_start(l3w1[:, :, :], a["l3w1"]).then_inc(loaded["l3"], 16)
                sp.dma_start(l3w2[:, :, :, :], a["l3w2"]).then_inc(loaded["l3"], 16)

            masks = [a["m0"], a["m1"], a["m2"], a["m1"], a["m4"], None]

            def load(pr):
                ph, i, p = pr.phase, pr.i, pr.p
                if ph == FF + 1:
                    sp.wait_ge(f_xt, i + 1 if isinstance(i, int) else NP)
                elif ph == RO + 1:
                    sp.wait_ge(m_xt, i // SUB + 1 if isinstance(i, int) else NT)
                wait_pair(sp, proj_d, pr, 2)
                if ph == 0:
                    tok = a["x_t"][bass.ds(i, 1), :, :].rearrange("a p t -> p (a t)")
                else:
                    tok = x_t[:, bass.ds(i * TOK, TOK)]
                sp.dma_start(stage_x[:, p, :], tok).then_inc(ld_x[p], 16)
                src = tok if SELF[ph] else a["ctx_t"][bass.ds(i, 1), :, :].rearrange("a p t -> p (a t)")
                wait_pair(sp, vproj_d, pr, 2)
                sp.dma_start(stage_kv[:, p, :], src).then_inc(ld_kv[p], 16)
                if MASKED[ph]:
                    wait_pair(sp, neg_d, pr, 2)
                    sp.dma_start(stage_m[:, p, :], masks[ph][bass.ds(i, 1), :, :].rearrange("a p t -> p (a t)"))\
                        .then_inc(ld_m[p], 16)

            def slot(at):
                pr = at(OFF_PROJ)
                if pr is not None:
                    load(pr)
                pr = follows(at, OFF_ST, LAST)
                if pr is not None:
                    wait_own(sp, l_y, pr)
                    cols = bass.ds(pr.i * TOK, TOK)
                    sp.dma_start(out_t[:, cols], x_t[:, cols]).then_inc(stored, 16)

            run_slots(sp, GROUPS[0], slot,
                      {5: load_ff, NP: load_last, **{s: lambda n=n: load_piece(n) for s, n in split_at.items()}})
            run_slots(sp, GROUPS[1], slot)
            sp.wait_ge(stored, 16 * NP)

        @block.gpsimd
        def _(pool):
            pool.memset(v_16[:, :, :, :, :], 0.0).then_inc(set_zero, 1)
            pool.memset(v_8[:, :, :, :, :], 0.0).then_inc(set_zero, 1)
            pool.memset(half_neg[:, :], -0.5).then_inc(set_zero, 1)
            pool.memset(ones[:, :], 1.0).then_inc(set_zero, 1)
            pool.memset(gates_t[:, :].bitcast(F32), 0.0).then_inc(set_zero, 1)
            pool.memset(sel[:, :, :].bitcast(F32), 0.0).then_inc(set_zero, 1)
            pool.wait_ge(set_zero, 6)
            pool.wait_ge(loaded["small"], 48)

            def slot(at):
                pr = follows(at, OFF_FN, FF)
                if pr is not None:
                    wait_own(pool, f_sp, pr)
                    wait_own(pool, f_nn, pr, 2)
                    pool.tensor_tensor(rstd_f[:, pr.p, :], spread_f[:, pr.p, :], half_neg[:, :], ALU.pow)\
                        .then_inc(f_rs, 1)
                pr = follows(at, OFF_FB, FF)
                if pr is not None:
                    wait_own(pool, f_ms, pr)
                    wait_own(pool, f_xn, pr, 2)
                    pool.tensor_tensor(rrms_f[:, pr.p, :], meansq_f[:, pr.p, :], half_neg[:, :], ALU.pow)\
                        .then_inc(f_rr, 1)
                pr = follows(at, OFF_FN, FF)
                if pr is not None:
                    p = pr.p
                    wait_own(pool, f_nn, pr)
                    wait_own(pool, f_x, pr, 2)
                    pool.tensor_tensor(z_f[:, p, :], n_f[:, p, :], rows[:, ROW["g3"], :], ALU.mult).then_inc(f_z, 1)
                    wait_own(pool, f_z, pr)
                    wait_own(pool, f_xn, pr, 2)
                    pool.tensor_tensor(w_f[:, p, :], z_f[:, p, :], rows[:, ROW["b3"], :], ALU.add).then_inc(f_w, 1)
                    pool.tensor_tensor(x_tok[:, pr.i, :], z_f[:, p, :], rows[:, ROW["b3"], :], ALU.add).then_inc(f_x, 1)
                pr = at(OFF_XT)
                if pr is not None and POST[pr.phase] == "ln":
                    p = pr.p
                    g, b = {0: (rows[:, ROW["g1"], :], row_bias[:, 1, :]),
                            1: (rows[:, ROW["g2"], :], rows[:, ROW["b2"], :]),
                            4: (rows[:, ROW["gL2"], :], rows[:, ROW["bL2"], :])}[pr.phase]
                    if isinstance(pr.n, int) and pr.n == 0:
                        pool.wait_ge(loaded["rows"], 16)
                        pool.wait_ge(set_bias, 3)
                    wait_pair(pool, norm_d, pr)
                    if not (isinstance(pr.n, int) and pr.n == 0):
                        pool.wait_ge(res_d, pr.n)
                    pool.tensor_tensor(scaled[:, p, :], normed[:, p, :], g, ALU.mult).then_inc(gsc_d, 1)
                    pool.wait_ge(gsc_d, pr.i + LN_BEFORE[pr.phase] + 1)
                    pool.tensor_tensor(x_tok[:, pr.i, :], scaled[:, p, :], b, ALU.add).then_inc(res_d, 1)
                elif pr is not None and POST[pr.phase] == "rms":
                    wait_pair(pool, y_d, pr, 0, apart=True)
                    pool.tensor_copy(x_tok[:, pr.i, :], y[:, pr.p, :]).then_inc(res_d, 1)
                pr = at(OFF_PROJ)
                if pr is not None:
                    p = pr.p
                    wait_pair(pool, q_e, pr)
                    wait_pair(pool, score_d, pr, 2)
                    pool.tensor_tensor(q_by_g[:, p, :, :], q_t[:, p:p + 1, :].broadcast_to([128, 4, TOK]),
                                       maskg.unsqueeze(2).broadcast_to([128, 4, TOK]), ALU.mult).then_inc(qg_d, 1)
                pr = at(OFF_OUT)
                if pr is not None and POST[pr.phase] != "none":
                    p = pr.p
                    wait_pair(pool, spread_d, pr)
                    wait_pair(pool, norm_d, pr, 2)
                    pool.tensor_tensor(rstd[:, p, :], spread[:, p, :], half_neg[:, :], ALU.pow)\
                        .then_inc(rstd_d, 1)
                pr = at(OFF_PROJ)
                if pr is not None:
                    p, nj = pr.p, heads(pr) // 4
                    cj = C_J16 if nj == 4 else C_J8
                    wait_pair(pool, k_e, pr)
                    pool.tensor_tensor(k_by_j[:, p, 0:nj, :], k_t[:, p:p + 1, :].broadcast_to([128, nj, TOK]),
                                       cst[:, cj:cj + nj].unsqueeze(2).broadcast_to([128, nj, TOK]), ALU.mult)\
                        .then_inc(kj_d, 1)
                pr = follows(at, OFF_R2, RO)
                if pr is not None:
                    p = pr.p
                    wait_own(pool, r_h, pr)
                    wait_own(pool, r_a, pr)
                    pool.tensor_tensor(gate_f[:, p, :], hot1[:, p, :], hot2[:, p, :], ALU.add).then_inc(r_gf, 1)
                    wait_own(pool, r_gf, pr)
                    wait_own(pool, r_t, pr, 2)
                    pool.tensor_tensor(gates[:, p, 0:E].bitcast(F32R), gate_f[:, p, :], ones[:, :], ALU.mult)\
                        .then_inc(r_gh, 1)
                    wait_own(pool, r_gh, pr)
                    pool.tensor_tensor(gates[:, p, E:2 * E], gate_f[:, p, :], gates[:, p, 0:E], ALU.subtract)\
                        .then_inc(r_g, 1)

            def experts_end(t):
                pool.wait_ge(m_y, t + 1)
                pool.tensor_tensor(x_tok[:, bass.ds(t * SUB, SUB), :], y4,
                                   row_bias[:, 2:3, :].broadcast_to([128, SUB, D]), ALU.add).then_inc(m_res, 1)

            def split_low(n):
                pool.wait_ge(split_hi, n + 1)
                high, low = piece(n)
                pool.tensor_tensor(low, stage_w[:, n % 2, :], high.bitcast(F32), ALU.subtract).then_inc(split_lo, 1)

            def experts(t, first):
                chunks = (1 + E) * HC
                for k in range(chunks):
                    if low_by_pool(k):
                        pool.wait_ge(m_hi, chunks * t + (k + 1))
                        if not (first and k < ring):
                            pool.wait_ge(m_acc, chunks * t + (k - ring + 1))
                        pool.tensor_tensor(hid_lo[:, k % ring, :], hid[:, k % ring, :], hid_hi[:, k % ring, :].bitcast(F32),
                                           ALU.subtract).then_inc(m_lop, 1)
                    if not first and k == 20:
                        experts_end(t - 1)

            run_slots(pool, GROUPS[0], slot, after={s: lambda n=n: split_low(n) for s, n in split_at.items()})
            tiles(pool, experts)
            experts_end(NT - 1)
            run_slots(pool, GROUPS[1], slot)

        @block.tensor
        def _(pe):
            def bias_rows():
                pe.wait_ge(set_bv, 3)
                pe.wait_ge(loaded["wat"], 32)
                for ph, c in BIASED.items():
                    mm = pe.matmul(ps[:, B_OUT, c * D:(c + 1) * D], bv_cols[:, c, :], wat[:, ph, 3, :],
                                   start=True, stop=True)
                mm.then_inc(set_mm, 1)

            def bias_out():
                pe.wait_ge(set_bias, 1)

            pe.wait_ge(loaded["wat"], 16)
            pe.wait_ge(set_id, 1)

            def slot(at):
                pr = at(OFF_SCORE)
                if pr is not None:
                    p, nj = pr.p, heads(pr) // 4
                    masked = MASKED[pr.phase]
                    hb = min(8, heads(pr))
                    if masked:
                        wait_pair(pe, neg_d, pr)
                    wait_pair(pe, pt1_e, pr, 2)
                    wait_pair(pe, qg_d, pr)
                    wait_pair(pe, kj_d, pr)
                    for bank in range(heads(pr) // hb):
                        if masked:
                            pe.matmul(ps[:, 2 * p + bank, :].rearrange("p (h k) -> p h k", k=S), idb[:, :],
                                      neg_m[:, p:p + 1, :].broadcast_to([128, hb, S]), start=True, stop=False,
                                      skip_group_check=True)
                        per = hb // nj
                        for k in range(per):
                            g = bank * per + k
                            for b in range(2):
                                mm = pe.matmul(
                                    ps[S * b:S * b + S, 2 * p + bank, k * nj * S:(k + 1) * nj * S]
                                    .rearrange("p (h k) -> p h k", k=S),
                                    q_by_g[:, p, g, S * b:S * b + S], k_by_j[:, p, 0:nj, S * b:S * b + S],
                                    start=not masked and k == 0, stop=True, skip_group_check=True)
                    mm.then_inc(score_d, 1)
                pr = follows(at, OFF_FY, FF)
                if pr is not None:
                    wait_own(pe, f_r, pr)
                    for c in range(HC):
                        mm = pe.matmul(ps[:, B_F, 0:TOK], ffw2[:, 0, c, :], hid_f[:, pr.p, c, :], start=c == 0, stop=c == HC - 1)
                    mm.then_inc(f_acc, 1)
                pr = follows(at, OFF_L3, LAST)
                if pr is not None:
                    wait_own(pe, l_r, pr)
                    pe.matmul(ps[:, B_F, 128:128 + TOK], l3w2[:, 0, 0, :], hid_f[:, pr.p, 0, :], start=True, stop=True)\
                        .then_inc(l_acc, 1)
                pr = at(OFF_PV)
                if pr is not None:
                    p, npr = pr.p, heads(pr) // 2
                    wait_pair(pe, exp_d, pr)
                    for half, done in enumerate((pt0_d, pt1_d)):
                        for k in range(npr // 2):
                            q = half * (npr // 2) + k
                            mm = pe.transpose(ps[:, 2 * p + half, k * 128:(k + 1) * 128],
                                              prob[:, p, q * 128:(q + 1) * 128], ident)
                        mm.then_inc(done, 1)
                pr = at(OFF_XT)
                if pr is not None:
                    wait_pair(pe, norm_d, pr)
                    if pr.phase == FF or pr.phase == FF + 1:
                        done = follows(at, OFF_FN, FF)
                        if done is not None:
                            wait_own(pe, f_y, done)
                    done = follows(at, OFF_FB, FF)
                    if done is not None:
                        wait_own(pe, f_xn, done)
                        pe.transpose(ps[:, B_OUT, FB], xn_f[:, done.p, :], ident).then_inc(f_back, 1)
                    pe.transpose(ps[:, B_OUT, XT], normed[:, pr.p, :], ident).then_inc(xt_d, 1)
                pr = follows(at, OFF_RT, RO)
                if pr is not None:
                    wait_own(pe, r_te, pr, 1)
                    wait_own(pe, r_g, pr)
                    pe.wait_ge(r_lc, min(pr.i + 3, NP) if isinstance(pr.i, int) else pr.i + 3)
                    pe.transpose(ps[0:2 * E, B_F, 0:TOK], gates[:, pr.p, :], ident).then_inc(r_t, 1)
                pr = at(OFF_V)
                if pr is not None:
                    ph, p, dk = pr.phase, pr.p, D // heads(pr)
                    wait_pair(pe, k_e, pr)
                    wait_pair(pe, v_e, pr, 1)
                    turned = at(OFF_PV)
                    if turned is not None:
                        wait_pair(pe, rt_e, turned, 1)
                    wv = wat[:, ph, 2, :].rearrange("c (h par d) -> c par h d", par=2, d=dk)
                    for b in range(2):
                        for par in range(2):
                            mm = pe.matmul(ps[S * par:S * par + S, B_PROJ, 256 + 64 * b:320 + 64 * b]
                                           .rearrange("p (h d) -> p h d", d=dk),
                                           stage_kv[:, p, S * b:S * b + S], wv[:, par], start=True, stop=True,
                                           skip_group_check=True)
                    mm.then_inc(vproj_d, 1)
                pr = at(OFF_PROJ)
                if pr is not None:
                    ph, p = pr.phase, pr.p
                    pe.wait_ge(ld_x[p], 16 * (pr.half + 1))
                    pe.wait_ge(ld_kv[p], 16 * (pr.half + 1))
                    pe.matmul(ps[:, B_PROJ, 0:128], wat[:, ph, 0, :], stage_x[:, p, :], start=True, stop=True)
                    pe.matmul(ps[:, B_PROJ, 128:256], wat[:, ph, 1, :], stage_kv[:, p, :], start=True, stop=True)\
                        .then_inc(proj_d, 1)
                pr = at(OFF_PV)
                if pr is not None:
                    wait_pair(pe, inv_d, pr)
                    wait_pair(pe, rt_e, pr, 1)
                    if at(OFF_V) is None:
                        pe.wait_ge(v_e, NP * (pr.phase + 1))
                    pe.transpose(ps[:, B_PROJ, 384:512], inv[:, pr.p, :], ident).then_inc(rt_d, 1)
                pr = at(OFF_OUT)
                if pr is not None:
                    wait_pair(pe, heads_d, pr)
                    before = at(OFF_XT)
                    if before is not None:
                        wait_pair(pe, xt_e, before)
                        before = follows(at, OFF_FB, FF)
                        if before is not None:
                            wait_own(pe, f_xt, before)
                    done = follows(at, OFF_FY, FF)
                    if done is not None:
                        wait_own(pe, f_o, done)
                        pe.transpose(ps[:, B_OUT, TURN], sum_f[:, done.p, :], ident).then_inc(f_turn, 1)
                    pe.matmul(ps[:, B_OUT, OUT], heads_t[:, pr.p, :], wat[:, pr.phase, 3, :], start=True, stop=True)\
                        .then_inc(out_d, 1)
                pr = follows(at, OFF_F, FF)
                if pr is not None:
                    x = x_t[:, bass.ds(pr.i * TOK, TOK)]
                    if isinstance(pr.i, int) and pr.i == 0:
                        pe.wait_ge(loaded["ff"], 32)
                    wait_own(pe, f_o, pr, 1)
                    wait_pair(pe, xt_e, pr)
                    for c in range(HC):
                        mm = pe.matmul(ps[:, B_F, c * 128:(c + 1) * 128], ffw1[:, 0, c * 128:(c + 1) * 128], x,
                                       start=True, stop=True)
                    mm.then_inc(f_h, 1)
                pr = follows(at, OFF_F, LAST)
                if pr is not None:
                    if isinstance(pr.i, int) and pr.i == 0:
                        pe.wait_ge(loaded["l3"], 32)
                    wait_own(pe, l_o, pr, 1)
                    wait_pair(pe, xt_e, pr)
                    pe.matmul(ps[:, B_F, 0:TOK], l3w1[:, 0, :], x_t[:, bass.ds(pr.i * TOK, TOK)], start=True, stop=True)\
                        .then_inc(l_h, 1)
                pr = follows(at, OFF_R1, RO)
                if pr is not None:
                    wait_own(pe, r_te, pr, OFF_RT - OFF_R1)
                    wait_own(pe, r_lc, pr, 1)
                    wait_own(pe, r_x, pr)
                    pe.matmul(ps[:, B_F, 128:128 + E], hn_t[:, pr.p, :], gatew[:, 0:E], start=True, stop=True)\
                        .then_inc(r_l, 1)
                pr = at(OFF_PV)
                if pr is not None:
                    p, npr = pr.p, heads(pr) // 2
                    vb = v_16 if npr == 8 else v_8
                    wait_pair(pe, v_e, pr)
                    wait_pair(pe, heads_d, pr, 1)
                    wait_pair(pe, pt0_e, pr)
                    wait_pair(pe, pt1_e, pr)
                    step = npr // 4
                    for b in range(2):
                        for k in range(step):
                            for g in range(4):
                                q = g * step + k
                                half, c = divmod(q, npr // 2)
                                mm = pe.matmul(ps[32 * g:32 * g + 32, B_HEADS, S * b:S * b + S],
                                               vb[:, p, b, q, :],
                                               prob_t[:, p, half, c * 128 + S * b:c * 128 + S * b + S],
                                               start=k == 0, stop=k == step - 1, skip_group_check=True)
                    mm.then_inc(pv_d, 1)

            chunks = (1 + E) * HC

            def product(out, w_hi, w_lo, m_hi_, m_lo_, start, stop):
                pe.matmul(out, w_hi, m_hi_, start=start, stop=False)
                pe.matmul(out, w_hi, m_lo_, start=False, stop=False)
                return pe.matmul(out, w_lo, m_hi_, start=False, stop=stop)

            def turn(t):
                pe.wait_ge(m_add, E * t + E)
                if not (isinstance(t, int) and t == 0):
                    pe.wait_ge(m_xt, t)
                for s in range(SUB):
                    mm = pe.transpose(ps[:, B_TAIL, s * 128:(s + 1) * 128], mlp_o[:, s * 128:(s + 1) * 128], ident)
                mm.then_inc(m_turn, 1)

            def back(t):
                pe.wait_ge(m_y, t + 1)
                for s in range(SUB):
                    mm = pe.transpose(ps[:, B_TAIL, s * 128:(s + 1) * 128], y4[:, s, :], ident)
                mm.then_inc(m_back, 1)

            def experts(t, first):
                if first:
                    pe.wait_ge(split_lo, pieces)
                    pe.wait_ge(r_te, NP)
                pe.wait_ge(m_x, t + 1)
                lag = 3
                for k in range(chunks + lag):
                    if k < chunks:
                        e, c = divmod(k, HC)
                        cols = slice(c * 128, (c + 1) * 128)
                        if not (first and k < h_banks):
                            pe.wait_ge(m_act, chunks * t + (k - h_banks + 1))
                        product(ps[:, k % h_banks, :], mow1_hi[:, e, cols], mow1_lo[:, e, cols], x_hi[:, :], x_lo[:, :],
                                True, True).then_inc(m_h, 1)
                        if e >= 1 and c == 0:
                            if not (first and e <= 2):
                                pe.wait_ge(m_gate_e, E * t + (e - 2))
                            pe.matmul(ps[:, B_GATE[e % 2], :], sel[:, e - 1, :], gates_t[:, bass.ds(t * TILE, TILE)], start=True, stop=True).then_inc(m_gate, 1)
                    if k >= lag:
                        q = k - lag
                        e, c = divmod(q, HC)
                        wait_low(pe, q, t)
                        if c == 0:
                            if e == 2:
                                pe.wait_ge(m_first, t + 1)
                            elif e > 2:
                                pe.wait_ge(m_mul, E * t + (e - 2))
                            elif not first:
                                pe.wait_ge(m_mul, E * t - (1 if e else 0))
                        cols = slice(c * 128, (c + 1) * 128)
                        product(ps[:, B_ACC[e % 2], :], mow2_hi[:, e, cols], mow2_lo[:, e, cols], hid_hi[:, q % ring, :],
                                hid_lo[:, q % ring, :], c == 0, c == HC - 1).then_inc(m_acc, 1)
                    if not first and k == 7:
                        turn(t - 1)
                    if not first and k == 18:
                        back(t - 1)

            run_slots(pe, GROUPS[0], slot, {3: bias_rows, 4: bias_out})
            tiles(pe, experts)
            turn(NT - 1)
            back(NT - 1)
            run_slots(pe, GROUPS[1], slot)

        @block.scalar
        def _(act):
            act.wait_ge(loaded["small"], 48)
            act.dma_start(wat[:, 1:6, :, :], a["wat"][:, 1:6, :, :]).then_inc(loaded["wat"], 16)
            act.dma_start(rows[:, :, :], a["rows"].partition_broadcast(128)).then_inc(loaded["rows"], 16)
            act.dma_start(x_tok[:, :, :], a["x_tok"].rearrange("i p d -> p i d")).then_inc(loaded["x_tok"], 16)
            act.wait_ge(set_zero, 2)
            biases = {0: ("bq0", "bk0"), 1: ("bq1", "bk1"), 4: ("bq4", "bk4")}

            def slot(at):
                pr = follows(at, OFF_FY, FF)
                if pr is not None:
                    wait_own(act, f_acc, pr)
                    wait_own(act, f_turn, pr, 2)
                    act.activation(sum_f[:, pr.p, :], ps[:, B_F, 0:TOK], ACT.Identity, bias=v("ffb2")).then_inc(f_o, 1)
                pr = follows(at, OFF_L3, LAST)
                if pr is not None:
                    wait_own(act, l_acc, pr)
                    wait_own(act, l_y, pr, 2)
                    act.activation(sum_f[:, pr.p, :], ps[:, B_F, 128:128 + TOK], ACT.Identity, bias=v("l3b2"))\
                        .then_inc(l_o, 1)
                pr = at(OFF_PV)
                if pr is not None:
                    p = pr.p
                    w = 128 * (heads(pr) // 4)
                    wait_pair(act, pv_d, pr, 2)
                    wait_pair(act, pt0_d, pr)
                    act.activation(prob_t[:, p, 0, 0:w], ps[:, 2 * p, 0:w], ACT.Copy).then_inc(pt0_e, 1)
                    wait_pair(act, pt1_d, pr)
                    act.activation(prob_t[:, p, 1, 0:w], ps[:, 2 * p + 1, 0:w], ACT.Copy).then_inc(pt1_e, 1)
                pr = at(OFF_XT)
                if pr is not None:
                    ph = pr.phase
                    wait_pair(act, xt_d, pr)
                    dst, src = x_t[:, bass.ds(pr.i * TOK, TOK)], ps[:, B_OUT, XT]
                    if ph == RO:
                        wait_own(act, r_l, pr, 2)
                        act.activation(hn_t[:, pr.p, :], src, ACT.Copy, scale=v("n3")).then_inc(r_x, 1)
                    if POST[ph] == "ln":
                        g, b = {0: ("g1", "b1"), 1: ("g2", "b2"), 4: ("gL2", "bL2")}[ph]
                        act.activation(dst, src, ACT.Identity, bias=v(b), scale=v(g)).then_inc(xt_e, 1)
                    elif POST[ph] == "rms":
                        act.activation(dst, src, ACT.Copy, scale=v({2: "n2", 3: "n3"}[ph])).then_inc(xt_e, 1)
                    else:
                        act.activation(dst, src, ACT.Copy).then_inc(xt_e, 1)
                pr = follows(at, OFF_FB, FF)
                if pr is not None:
                    wait_own(act, f_back, pr)
                    act.activation(x_t[:, bass.ds(pr.i * TOK, TOK)], ps[:, B_OUT, FB], ACT.Copy, scale=v("n1"))\
                        .then_inc(f_xt, 1)
                pr = follows(at, OFF_RT, RO)
                if pr is not None:
                    wait_own(act, r_t, pr)
                    act.activation(gates_t[0:2 * E, bass.ds(pr.i * TOK, TOK)], ps[0:2 * E, B_F, 0:TOK], ACT.Copy).then_inc(r_te, 1)
                pr = at(OFF_PROJ)
                if pr is not None:
                    p = pr.p
                    wait_pair(act, proj_d, pr)
                    turned = at(OFF_PV)
                    if turned is not None:
                        wait_pair(act, rt_d, turned)
                    wait_pair(act, qg_d, pr, 2)
                    wait_pair(act, kj_d, pr, 2)
                    for n, (dst, done) in enumerate(((q_t, q_e), (k_t, k_e))):
                        src = ps[:, B_PROJ, 128 * n:128 * n + 128]
                        if pr.phase in biases:
                            act.activation(dst[:, p, :], src, ACT.Identity, bias=v(biases[pr.phase][n])).then_inc(done, 1)
                        else:
                            act.activation(dst[:, p, :], src, ACT.Copy).then_inc(done, 1)
                pr = at(OFF_PV)
                if pr is not None:
                    p = pr.p
                    wait_pair(act, rt_d, pr)
                    wait_pair(act, heads_d, pr, 2)
                    act.activation(inv_t[:, p, :], ps[:, B_PROJ, 384:512], ACT.Copy).then_inc(rt_e, 1)
                pr = follows(at, OFF_F, FF)
                if pr is not None:
                    wait_own(act, f_h, pr)
                    wait_own(act, f_acc, pr, 2)
                    for c in range(HC):
                        ins = act.activation(hid_f[:, pr.p, c, :], ps[:, B_F, c * 128:(c + 1) * 128], ACT.Relu,
                                             bias=v(f"ffb1_{c}"))
                    ins.then_inc(f_r, 1)
                pr = follows(at, OFF_F, LAST)
                if pr is not None:
                    wait_own(act, l_h, pr)
                    wait_own(act, l_acc, pr, 2)
                    act.activation(hid_f[:, pr.p, 0, :], ps[:, B_F, 0:TOK], ACT.Relu, bias=v("l3b1")).then_inc(l_r, 1)
                pr = at(OFF_SCORE)
                if pr is not None:
                    p, w = pr.p, heads(pr) * S
                    wait_pair(act, sub_d, pr)
                    act.activation(prob[:, p, 0:w], prob[:, p, 0:w], ACT.Exp,
                                   scale=float(D // heads(pr)) ** -0.5).then_inc(exp_d, 1)
                pr = at(OFF_V)
                if pr is not None:
                    p, dk = pr.p, D // heads(pr)
                    wait_pair(act, vproj_d, pr)
                    wait_pair(act, pv_d, pr, 2)
                    for par in range(2):
                        rows_p = slice(S * par, S * par + S)
                        src = ps[rows_p, B_PROJ, 256:384]
                        if dk == 8:
                            dst = v_16[rows_p, p, :, :, :].rearrange("r b (g k) c -> r (b g) (k c)", k=2)
                            dst = dst.rearrange("r bg (k c) -> r bg k c", k=2)
                            for k in range(2):
                                ins = act.activation(
                                    dst[:, :, k, 16 * k + 8 * par:16 * k + 8 * par + 8],
                                    src.rearrange("r (bg k d) -> r bg k d", k=2, d=8)[:, :, k, :], ACT.Copy)
                        else:
                            ins = act.activation(
                                v_8[rows_p, p, :, :, 16 * par:16 * par + 16].rearrange("r b q c -> r (b q) c"),
                                src.rearrange("r (bq d) -> r bq d", d=16), ACT.Copy)
                    ins.then_inc(v_e, 1)
                pr = follows(at, OFF_R1, RO)
                if pr is not None:
                    wait_own(act, r_gap, pr)
                    wait_own(act, r_g2, pr, 2)
                    act.activation(e_gap[:, pr.p, :], gap[:, pr.p, :], ACT.Exp).then_inc(r_exp, 1)
                pr = at(OFF_OUT)
                if pr is not None and POST[pr.phase] != "ln":
                    p = pr.p
                    wait_pair(act, xt_d, pr, 2)
                    if POST[pr.phase] == "rms":
                        wait_pair(act, res_d, pr, 2)
                        wait_pair(act, rstd_d, pr)
                        act.activation(normed[:, p, :], y[:, p, :], ACT.Copy, scale=rstd[:, p, :]).then_inc(norm_d, 1)
                    else:
                        act.wait_ge(res_d, LAST * NP - 1 if isinstance(pr.i, int) and pr.i == 0 else LAST * NP)
                        wait_pair(act, y_d, pr)
                        act.activation(normed[:, p, :], y[:, p, :], ACT.Copy).then_inc(norm_d, 1)

            chunks = (1 + E) * HC

            def back(t):
                act.wait_ge(m_back, t + 1)
                act.activation(x_t[:, bass.ds(t * TILE, TILE)], ps[:, B_TAIL, :], ACT.Copy).then_inc(m_xt, 1)

            def experts(t, first):
                for k in range(chunks):
                    act.wait_ge(m_h, chunks * t + (k + 1))
                    if not (first and k < ring):
                        wait_low(act, k - ring, t)
                    act.activation(hid[:, k % ring, :], ps[:, k % h_banks, :], ACT.Silu).then_inc(m_act, 1)
                    e, c = divmod(k, HC)
                    if e >= 1 and c == 1:
                        act.wait_ge(m_gate, E * t + e)
                        if not (first and e <= 2):
                            act.wait_ge(m_mul, E * t + (e - 2))
                        act.activation(gate_b[:, e % 2, :], ps[:, B_GATE[e % 2], :], ACT.Copy).then_inc(m_gate_e, 1)
                    if k == 10:
                        act.wait_ge(m_acc, chunks * t + HC)
                        if not first:
                            act.wait_ge(m_turn, t)
                        act.activation(mlp_o, ps[:, B_ACC[0], :], ACT.Copy).then_inc(m_first, 1)
                    if not first and k == 22:
                        back(t - 1)

            run_slots(act, GROUPS[0], slot)
            tiles(act, experts)
            back(NT - 1)
            run_slots(act, GROUPS[1], slot)

        @block.vector
        def _(dve):
            dve.wait_ge(loaded["small"], 48)
            dve.tensor_scalar(idb[:, :], ident, NEG, None, ALU.mult).then_inc(set_id, 1)
            for ph, c in BIASED.items():
                dve.tensor_copy(bv_cols[:, c, :], v(f"bv{ph}").broadcast_to([128, TOK])).then_inc(set_bv, 1)
            dve.wait_ge(loaded["sel"], 16)
            dve.wait_ge(set_zero, 6)
            dve.tensor_copy(sel[0:2 * E, :, :], sel_raw).then_inc(set_sel, 1)
            dve.wait_ge(set_sel, 1)

            def residuals():
                dve.wait_ge(set_mm, 1)
                dve.wait_ge(loaded["rows"], 16)
                bo = rows[:, ROW["bo0"]:ROW["bo0"] + 3, :]
                dve.tensor_tensor(row_bias[:, :, :], ps[:, B_OUT, 0:3 * D].rearrange("p (c d) -> p c d", c=3), bo, ALU.add)\
                    .then_inc(set_bias, 1)
                dve.wait_ge(set_bias, 1)
                dve.tensor_tensor(row_bias[:, 1, :], row_bias[:, 1, :], rows[:, ROW["b1"], :], ALU.add).then_inc(set_bias, 1)
                dve.wait_ge(loaded["x_tok"], 16)
                dve.tensor_tensor(x_tok[:, :, :], x_tok[:, :, :], row_bias[:, 0:1, :].broadcast_to([128, NP, D]), ALU.add)\
                    .then_inc(set_bias, 1)
                dve.wait_ge(set_bias, 3)

            def slot(at):
                pr = at(OFF_OUT)
                if pr is not None:
                    p = pr.p
                    wait_pair(dve, rt_e, pr)
                    wait_pair(dve, pv_d, pr)
                    wait_pair(dve, out_d, pr, 2)
                    dve.tensor_tensor(heads_t[:, p, :], ps[:, B_HEADS, 0:TOK], inv_t[:, p, :], ALU.mult)\
                        .then_inc(heads_d, 1)
                pr = at(OFF_PV)
                if pr is not None:
                    p, nh = pr.p, heads(pr)
                    wait_pair(dve, exp_d, pr)
                    wait_pair(dve, inv_d, pr, 2)
                    dve.tensor_reduce(total[:, p, 0:nh], prob[:, p, 0:nh * S].rearrange("p (h k) -> p h k", k=S),
                                      AX.X, ALU.add).then_inc(sum_d, 1)
                pr = at(OFF_XT)
                if pr is not None and POST[pr.phase] == "ln":
                    p = pr.p
                    wait_pair(dve, xt_d, pr, 2)
                    wait_pair(dve, rstd_d, pr)
                    wait_pair(dve, res_d, pr, 2)
                    dve.tensor_scalar(normed[:, p, :], y[:, p, :], moments[:, p, 0:1], rstd[:, p, :],
                                      ALU.subtract, ALU.mult).then_inc(norm_d, 1)
                pr = at(OFF_PV)
                if pr is not None:
                    p, nh = pr.p, heads(pr)
                    wait_pair(dve, sum_d, pr)
                    wait_pair(dve, inv_d, pr, 2)
                    dve.reciprocal(inv_h[:, p, 0:nh], total[:, p, 0:nh]).then_inc(rcp_d, 1)
                pr = follows(at, OFF_FN, FF)
                if pr is not None:
                    p = pr.p
                    wait_own(dve, f_rs, pr)
                    wait_own(dve, f_z, pr, 2)
                    dve.tensor_scalar(n_f[:, p, :], y_f[:, p, :], mom_f[:, p, 0:1], rstd_f[:, p, :],
                                      ALU.subtract, ALU.mult).then_inc(f_nn, 1)
                pr = follows(at, OFF_FB, FF)
                if pr is not None:
                    p = pr.p
                    wait_own(dve, f_rr, pr)
                    wait_own(dve, f_back, pr, 2)
                    dve.tensor_scalar(xn_f[:, p, :], w_f[:, p, :], rrms_f[:, p, :], None, ALU.mult).then_inc(f_xn, 1)
                pr = at(OFF_SCORE)
                if pr is not None:
                    p, nh = pr.p, heads(pr)
                    sc = ps[:, 2 * p:2 * p + nh // 8, :].rearrange("p b (h k) -> p (b h) k", k=S)
                    wait_pair(dve, score_d, pr)
                    wait_pair(dve, sub_d, pr, 2)
                    dve.tensor_reduce(top[:, p, 0:nh], sc, AX.X, ALU.max).then_inc(top_d, 1)
                pr = at(OFF_PV)
                if pr is not None:
                    p, nh = pr.p, heads(pr)
                    wait_pair(dve, rcp_d, pr)
                    wait_pair(dve, rt_d, pr, 2)
                    dve.tensor_copy(inv[:, p, :].rearrange("p (h d) -> p h d", h=nh),
                                    inv_h[:, p, 0:nh].unsqueeze(2).broadcast_to([128, nh, D // nh])).then_inc(inv_d, 1)
                pr = at(OFF_PROJ)
                if pr is not None and MASKED[pr.phase]:
                    p = pr.p
                    dve.wait_ge(ld_m[p], 16 * (pr.half + 1))
                    wait_pair(dve, score_d, pr, 2)
                    dve.tensor_scalar(neg_m[:, p, :], stage_m[:, p, :], 0, None, ALU.is_equal).then_inc(neg_d, 1)
                pr = at(OFF_SCORE)
                if pr is not None:
                    p, nh = pr.p, heads(pr)
                    sc = ps[:, 2 * p:2 * p + nh // 8, :].rearrange("p b (h k) -> p (b h) k", k=S)
                    wait_pair(dve, top_d, pr)
                    wait_pair(dve, pt1_d, pr, 2)
                    wait_pair(dve, sum_d, pr, 2)
                    dve.tensor_tensor(prob[:, p, 0:nh * S].rearrange("p (h k) -> p h k", k=S), sc,
                                      top[:, p, 0:nh].unsqueeze(2).broadcast_to([128, nh, S]), ALU.subtract)\
                        .then_inc(sub_d, 1)
                one, two = follows(at, OFF_R1, RO), follows(at, OFF_R2, RO)
                if two is not None:
                    q = two.p
                    wait_own(dve, r_ix, two)
                    dve.tensor_copy(best_f[:, q, :], best_at[:, q, :]).then_inc(r_fx, 1)
                    wait_own(dve, r_exp, two)
                    dve.tensor_scalar(den[:, q, :], e_gap[:, q, :], 1.0, None, ALU.add).then_inc(r_den, 1)
                if one is not None:
                    p = one.p
                    wait_own(dve, r_l, one)
                    dve.tensor_copy(logit[:, p, :], ps[:, B_F, 128:128 + E]).then_inc(r_lc, 1)
                if two is not None:
                    wait_own(dve, r_den, two)
                    dve.reciprocal(gate1[:, q, :], den[:, q, :]).then_inc(r_g1, 1)
                if one is not None:
                    wait_own(dve, r_lc, one, apart=True)
                    dve.max(best[:, p, :], logit[:, p, :]).then_inc(r_mx, 1)
                if two is not None:
                    wait_own(dve, r_g1, two)
                    dve.tensor_tensor(gate2[:, q, :], e_gap[:, q, :], gate1[:, q, :], ALU.mult).then_inc(r_g2, 1)
                    wait_own(dve, r_fx, two)
                    wait_own(dve, r_gf, two, 2)
                    dve.tensor_scalar(hot1[:, q, :], iota, best_f[:, q, 0:1], gate1[:, q, :],
                                      ALU.is_equal, ALU.mult).then_inc(r_h, 1)
                if one is not None:
                    wait_own(dve, r_mx, one, apart=True)
                    dve.max_index(best_at[:, p, :], best[:, p, :], logit[:, p, :]).then_inc(r_ix, 1)
                    dve.tensor_tensor(gap[:, p, :], best[:, p, 1:2], best[:, p, 0:1], ALU.subtract).then_inc(r_gap, 1)
                if two is not None:
                    wait_own(dve, r_g2, two)
                    dve.tensor_scalar(hot2[:, q, :], iota, best_f[:, q, 1:2], gate2[:, q, :],
                                      ALU.is_equal, ALU.mult).then_inc(r_a, 1)
                pr = at(OFF_OUT)
                if pr is not None:
                    p, ph = pr.p, pr.phase
                    wait_pair(dve, out_d, pr)
                    wait_pair(dve, norm_d, pr, 2)
                    if ph > 0:
                        if ph == FF + 1:
                            wait_own(dve, f_x, pr)
                        elif ph == RO + 1:
                            dve.wait_ge(m_res, pr.i // SUB + 1 if isinstance(pr.i, int) else NT)
                        else:
                            dve.wait_ge(res_d, RES_BEFORE[ph - 1] + 1 + pr.i)
                    if not (isinstance(pr.n, int) and pr.n < 2) and POST[ph] != "none":
                        wait_pair(dve, res_d, pr, 2)
                    dve.tensor_tensor(y[:, p, :], ps[:, B_OUT, OUT], x_tok[:, pr.i, :], ALU.add).then_inc(y_d, 1)
                pr = at(OFF_OUT)
                if pr is not None:
                    p, ph = pr.p, pr.phase
                    if POST[ph] == "ln":
                        wait_pair(dve, y_d, pr)
                        dve.bn_stats(stats[:, p, :], y[:, p, :]).then_inc(bns_d, 1)
                        wait_pair(dve, bns_d, pr, apart=True)
                        dve.bn_aggr(moments[:, p, :], stats[:, p, :]).then_inc(agg_d, 1)
                        wait_pair(dve, agg_d, pr)
                        dve.tensor_scalar(spread[:, p, :], moments[:, p, 1:2], EPS, None, ALU.add).then_inc(spread_d, 1)
                    elif POST[ph] == "rms":
                        wait_pair(dve, y_d, pr)
                        dve.tensor_tensor_reduce(squares[:, p, :], y[:, p, :], y[:, p, :], 1.0 / D, EPS,
                                                 ALU.mult, ALU.add, spread[:, p, :]).then_inc(spread_d, 1)
                pr = follows(at, OFF_FY, FF)
                if pr is not None:
                    p = pr.p
                    wait_own(dve, f_turn, pr)
                    wait_own(dve, f_nn, pr, 2)
                    wait_pair(dve, res_d, pr)
                    dve.tensor_tensor(y_f[:, p, :], ps[:, B_OUT, TURN], x_tok[:, pr.i, :], ALU.add).then_inc(f_y, 1)
                    wait_own(dve, f_y, pr)
                    dve.bn_stats(stats_f[:, p, :], y_f[:, p, :]).then_inc(f_st, 1)
                    wait_own(dve, f_st, pr, apart=True)
                    dve.bn_aggr(mom_f[:, p, :], stats_f[:, p, :]).then_inc(f_ag, 1)
                    wait_own(dve, f_ag, pr)
                    dve.tensor_scalar(spread_f[:, p, :], mom_f[:, p, 1:2], EPS, None, ALU.add).then_inc(f_sp, 1)
                pr = follows(at, OFF_FN, FF)
                if pr is not None:
                    p = pr.p
                    wait_own(dve, f_x, pr)
                    dve.tensor_tensor_reduce(z_f[:, p, :], w_f[:, p, :], w_f[:, p, :], 1.0 / D, EPS,
                                             ALU.mult, ALU.add, meansq_f[:, p, :]).then_inc(f_ms, 1)
                pr = follows(at, OFF_L3, LAST)
                if pr is not None:
                    wait_own(dve, l_o, pr)
                    x = x_t[:, bass.ds(pr.i * TOK, TOK)]
                    dve.tensor_tensor(x, sum_f[:, pr.p, :], x, ALU.add).then_inc(l_y, 1)

            def experts_end(t):
                dve.wait_ge(m_turn, t + 1)
                if not (isinstance(t, int) and t == 0):
                    dve.wait_ge(m_res, t)
                dve.tensor_tensor(y4, ps[:, B_TAIL, :].rearrange("p (s d) -> p s d", s=SUB),
                                  x_tok[:, bass.ds(t * SUB, SUB), :], ALU.add).then_inc(m_y, 1)

            def split_high(n):
                dve.wait_ge(ld_w[n % 2], 16 * (n // 2 + 1))
                dve.tensor_copy(piece(n)[0], stage_w[:, n % 2, :]).then_inc(split_hi, 1)

            def weigh(e, t):
                if not (isinstance(t, int) and t == 0 and e == 1):
                    dve.wait_ge(m_add, E * t + (e - 1))
                dve.wait_ge(m_gate_e, E * t + e)
                dve.wait_ge(m_acc, (1 + E) * HC * t + HC * (e + 1))
                dve.tensor_tensor(weighted, ps[:, B_ACC[e % 2], :], gate_b[:, e % 2, :], ALU.mult)\
                    .then_inc(m_mul, 1)
                dve.wait_ge(m_first, t + 1)
                dve.wait_ge(m_mul, E * t + e)
                dve.tensor_tensor(mlp_o, mlp_o, weighted, ALU.add).then_inc(m_add, 1)

            def experts(t, first):
                chunks = (1 + E) * HC
                if first:
                    dve.wait_ge(xt_e, NP * (RO + 1))
                else:
                    dve.wait_ge(m_h, chunks * t)
                x = x_t[:, bass.ds(t * TILE, TILE)]
                dve.tensor_copy(x_hi[:, :], x).then_inc(m_xh, 1)
                dve.wait_ge(m_xh, t + 1)
                dve.tensor_tensor(x_lo[:, :], x, x_hi[:, :].bitcast(F32), ALU.subtract).then_inc(m_x, 1)
                if not first:
                    weigh(E, t - 1)
                for k in range(chunks):
                    dve.wait_ge(m_act, chunks * t + (k + 1))
                    if not (first and k < ring):
                        dve.wait_ge(m_acc, chunks * t + (k - ring + 1))
                    dve.tensor_copy(hid_hi[:, k % ring, :], hid[:, k % ring, :]).then_inc(m_hi, 1)
                    if not low_by_pool(k):
                        dve.wait_ge(m_hi, chunks * t + (k + 1))
                        dve.tensor_tensor(hid_lo[:, k % ring, :], hid[:, k % ring, :], hid_hi[:, k % ring, :].bitcast(F32),
                                          ALU.subtract).then_inc(m_lo, 1)
                    if k % HC == HC - 1 and k >= 3 * HC - 1:
                        weigh(k // HC - 1, t)
                    if k == 12 and not first:
                        experts_end(t - 1)

            run_slots(dve, GROUPS[0], slot, {4: residuals, **{s: lambda n=n: split_high(n) for s, n in split_at.items()}})
            tiles(dve, experts)
            weigh(E, NT - 1)
            experts_end(NT - 1)
            dve.sem_inc(bns_d, 2 * NP)
            dve.sem_inc(agg_d, 2 * NP)
            run_slots(dve, GROUPS[1], slot)


RES_BEFORE = [NP * sum(k != "none" for k in POST[:n]) for n in range(len(POST))]


def constants():
    r = np.arange(128)
    cst = np.zeros((128, C_END), np.float32)
    cst[:, C_ID:C_ID + 128] = np.eye(128)
    cst[:, C_G:C_G + 4] = r[:, None] // 32 == np.arange(4)
    cst[:, C_J16:C_J16 + 4] = r[:, None] % 32 // 8 == np.arange(4)
    cst[:, C_J8:C_J8 + 2] = r[:, None] % 32 // 16 == np.arange(2)
    cst[:, C_IOTA:C_IOTA + E] = np.arange(E)
    sel = np.zeros((2, E, E, 128), np.float32)
    sel[:, np.arange(E), np.arange(E)] = 1.0
    sel = sel.reshape(2 * E, E, 128)
    return cst, sel


def kernel(**inputs):
    import concourse.bacc as _bacc
    from concourse.bass_utils import run_bass_kernel_spmd as _run

    w = {k: np.asarray(x) for k, x in inputs.items()}
    L0, L1, L2, L3 = ({k[9:]: x for k, x in w.items() if k.startswith(f"L{n}_xattn_")} for n in range(4))
    cst, sel = constants()
    wat = np.stack([
        np.stack([L0["sa_wq"], L0["sa_wk"], L0["sa_wv"], L0["sa_wo"]]),
        np.stack([L0["ca_wq"], L0["ca_wk"], L0["ca_wv"], L0["ca_wo"]]),
        np.stack([L1[f"sa_w{k}"].T for k in "qkvo"]),
        np.stack([L1[f"ca_w{k}"].T for k in "qkvo"]),
        np.stack([L2[f"W{k}"].T for k in "qkvo"]),
        np.stack([L3[f"W_{k}"] for k in "qkvo"]),
    ])
    by_name = {
        "bq0": L0["sa_bq"], "bk0": L0["sa_bk"], "bv0": L0["sa_bv"], "bo0": L0["sa_bo"],
        "bq1": L0["ca_bq"], "bk1": L0["ca_bk"], "bv1": L0["ca_bv"], "bo1": L0["ca_bo"],
        "bq4": L2["bq"], "bk4": L2["bk"], "bv4": L2["bv"], "bo4": L2["bo"],
        "g1": L0["ln1_g"], "b1": L0["ln1_b"], "g2": L0["ln2_g"], "b2": L0["ln2_b"],
        "g3": L0["ln3_g"], "b3": L0["ln3_b"], "n1": L1["norm1_w"], "n2": L1["norm2_w"], "n3": L1["norm3_w"],
        "gL2": L2["ln_g"], "bL2": L2["ln_b"], "ffb2": L0["ff_b2"], "l3b1": L3["b1"], "l3b2": L3["b2"],
    }
    for c in range(HC):
        by_name[f"ffb1_{c}"] = L0["ff_b1"][128 * c:128 * c + 128]
    x = w["x"].reshape(NP, TOK, D)
    arrays = {
        "x_tok": x,
        "x_t": x.transpose(0, 2, 1),
        "ctx_t": w["ctx_1024"].reshape(NP, TOK, D).transpose(0, 2, 1),
        "m0": w["mask_BxSxS2_ik0"].reshape(NP, TOK, S),
        "m1": w["mask_BxSxS2_if1"].reshape(NP, TOK, S),
        "m2": w["mask_BxSxS_ik0"].reshape(NP, TOK, S),
        "m4": w["mask_BxSxS2_ik1"].reshape(NP, TOK, S),
        "cst": cst,
        "sel": sel,
        "vec": np.stack([by_name[k] for k in VECS], axis=1),
        "rows": np.stack([by_name[k] for k in ROWS]),
        "wat": wat.transpose(2, 0, 1, 3),
        "ffw1": L0["ff_w1"][:, None, :],
        "ffw2": L0["ff_w2"].reshape(HC, 128, D).transpose(1, 0, 2)[:, None],
        "gatew": np.pad(L1["gate_w"].T, ((0, 0), (0, 128 - E))),
        "mow1": np.concatenate([L1["sh_w1"][None], L1["exp_w1"]]).transpose(2, 0, 1),
        "mow2": np.concatenate([L1["sh_w2"][None], L1["exp_w2"]]).reshape(1 + E, D, HC, 128).transpose(3, 0, 2, 1)
                .reshape(128, 1 + E, HID),
        "l3w1": L3["w1"].T[:, None, :],
        "l3w2": L3["w2"].T[:, None, None, :],
    }
    nc = _bacc.Bacc("TRN2", target_bir_lowering=False, num_devices=1)
    feed, aps = {}, {}
    for name, arr in arrays.items():
        arr = np.ascontiguousarray(arr)
        feed[f"in_{name}"] = arr
        aps[name] = nc.dram_tensor(f"in_{name}", arr.shape, mybir.dt.from_np(arr.dtype), kind="ExternalInput").ap()
    out_t = nc.dram_tensor("out_t", [D, NP * TOK], F32, kind="ExternalOutput").ap()
    build(nc, aps, out_t)
    r = _run(nc, [feed], core_ids=[0])
    return np.ascontiguousarray(r.results[0]["out_t"].T).reshape(B, S, D)
```
